# Optimizing a Trainium2 kernel written in Bass

```python
import numpy as np
import jax
import jax.numpy as jnp

def _softmax(x, axis=-1):
    return jax.nn.softmax(x, axis=axis)

def _gelu(x):
    return jax.nn.gelu(x, approximate=True)

def _silu(x):
    return jax.nn.silu(x)

def _sigmoid(x):
    return jax.nn.sigmoid(x)

def _layernorm(x, axis=-1, eps=1e-05):
    m = jnp.mean(x, axis=axis, keepdims=True)
    v = jnp.var(x, axis=axis, keepdims=True)
    return (x - m) / jnp.sqrt(v + eps)

def _scatter_add(tgt, idx, src, axis=0):
    return tgt.at[idx].add(src)

def _segment_sum(src, seg, n):
    return jax.ops.segment_sum(src, seg, n)
kernel_name = 'mk_conv_attn_hybrid_d4_conv_nhwc256_r2_5c16b1'

def setup_inputs(seed: int=0):
    np.random.seed(seed)
    _w = jnp.asarray

    def _rec_inputs():
        import jax
        import jax.numpy as jnp
        _gk = jax.random.key(seed)
        x = -0.000929 + 1 * jax.random.normal(jax.random.fold_in(_gk, 1), (1, 32, 32, 128), jnp.float32)
        return x
    x = _rec_inputs()

    def _L0_conv_setup():
        import jax, jax.numpy as jnp
        import numpy as np
        B, H, W, C = (1, 32, 32, 128)
        NH = 8
        K = 7

        def _neighbor_idx(n, k):
            start = jnp.clip(jnp.arange(n) - k // 2, 0, n - k)
            return start[:, None] + jnp.arange(k)[None, :]
        key = jax.random.key(seed)
        ks = jax.random.split(key, 6)
        x = jax.random.normal(ks[0], (B, H, W, C), dtype=jnp.float32)
        qkv_w = jax.random.normal(ks[1], (3 * C, C), dtype=jnp.float32) * 0.02
        qkv_b = jnp.zeros((3 * C,), dtype=jnp.float32)
        proj_w = jax.random.normal(ks[2], (C, C), dtype=jnp.float32) * 0.02
        proj_b = jnp.zeros((C,), dtype=jnp.float32)
        rpb = jax.random.normal(ks[3], (NH, 2 * K - 1, 2 * K - 1), dtype=jnp.float32) * 0.02
        return {'x': x, 'qkv_w': qkv_w, 'qkv_b': qkv_b, 'proj_w': proj_w, 'proj_b': proj_b, 'rpb': rpb}
    _L0_conv_all = _L0_conv_setup()
    _L0_conv_in = {k: v for k, v in _L0_conv_all.items() if k in ('qkv_w', 'qkv_b', 'proj_w', 'proj_b', 'rpb')}
    del _L0_conv_all

    def _L1_conv_setup():
        import jax, jax.numpy as jnp
        import numpy as np
        P_, K_, NH = (8, 4, 8)
        B, H, W, C = (2, 32, 24, 128)

        def _layer_norm(t, g, b, eps=1e-05):
            m = t.mean(-1, keepdims=True)
            v = ((t - m) ** 2).mean(-1, keepdims=True)
            return (t - m) / jnp.sqrt(v + eps) * g + b
        key = jax.random.key(seed)
        ks = jax.random.split(key, 16)

        def w(k, shape, s=0.02):
            return (jax.random.normal(k, shape) * s).astype(jnp.float32)
        z = lambda *shape: jnp.zeros(shape, jnp.float32)
        return {'x_2d': jax.random.normal(ks[0], (B, H, W, C), dtype=jnp.float32), 'wq_proj': w(ks[1], (C, C)), 'bq_proj': z(C), 'wk_proj': w(ks[2], (C, C)), 'bk_proj': z(C), 'wv_proj': w(ks[3], (C, C)), 'bv_proj': z(C), 'wq_a': w(ks[4], (C, C)), 'bq_a': z(C), 'wk_a': w(ks[5], (C, C)), 'bk_a': z(C), 'wv_a': w(ks[6], (C, C)), 'bv_a': z(C), 'wo_a': w(ks[7], (C, C)), 'bo_a': z(C), 'conv_w': w(ks[8], (5, 5, C, C)), 'conv_b': z(C), 'ln1_g': jnp.ones((C,), jnp.float32), 'ln1_b': z(C), 'ln2_g': jnp.ones((C,), jnp.float32), 'ln2_b': z(C)}
    _L1_conv_all = _L1_conv_setup()
    _L1_conv_in = {k: v for k, v in _L1_conv_all.items() if k in ('wq_proj', 'bq_proj', 'wk_proj', 'bk_proj', 'wv_proj', 'bv_proj', 'wq_a', 'bq_a', 'wk_a', 'bk_a', 'wv_a', 'bv_a', 'wo_a', 'bo_a', 'conv_w', 'conv_b', 'ln1_g', 'ln1_b', 'ln2_g', 'ln2_b')}
    del _L1_conv_all

    def _L2_attn_setup():
        import jax, jax.numpy as jnp
        import numpy as np
        DIM = 128
        HEADS = 4
        WIN = 128
        RADIUS = 32
        HEAD_DIM = DIM // HEADS
        SCALE = HEAD_DIM ** (-0.5)
        NEG_INF = -1e+30

        def _band_mask(T, radius):
            i = jnp.arange(T)[:, None]
            j = jnp.arange(T)[None, :]
            d = i - j
            return jnp.where((d >= 0) & (d <= radius), 0.0, -jnp.inf).astype(jnp.float32)
        key = jax.random.key(seed)
        k1, k2, k3 = jax.random.split(key, 3)
        B, T, C = (16, 2048, DIM)
        x = jax.random.normal(k1, (B, T, C), dtype=jnp.float32)
        Wqkv = jax.random.normal(k2, (C, 3 * C), dtype=jnp.float32) * 0.02
        Wproj = jax.random.normal(k3, (C, C), dtype=jnp.float32) * 0.02
        bproj = jnp.zeros((C,), dtype=jnp.float32)
        return {'x': x, 'Wqkv': Wqkv, 'Wproj': Wproj, 'bproj': bproj}
    _L2_attn_all = _L2_attn_setup()
    _L2_attn_in = {k: v for k, v in _L2_attn_all.items() if k in ('Wqkv', 'Wproj', 'bproj')}
    del _L2_attn_all

    def _L2_ffn_setup():
        import jax, jax.numpy as jnp
        import numpy as np
        TOP_K = 2
        LN_EPS = 1e-05
        key = jax.random.key(seed)
        ks = jax.random.split(key, 8)
        B, S, D, E, H = (16, 512, 128, 8, 512)
        x = jax.random.normal(ks[0], (B, S, D), dtype=jnp.float32)
        Wr = jax.random.normal(ks[1], (D, E), dtype=jnp.float32) * 0.1
        br = jnp.zeros((E,), dtype=jnp.float32)
        ln_g = jnp.ones((E, D), dtype=jnp.float32)
        ln_b = jnp.zeros((E, D), dtype=jnp.float32)
        W1 = jax.random.normal(ks[2], (E, D, H), dtype=jnp.float32) * (1.0 / np.sqrt(D))
        b1 = jnp.zeros((E, H), dtype=jnp.float32)
        W2 = jax.random.normal(ks[3], (E, H, D), dtype=jnp.float32) * (1.0 / np.sqrt(H))
        b2 = jnp.zeros((E, D), dtype=jnp.float32)
        return {'x': x, 'Wr': Wr, 'br': br, 'ln_g': ln_g, 'ln_b': ln_b, 'W1': W1, 'b1': b1, 'W2': W2, 'b2': b2}
    _L2_ffn_all = _L2_ffn_setup()
    _L2_ffn_in = {k: v for k, v in _L2_ffn_all.items() if k in ('Wr', 'br', 'ln_g', 'ln_b', 'W1', 'b1', 'W2', 'b2')}
    del _L2_ffn_all

    def _L3_attn_setup():
        import jax, jax.numpy as jnp
        import numpy as np
        B, S, D, U = (8, 1024, 128, 64)
        key = jax.random.key(seed)
        ks = jax.random.split(key, 5)
        inputs = jax.random.normal(ks[0], (B, S, D), dtype=jnp.float32)
        W_q = jax.random.normal(ks[1], (D, U), dtype=jnp.float32) * (1.0 / np.sqrt(D))
        W_k = jax.random.normal(ks[2], (D, U), dtype=jnp.float32) * (1.0 / np.sqrt(D))
        W_v = jax.random.normal(ks[3], (D, U), dtype=jnp.float32) * (1.0 / np.sqrt(D))
        W_o = jax.random.normal(ks[4], (U, D), dtype=jnp.float32) * (1.0 / np.sqrt(U))
        b_o = jnp.zeros((D,), dtype=jnp.float32)
        return {'inputs': inputs, 'W_q': W_q, 'W_k': W_k, 'W_v': W_v, 'W_o': W_o, 'b_o': b_o}
    _L3_attn_all = _L3_attn_setup()
    _L3_attn_in = {k: v for k, v in _L3_attn_all.items() if k in ('W_q', 'W_k', 'W_v', 'W_o', 'b_o')}
    del _L3_attn_all

    def _L3_ffn_setup():
        import math
        import jax, jax.numpy as jnp
        import numpy as np
        CAPACITY_FACTOR = 1.25
        key = jax.random.key(seed)
        ks = jax.random.split(key, 5)
        B, L, D, F, E = (8, 4096, 128, 512, 8)
        h = jax.random.normal(ks[0], (B, L, D), dtype=jnp.float32)
        gate_w = jax.random.normal(ks[1], (D, E), dtype=jnp.float32) * 0.02
        gate_b = jnp.zeros((E,), dtype=jnp.float32)
        w1 = jax.random.normal(ks[2], (E, D, F), dtype=jnp.float32) * (1.0 / math.sqrt(D))
        b1 = jnp.zeros((E, F), dtype=jnp.float32)
        w2 = jax.random.normal(ks[3], (E, F, D), dtype=jnp.float32) * (1.0 / math.sqrt(F))
        b2 = jnp.zeros((E, D), dtype=jnp.float32)
        return {'h': h, 'gate_w': gate_w, 'gate_b': gate_b, 'w1': w1, 'b1': b1, 'w2': w2, 'b2': b2}
    _L3_ffn_all = _L3_ffn_setup()
    _L3_ffn_in = {k: v for k, v in _L3_ffn_all.items() if k in ('gate_w', 'gate_b', 'w1', 'b1', 'w2', 'b2')}
    del _L3_ffn_all
    return {'x': x, 'L0_conv_qkv_w': _L0_conv_in['qkv_w'], 'L0_conv_qkv_b': _L0_conv_in['qkv_b'], 'L0_conv_proj_w': _L0_conv_in['proj_w'], 'L0_conv_proj_b': _L0_conv_in['proj_b'], 'L0_conv_rpb': _L0_conv_in['rpb'], 'L1_conv_wq_proj': _L1_conv_in['wq_proj'], 'L1_conv_bq_proj': _L1_conv_in['bq_proj'], 'L1_conv_wk_proj': _L1_conv_in['wk_proj'], 'L1_conv_bk_proj': _L1_conv_in['bk_proj'], 'L1_conv_wv_proj': _L1_conv_in['wv_proj'], 'L1_conv_bv_proj': _L1_conv_in['bv_proj'], 'L1_conv_wq_a': _L1_conv_in['wq_a'], 'L1_conv_bq_a': _L1_conv_in['bq_a'], 'L1_conv_wk_a': _L1_conv_in['wk_a'], 'L1_conv_bk_a': _L1_conv_in['bk_a'], 'L1_conv_wv_a': _L1_conv_in['wv_a'], 'L1_conv_bv_a': _L1_conv_in['bv_a'], 'L1_conv_wo_a': _L1_conv_in['wo_a'], 'L1_conv_bo_a': _L1_conv_in['bo_a'], 'L1_conv_conv_w': _L1_conv_in['conv_w'], 'L1_conv_conv_b': _L1_conv_in['conv_b'], 'L1_conv_ln1_g': _L1_conv_in['ln1_g'], 'L1_conv_ln1_b': _L1_conv_in['ln1_b'], 'L1_conv_ln2_g': _L1_conv_in['ln2_g'], 'L1_conv_ln2_b': _L1_conv_in['ln2_b'], 'L2_attn_Wqkv': _L2_attn_in['Wqkv'], 'L2_attn_Wproj': _L2_attn_in['Wproj'], 'L2_attn_bproj': _L2_attn_in['bproj'], 'L2_ffn_Wr': _L2_ffn_in['Wr'], 'L2_ffn_br': _L2_ffn_in['br'], 'L2_ffn_ln_g': _L2_ffn_in['ln_g'], 'L2_ffn_ln_b': _L2_ffn_in['ln_b'], 'L2_ffn_W1': _L2_ffn_in['W1'], 'L2_ffn_b1': _L2_ffn_in['b1'], 'L2_ffn_W2': _L2_ffn_in['W2'], 'L2_ffn_b2': _L2_ffn_in['b2'], 'L3_attn_W_q': _L3_attn_in['W_q'], 'L3_attn_W_k': _L3_attn_in['W_k'], 'L3_attn_W_v': _L3_attn_in['W_v'], 'L3_attn_W_o': _L3_attn_in['W_o'], 'L3_attn_b_o': _L3_attn_in['b_o'], 'L3_ffn_gate_w': _L3_ffn_in['gate_w'], 'L3_ffn_gate_b': _L3_ffn_in['gate_b'], 'L3_ffn_w1': _L3_ffn_in['w1'], 'L3_ffn_b1': _L3_ffn_in['b1'], 'L3_ffn_w2': _L3_ffn_in['w2'], 'L3_ffn_b2': _L3_ffn_in['b2']}

def reference(x, L0_conv_qkv_w, L0_conv_qkv_b, L0_conv_proj_w, L0_conv_proj_b, L0_conv_rpb, L1_conv_wq_proj, L1_conv_bq_proj, L1_conv_wk_proj, L1_conv_bk_proj, L1_conv_wv_proj, L1_conv_bv_proj, L1_conv_wq_a, L1_conv_bq_a, L1_conv_wk_a, L1_conv_bk_a, L1_conv_wv_a, L1_conv_bv_a, L1_conv_wo_a, L1_conv_bo_a, L1_conv_conv_w, L1_conv_conv_b, L1_conv_ln1_g, L1_conv_ln1_b, L1_conv_ln2_g, L1_conv_ln2_b, L2_attn_Wqkv, L2_attn_Wproj, L2_attn_bproj, L2_ffn_Wr, L2_ffn_br, L2_ffn_ln_g, L2_ffn_ln_b, L2_ffn_W1, L2_ffn_b1, L2_ffn_W2, L2_ffn_b2, L3_attn_W_q, L3_attn_W_k, L3_attn_W_v, L3_attn_W_o, L3_attn_b_o, L3_ffn_gate_w, L3_ffn_gate_b, L3_ffn_w1, L3_ffn_b1, L3_ffn_w2, L3_ffn_b2):
    import jax
    import jax.numpy as jnp

    def _L0_conv_ref(x, qkv_w, qkv_b, proj_w, proj_b, rpb):
        import jax, jax.numpy as jnp
        import numpy as np
        B, H, W, C = (1, 32, 32, 128)
        NH = 8
        K = 7

        def _neighbor_idx(n, k):
            start = jnp.clip(jnp.arange(n) - k // 2, 0, n - k)
            return start[:, None] + jnp.arange(k)[None, :]
        b, h, w, c = x.shape
        nh = rpb.shape[0]
        k = (rpb.shape[1] + 1) // 2
        hd = c // nh
        scale = hd ** (-0.5)
        qkv = x @ qkv_w.T + qkv_b
        qkv = qkv.reshape(b, h, w, 3, nh, hd)
        qkv = jnp.transpose(qkv, (3, 0, 4, 1, 2, 5))
        q, kk, v = (qkv[0], qkv[1], qkv[2])
        ni = _neighbor_idx(h, k)
        nj = _neighbor_idx(w, k)
        k_nb = kk[:, :, ni][:, :, :, :, nj]
        v_nb = v[:, :, ni][:, :, :, :, nj]
        attn = jnp.einsum('bnijd,bniajcd->bnijac', q * scale, k_nb)
        bi = ni - jnp.arange(h)[:, None] + (k - 1)
        bj = nj - jnp.arange(w)[:, None] + (k - 1)
        bias = rpb[:, bi][:, :, :, bj]
        attn = attn + jnp.transpose(bias, (0, 1, 3, 2, 4))[None]
        attn = jax.nn.softmax(attn.reshape(b, nh, h, w, k * k), axis=-1)
        attn = attn.reshape(b, nh, h, w, k, k)
        out = jnp.einsum('bnijac,bniajcd->bnijd', attn, v_nb)
        out = jnp.transpose(out, (0, 2, 3, 1, 4)).reshape(b, h, w, c)
        out = out @ proj_w.T + proj_b
        return out

    def _L1_conv_ref(x_2d, wq_proj, bq_proj, wk_proj, bk_proj, wv_proj, bv_proj, wq_a, bq_a, wk_a, bk_a, wv_a, bv_a, wo_a, bo_a, conv_w, conv_b, ln1_g, ln1_b, ln2_g, ln2_b):
        import jax, jax.numpy as jnp
        import numpy as np
        P_, K_, NH = (8, 4, 8)
        B, H, W, C = (2, 32, 24, 128)

        def _layer_norm(t, g, b, eps=1e-05):
            m = t.mean(-1, keepdims=True)
            v = ((t - m) ** 2).mean(-1, keepdims=True)
            return (t - m) / jnp.sqrt(v + eps) * g + b
        Bb, Hh, Ww, Cc = x_2d.shape
        hp = Hh // P_
        dk = Cc // NH
        kv = min(K_, P_)
        x_p = x_2d.reshape(Bb, P_, hp, Ww, Cc)
        q_p = x_p @ wq_proj + bq_proj
        k_p = x_p @ wk_proj + bk_proj
        v_p = x_p @ wv_proj + bv_proj
        q_loc = q_p.mean((2, 3))
        k_loc = k_p.mean((2, 3))
        S_loc = jnp.einsum('bpc,bqc->bpq', q_loc, k_loc)
        _, R = jax.lax.top_k(S_loc, kv)
        k_flat = k_p.reshape(Bb, P_, hp * Ww, Cc)
        v_flat = v_p.reshape(Bb, P_, hp * Ww, Cc)
        k_fil = jax.vmap(lambda t, r: t[r])(k_flat, R).reshape(Bb, P_, kv, hp, Ww, Cc)
        v_fil = jax.vmap(lambda t, r: t[r])(v_flat, R).reshape(Bb, P_, kv, hp, Ww, Cc)
        q_un = jnp.broadcast_to(q_p[:, :, None], (Bb, P_, kv, hp, Ww, Cc))
        L = kv * hp * Ww

        def to_heads(t, w, b):
            t = t @ w + b
            t = t.reshape(Bb, P_, kv, hp, Ww, NH, dk)
            return t.transpose(0, 5, 1, 2, 3, 4, 6).reshape(Bb, NH, P_, L, dk)
        qh = to_heads(q_un, wq_a, bq_a)
        kh = to_heads(k_fil, wk_a, bk_a)
        vh = to_heads(v_fil, wv_a, bv_a)
        scores = jnp.einsum('bhpqd,bhpkd->bhpqk', qh, kh) / jnp.sqrt(jnp.float32(dk))
        attn = jax.nn.softmax(scores, axis=-1)
        ctx = jnp.einsum('bhpqk,bhpkd->bhpqd', attn, vh)
        ctx = ctx.reshape(Bb, NH, P_, kv, hp, Ww, dk).transpose(0, 2, 3, 4, 5, 1, 6)
        ctx = ctx.reshape(Bb, P_, kv, hp, Ww, Cc)
        routing_out = (ctx @ wo_a + bo_a).mean(2)
        x_res = _layer_norm(x_p + routing_out, ln1_g, ln1_b)
        kv_g = (k_p + v_p).reshape(Bb, Hh, Ww, Cc)
        g = jax.lax.conv_general_dilated(kv_g, conv_w, (1, 1), 'SAME', dimension_numbers=('NHWC', 'HWIO', 'NHWC')) + conv_b
        g = g.reshape(Bb, P_, hp, Ww, Cc)
        out = _layer_norm(x_res + g, ln2_g, ln2_b)
        return out.reshape(Bb, Hh, Ww, Cc)

    def _L2_attn_ref(x, Wqkv, Wproj, bproj):
        import jax, jax.numpy as jnp
        import numpy as np
        DIM = 128
        HEADS = 4
        WIN = 128
        RADIUS = 32
        HEAD_DIM = DIM // HEADS
        SCALE = HEAD_DIM ** (-0.5)
        NEG_INF = -1e+30

        def _band_mask(T, radius):
            i = jnp.arange(T)[:, None]
            j = jnp.arange(T)[None, :]
            d = i - j
            return jnp.where((d >= 0) & (d <= radius), 0.0, -jnp.inf).astype(jnp.float32)
        B_prev, T_prev, C = x.shape
        xw = x.reshape(-1, WIN, C)
        Bw = xw.shape[0]
        qkv = xw @ Wqkv
        qkv = qkv.reshape(Bw, WIN, 3, HEADS, HEAD_DIM)
        qkv = qkv.transpose(2, 0, 3, 1, 4)
        q, k, v = (qkv[0], qkv[1], qkv[2])
        attn = jnp.einsum('bhid,bhjd->bhij', q, k) * SCALE
        attn = attn + _band_mask(WIN, RADIUS)[None, None]
        attn = jax.nn.softmax(attn, axis=-1)
        out = jnp.einsum('bhij,bhjd->bhid', attn, v)
        out = out.transpose(0, 2, 1, 3).reshape(Bw, WIN, C)
        out = out @ Wproj + bproj
        return out.reshape(B_prev, T_prev, C)

    def _L2_ffn_ref(x, Wr, br, ln_g, ln_b, W1, b1, W2, b2):
        import jax, jax.numpy as jnp
        import numpy as np
        TOP_K = 2
        LN_EPS = 1e-05
        B, S, D = x.shape
        N = B * S
        xt = x.reshape(N, D)
        logits = xt @ Wr + br
        probs = jax.nn.softmax(logits, axis=-1)
        top_p, top_idx = jax.lax.top_k(probs, TOP_K)
        weights = top_p / top_p.sum(axis=-1, keepdims=True)
        mu = xt.mean(axis=-1, keepdims=True)
        var = ((xt - mu) ** 2).mean(axis=-1, keepdims=True)
        xn = (xt - mu) * jax.lax.rsqrt(var + LN_EPS)
        xe = xn[None, :, :] * ln_g[:, None, :] + ln_b[:, None, :]
        h = jax.nn.gelu(jnp.einsum('end,edh->enh', xe, W1) + b1[:, None, :], approximate=False)
        y = jnp.einsum('enh,ehd->end', h, W2) + b2[:, None, :]
        y_tok = jnp.transpose(y, (1, 0, 2))
        sel = jnp.take_along_axis(y_tok, top_idx[:, :, None], axis=1)
        out = (weights[:, :, None] * sel).sum(axis=1)
        return out.reshape(B, S, D)

    def _L3_attn_ref(inputs, W_q, W_k, W_v, W_o, b_o):
        import jax, jax.numpy as jnp
        import numpy as np
        B, S, D, U = (8, 1024, 128, 64)
        Q = jnp.einsum('bsd,du->bsu', inputs, W_q)
        K = jnp.einsum('bsd,du->bsu', inputs, W_k)
        V = jnp.einsum('bsd,du->bsu', inputs, W_v)
        scale = 1.0 / jnp.sqrt(jnp.asarray(U, dtype=inputs.dtype))
        attn = jnp.einsum('bqu,bku->bqk', Q, K) * scale
        w = jax.nn.softmax(attn, axis=-1)
        out = jnp.einsum('bqk,bku->bqu', w, V)
        return jnp.einsum('bsu,ud->bsd', out, W_o) + b_o + inputs

    def _L3_ffn_ref(h, gate_w, gate_b, w1, b1, w2, b2):
        import math
        import jax, jax.numpy as jnp
        import numpy as np
        CAPACITY_FACTOR = 1.25
        B, L, D = h.shape
        E = gate_w.shape[1]
        T = B * L
        C = max(1, math.ceil(CAPACITY_FACTOR * T / E))
        x = h.reshape(T, D)
        logits = x @ gate_w + gate_b
        probs = jax.nn.softmax(logits, axis=-1)
        idx = jnp.argmax(probs, axis=-1)
        prb = jnp.take_along_axis(probs, idx[:, None], axis=1)[:, 0]
        one_hot = jax.nn.one_hot(idx, E, dtype=jnp.float32)
        pos = (jnp.cumsum(one_hot, axis=0) * one_hot).sum(-1).astype(jnp.int32) - 1
        kept = pos < C
        pos_safe = jnp.where(kept, pos, C)
        buf = jnp.zeros((E, C, D), dtype=h.dtype).at[idx, pos_safe].set(x, mode='drop')
        hmid = jax.nn.relu(jnp.einsum('ecd,edf->ecf', buf, w1) + b1[:, None, :])
        ybuf = jnp.einsum('ecf,efd->ecd', hmid, w2) + b2[:, None, :]
        pos_g = jnp.minimum(pos, C - 1)
        y_tok = ybuf[idx, pos_g] * (prb * kept)[:, None]
        y = y_tok.reshape(B, L, D)
        y = jnp.nan_to_num(y, nan=0.0, posinf=10000.0, neginf=-10000.0)
        return y

    def _gn(v, G=32, eps=1e-05):
        B_, H_, W_, C_ = v.shape
        g = v.reshape(B_, H_, W_, G, C_ // G)
        m = jnp.mean(g, axis=(1, 2, 4), keepdims=True)
        s = jnp.var(g, axis=(1, 2, 4), keepdims=True)
        return ((g - m) / jnp.sqrt(s + eps)).reshape(v.shape)

    def _ln_c(v, eps=1e-06):
        m = jnp.mean(v, axis=-1, keepdims=True)
        s = jnp.var(v, axis=-1, keepdims=True)
        return (v - m) / jnp.sqrt(s + eps)

    def _ln_t(v, eps=1e-05):
        m = jnp.mean(v, axis=-1, keepdims=True)
        s = jnp.var(v, axis=-1, keepdims=True)
        return (v - m) / jnp.sqrt(s + eps)

    def _to_tokens(v):
        B_, H_, W_, C_ = v.shape
        return v.reshape(B_, H_ * W_, C_)

    def _from_tokens(t, like):
        return t.reshape(like.shape)
    x = x + _L0_conv_ref(_gn(x), L0_conv_qkv_w, L0_conv_qkv_b, L0_conv_proj_w, L0_conv_proj_b, L0_conv_rpb)
    x = x + _L1_conv_ref(_gn(x), L1_conv_wq_proj, L1_conv_bq_proj, L1_conv_wk_proj, L1_conv_bk_proj, L1_conv_wv_proj, L1_conv_bv_proj, L1_conv_wq_a, L1_conv_bq_a, L1_conv_wk_a, L1_conv_bk_a, L1_conv_wv_a, L1_conv_bv_a, L1_conv_wo_a, L1_conv_bo_a, L1_conv_conv_w, L1_conv_conv_b, L1_conv_ln1_g, L1_conv_ln1_b, L1_conv_ln2_g, L1_conv_ln2_b)
    t = _to_tokens(x)
    t = t + _L2_attn_ref(_ln_t(t), L2_attn_Wqkv, L2_attn_Wproj, L2_attn_bproj)
    t = t + _L2_ffn_ref(_ln_t(t), L2_ffn_Wr, L2_ffn_br, L2_ffn_ln_g, L2_ffn_ln_b, L2_ffn_W1, L2_ffn_b1, L2_ffn_W2, L2_ffn_b2)
    t = t + _L3_attn_ref(_ln_t(t), L3_attn_W_q, L3_attn_W_k, L3_attn_W_v, L3_attn_W_o, L3_attn_b_o)
    t = t + _L3_ffn_ref(_ln_t(t), L3_ffn_gate_w, L3_ffn_gate_b, L3_ffn_w1, L3_ffn_b1, L3_ffn_w2, L3_ffn_b2)
    x = _from_tokens(t, x)
    return x

_drawn_inputs = setup_inputs


def setup_inputs(seed=0):
    import zlib

    import numpy as np

    out = dict(_drawn_inputs(seed))
    spreads = {'L0_conv_qkv_b': (0.0, 0.1),
     'L0_conv_proj_b': (0.0, 0.1),
     'L1_conv_bq_proj': (0.0, 2.0),
     'L1_conv_bk_proj': (0.0, 0.1),
     'L1_conv_bv_proj': (0.0, 0.1),
     'L1_conv_bq_a': (0.0, 2.0),
     'L1_conv_bk_a': (0.0, 2.0),
     'L1_conv_bv_a': (0.0, 0.289),
     'L1_conv_bo_a': (0.0, 0.1),
     'L1_conv_conv_b': (0.0, 0.1),
     'L1_conv_ln1_g': (1.0, 0.2),
     'L1_conv_ln1_b': (0.0, 0.1),
     'L1_conv_ln2_g': (1.0, 0.2),
     'L1_conv_ln2_b': (0.0, 0.1),
     'L2_attn_bproj': (0.0, 0.1),
     'L2_ffn_br': (0.0, 0.1),
     'L2_ffn_ln_g': (1.0, 0.2),
     'L2_ffn_ln_b': (0.0, 0.302),
     'L2_ffn_b1': (0.0, 0.322),
     'L2_ffn_b2': (0.0, 0.1),
     'L3_attn_b_o': (0.0, 0.1),
     'L3_ffn_gate_b': (0.0, 0.272),
     'L3_ffn_b1': (0.0, 2.0),
     'L3_ffn_b2': (0.0, 0.8)}
    factors = {'L0_conv_qkv_w': 3.747,
     'L0_conv_rpb': 41.789,
     'L1_conv_wq_proj': 47.626,
     'L1_conv_wq_a': 41.522,
     'L1_conv_wk_a': 33.86,
     'L1_conv_wv_a': 5.225,
     'L2_attn_Wqkv': 3.681,
     'L2_attn_Wproj': 4.444}
    for name, (base, spread) in spreads.items():
        noise = np.random.default_rng([zlib.crc32(name.encode()), seed]).standard_normal(out[name].shape)
        drawn = base * np.exp(spread * noise) if base else spread * noise
        out[name] = jnp.asarray(drawn.astype(out[name].dtype))
    for name, factor in factors.items():
        out[name] = (out[name] * factor).astype(out[name].dtype)
    return out
```

```python
from contextlib import ExitStack

import concourse.bass as bass
from concourse import mybir

P = 128
IMG = 32
T = IMG * IMG // P
N = T * P
HALF = 512

F32 = mybir.dt.float32
U32 = mybir.dt.uint32
U8 = mybir.dt.uint8
ALU = mybir.AluOpType
ACT = mybir.ActivationFunctionType
AX = mybir.AxisListType

NEG = -1.0e30
FMAX = 3.4028234e38

NH8, HD8 = 8, 16
NH4, HD4 = 4, 32
KW = 7
REL = 2 * KW - 1
ROWS = P // IMG
LR = 3 * ROWS
KV = 4
HEADS = T * NH8
N0_EXP, N0_T, N0_V = 8, 10, 11
N1_EXP, N1_T, N1_V = 2, 3, 4
N0_ACT, N1_ACT = 4, 2
RADIUS = 32
U = 64
E = 8
FH = 512
FC = FH // P
CAP = 160

VEC = {}
for _name, _rows in (("L0_conv_qkv_b", 3), ("L0_conv_proj_b", 1), ("L1_conv_bq_proj", 1), ("L1_conv_bk_proj", 1),
                     ("L1_conv_bv_proj", 1), ("L1_conv_bq_a", 1), ("L1_conv_bk_a", 1), ("L1_conv_bo_a", 1),
                     ("L1_conv_conv_b", 1), ("L2_ffn_ln_g", E), ("L2_ffn_ln_b", E), ("L2_ffn_b1", E * FC),
                     ("L3_ffn_b1", E * FC)):
    VEC[_name] = (sum(r for _, r in VEC.values()), _rows)
NVEC = sum(r for _, r in VEC.values())

ROWVEC = ["L0_conv_v_b", "L1_conv_bv_a", "L1_conv_ln1_g", "L1_conv_ln1_b", "L1_conv_ln2_g", "L1_conv_ln2_b",
          "L2_attn_bproj", "L3_attn_b_o"]

KINDS = {
    "turned_ps": [("xt_ps", 2), ("rt_ps", 2), ("gt_ps", 2), ("x1t_ps", 2), ("na_tps", 2), ("nb_tps", 2),
                  ("nn_tps", 2), ("nc_tps", 2), ("nd_tps", 2)],
    "product_ps": [("n0_q_ps", 2), ("n0_k_ps", 2), ("n0_proj_ps", 2), ("l1_qp_ps", 2), ("l1_kp_ps", 2),
                   ("l1_vp_ps", 2), ("l1_qh_ps", 2), ("l1_kh_ps", 2), ("conv_ps", 2), ("l1_wo_ps", 2),
                   ("n2_q_ps", 2), ("n2_k_ps", 2), ("n3_q_ps", 2), ("n3_k_ps", 2)],
    "values_ps": [("n0_v_ps", 2), ("l1_v_ps", 2), ("n2_v_ps", 2), ("n3_v_ps", 2)],
    "act_copied": [("xT_ready", 2), ("w0_ready", 1), ("vcols_ready", 1), ("rpbT_ready", 1), ("n0_k", 2), ("l1_qp", 2),
                   ("l1_vp", 2), ("l1_kh", 2), ("gT_ready", 2), ("g_tok", 2), ("x1_tok", 2), ("na_T", 2), ("n2_k", 2),
                   ("nb_T", 2), ("m2_xT", 2), ("nc_T", 2), ("n3_k", 2), ("nd_T", 2)],
    "dve_made": [("n0_q", 2), ("n0_v", 2), ("x1T_ready", 2), ("l1_kp", 2), ("loc_sum", 2), ("loc_ready", 1),
                 ("l1_qh", 2), ("l1_v", 2), ("topi_ready", 1), ("rT_ready", 2), ("n2_q", 2), ("n2_v", 2),
                 ("n3_q", 2), ("n3_v", 2)],
    "normalised": [("g0_norm", 2), ("g1_norm", 2)] + [(f"{x}_norm", T) for x in ("ln1", "ln2", "na", "nb", "nn", "nc", "nd")],
    "norm_stats": [(f"{x}_norm_st", T) for x in ("ln1", "ln2", "na", "nb", "nn", "nc", "nd")],
    "norm_mean": [(f"{x}_norm_mv", T) for x in ("ln1", "ln2", "na", "nb", "nn", "nc", "nd")],
    "pool_made": [("kvpad_zero", 1), ("kvpad_ready", 2), ("xres_ready", 2), ("x2_ready", 2), ("xb2_ready", 2),
                  ("xb3_ready", 2)],
    "queries_split": [("n0_qm", T), ("n1_qm", T), ("n2_qm", T)],
    "scores_ps": [("n0_s", HEADS), ("n1_s", HEADS), ("n2_s", T * NH4), ("n3_s", T)],
    "scores_read": [("n0_sr", HEADS), ("n2_sr", T)],
    "row_maxima": [("n0_nmx", T), ("n1_nmx", HEADS // 2), ("n2_nmx", T), ("n3_nmx", T)],
    "probabilities": [("n0_p", HEADS), ("n1_p", HEADS), ("n2_p", T * NH4), ("n3_p", T)],
    "turned_p_ps": [("n0_pt", HEADS), ("n1_pt", HEADS), ("n2_pt", T), ("n3_pt", 2 * T)],
    "turned_p_act": [("n0_pta", HEADS // N0_ACT), ("n1_pta", HEADS // N1_ACT), ("n3_pta", T)],
    "turned_p_dve": [("n0_ptd", HEADS - HEADS // N0_ACT), ("n1_ptd", HEADS - HEADS // N1_ACT), ("n2_ptd", T), ("n3_ptd", T)],
    "with_values_ps": [("n0_pv", HEADS), ("n1_pv", HEADS), ("n2_pv", T), ("n3_pv", T)],
    "output": [("n0_o", T), ("n1_o", T), ("n2_o", T), ("n3_o", T)],
    "turned_output_ps": [("n0_ot", T), ("n1_ot", T), ("n2_ot", T), ("n3_ot", T)],
    "turned_output": [("n0_oT", T), ("n1_oT", T), ("n2_oT", T), ("n3_oT", T)],
    "projected_ps": [("n2_proj", T), ("n3_proj", T)],
    "residual_added": [("n2_add", T), ("n3_add", T)],
}
for _kind, _count in (("lg_ps", 1), ("lg", 1), ("ex", 1), ("cmp", 2 * T), ("cwt_ps", 2), ("cwT", 2), ("b2_ps", 2), ("b2", 2),
                      ("cw", 1), ("fc1", 2 * FC * E), ("h", 2 * FC * E), ("fc2", 2 * E), ("acc", T * E)):
    KINDS["expert_" + _kind] = [(f"m2_{_kind}", _count), (f"m3_{_kind}", _count)]
PLACE = {name: (kind, sum(c for _, c in names[:i])) for kind, names in KINDS.items() for i, (name, _) in enumerate(names)}


class Chain:

    def __init__(self, eng, sem):
        self.eng, self.sem, self.n = eng, sem, 0

    def __call__(self, ins):
        self.n += 1
        ins.then_inc(self.sem, 1)
        self.eng.wait_ge(self.sem, self.n)


def build(nc, A, out):
    with ExitStack() as ctx:
        def sb(name, shape, dt=F32):
            return ctx.enter_context(nc.sbuf_tensor(name, shape, dt))

        sems = {}

        def S(name):
            name = PLACE.get(name, (name, 0))[0]
            if name not in sems:
                sems[name] = ctx.enter_context(nc.semaphore(name))
            return sems[name]

        def at(name, k):
            return S(name), PLACE.get(name, (name, 0))[1] + k

        ps = ctx.enter_context(nc.psum_tensor("ps", [P, 8, HALF], F32))

        ident = sb("ident", [P, P])
        ones = sb("ones", [P, P])
        upper = sb("upper", [P, P])
        band = sb("band", [P, P])
        gavg = sb("gavg", [P, P])
        mask8 = sb("mask8", [P, NH8])
        mask4 = sb("mask4", [P, NH4])
        tril8 = sb("tril8", [P, E, E])
        nhalf = sb("nhalf", [P, 8])
        vrows = sb("vrows", [P, P])
        vcols = sb("vcols", [P, NVEC])
        rowv = sb("rowv", [P, len(ROWVEC), P])
        rrow = sb("rrow", [P, 2, E])
        w0rows = sb("w0rows", [P, 4, P])
        w0 = sb("w0", [P, 4, P])
        w1 = sb("w1", [P, 7, P])
        convw = sb("convw", [P, 25, P])
        w2a = sb("w2a", [P, 3 * P])
        w2p = sb("w2p", [P, P])
        w3q = sb("w3q", [P, 3, U])
        w3o = sb("w3o", [U, P])
        rout = sb("rout", [P, 2, E])
        fw1 = sb("fw1", [P, E, FH])
        fw2 = sb("fw2", [P, E, FC, P])
        fb2 = sb("fb2", [E, 2, P])
        rprows = sb("rprows", [NH8 * REL, REL])
        rpbT = sb("rpbT", [33, NH8, REL + 2])
        shift = sb("shift", [33, IMG, IMG])
        rmask = sb("rmask", [P, 3, LR])
        arena = sb("arena", [P, 9216])
        tabs = sb("tabs", [P, 7168])
        tab_i = tabs[:, 0:3072].rearrange("p (h l j) -> p h l j", h=NH8, l=LR)
        tab_t = tabs[:, 3072:5120].rearrange("p (h l j) -> p h l j", h=NH8, l=8)
        tab_b = tabs[:, 5120:7168].rearrange("p (h l j) -> p h l j", h=NH8, l=8)

        dT = tabs[:, 0:N]
        eT = tabs[:, N:2 * N]
        bK = tabs[:, 2 * N:3 * N].rearrange("p (t c) -> p t c", t=T)
        cK = tabs[:, 3 * N:4 * N].rearrange("p (t c) -> p t c", t=T)
        cwT = tabs[0:E, 4 * N:5 * N]
        kvpad = tabs[:, 5 * N:5 * N + (IMG + 4) ** 2].rearrange("p (r w) -> p r w", r=IMG + 4)

        xT = sb("xT", [P, N])
        nT = sb("nT", [P, N])
        aT = sb("aT", [P, N])
        bT = sb("bT", [P, N])
        cT = sb("cT", [P, N])
        oT = sb("oT", [P, N])
        aK = sb("aK", [P, T, P])
        xK = aK
        vaug = sb("vaug", [P, T, NH8, HD8 + 1])
        vaug4 = sb("vaug4", [P, T, NH4, HD4 + 1])
        vaug1 = sb("vaug1", [P, T, U + 1])
        qm = sb("qm", [P, 2, NH8, P])
        pS = arena[:, 0:4 * HALF].rearrange("p (a k) -> p a k", a=4)
        pT = sb("pT", [P, 4, HALF])
        oK = sb("oK", [P, 2, P])
        mx = sb("mx", [P, 2, 8])
        nmx = sb("nmx", [P, 16, 8])
        rs = sb("rs", [P, 2, 8])
        st = sb("st", [P, T, 6])
        mv = sb("mv", [P, T, 2])
        ge = sb("ge", [P, 2])
        gm = sb("gm", [P, 2])
        gv = sb("gv", [P, 1])
        grs = sb("grs", [P, 1])
        ve = sb("ve", [P, T])
        rstd = sb("rstd", [P, T])
        loc = sb("loc", [P, 2, T])
        sloc = sb("sloc", [T, 8])
        top8 = sb("top8", [T, 8])
        topi = sb("topi", [T, 8], U32)
        lg = sb("lg", [P, T, E])
        lm = sb("lm", [P, T])
        ex = sb("ex", [P, T, E])
        cmp_ = sb("cmp", [P, T, E, E])
        cm2 = sb("cm2", [P, T, E, E])
        rank = sb("rank", [P, T, E])
        cw = sb("cw", [P, T, E])
        sm = sb("sm", [P, T])
        rsm = sb("rsm", [P, T])
        kept = sb("kept", [P, T, E])
        nanm = sb("nanm", [P, T, P], U8)
        fills = sb("fills", [P, 3, P])

        x_v = A["x"].rearrange("a (t r) w c -> (r w) (a t) c", t=T)
        out_v = out.rearrange("a (t r) w c -> (r w) (a t) c", t=T)

        def row(name):
            return rowv[:, ROWVEC.index(name), :]

        def col(name, i=0):
            k = VEC[name][0] + i
            return vcols[:, k:k + 1]

        def halves(t):
            return t[:, 0:HALF], t[:, HALF:N]

        def n0_lo(t):
            return max(t - 1, 0)

        def n0_hi(t):
            return min(t + 2, T)

        def n0_w(m):
            return P * (n0_hi(m // NH8) - n0_lo(m // NH8))

        def arena_s(t):
            return arena[:, 3072 * (t % 3):3072 * (t % 3) + 3072].rearrange("p (h k) -> p h k", h=NH8)

        def hid(e):
            return arena[:, 4096 * (e % 2):4096 * (e % 2) + 4096].rearrange("p (c n) -> p c n", c=FC)

        def by_act(m, every):
            return m % every == every - 1

        def copied(eng, name, m, every):
            if by_act(m, every):
                eng.wait_ge(*at(f"{name}_pta", (m + 1) // every))
            else:
                eng.wait_ge(*at(f"{name}_ptd", m + 1 - (m + 1) // every))

        block = ctx.enter_context(nc.Block())

        @block.sync
        def _(sp):
            for i in range(4):
                sp.dma_start(xK[:, 2 * i:2 * i + 2, :], x_v[:, 2 * i:2 * i + 2, :]).then_inc(S("x_in"), 16)
            sp.dma_start(w0rows[:, 0:3, :], A["L0_conv_qkv_w"].rearrange("(a p) c -> p a c", p=P)).then_inc(S("w0_in"), 16)
            sp.dma_start(w0rows[:, 3, :], A["L0_conv_proj_w"]).then_inc(S("w0_in"), 16)
            for i, name in enumerate(["L1_conv_wq_proj", "L1_conv_wk_proj", "L1_conv_wv_proj", "L1_conv_wq_a",
                                      "L1_conv_wk_a", "L1_conv_wv_a", "L1_conv_wo_a"]):
                sp.dma_start(w1[:, i, :], A[name]).then_inc(S("w1_in"), 16)
            sp.dma_start(convw[:, :, :], A["L1_conv_conv_w"].rearrange("a b c d -> c (a b) d")).then_inc(S("conv_in"), 16)
            sp.dma_start(w2a[:, :], A["L2_attn_Wqkv"]).then_inc(S("w2_in"), 16)
            sp.dma_start(w2p[:, :], A["L2_attn_Wproj"]).then_inc(S("w2_in"), 16)
            sp.dma_start(rout[:, 0, :], A["L2_ffn_Wr"]).then_inc(S("rout_in"), 16)
            sp.dma_start(rout[:, 1, :], A["L3_ffn_gate_w"]).then_inc(S("rout_in"), 16)
            sp.dma_start(fw1[:, :, :], A["L2_ffn_W1"].rearrange("e d h -> d e h")).then_inc(S("fw_in"), 16)
            sp.dma_start(fw2[:, :, :, :], A["L2_ffn_W2"].rearrange("e (c p) d -> p e c d", p=P)).then_inc(S("fw_in"), 16)
            sp.dma_start(fb2[:, 0, :], A["L2_ffn_b2"]).then_inc(S("fb2_in"), 16)
            sp.dma_start(fb2[:, 1, :], A["L3_ffn_b2"]).then_inc(S("fb2_in"), 16)
            for i, name in enumerate(["L3_attn_W_q", "L3_attn_W_k", "L3_attn_W_v"]):
                sp.dma_start(w3q[:, i, :], A[name]).then_inc(S("w3_in"), 16)
            sp.dma_start(w3o[:, :], A["L3_attn_W_o"]).then_inc(S("w3_in"), 16)
            for e in range(E):
                sp.wait_ge(*at("m2_fc1", 8 * (e + 1)))
                sp.dma_start(fw1[:, e, :], A["L3_ffn_w1"][e]).then_inc(S("fv_in"), 16)
                sp.wait_ge(*at("m2_fc2", 2 * (e + 1)))
                sp.dma_start(fw2[:, e, :, :], A["L3_ffn_w2"][e].rearrange("(c p) d -> p c d", p=P)).then_inc(S("fv_in"), 16)
            for t in range(T):
                sp.wait_ge(*at("y_ready", t + 1))
                sp.dma_start(out_v[:, t, :], aK[:, t, :]).then_inc(S("y_out"), 16)
            sp.wait_ge(*at("y_out", 16 * T))

        @block.gpsimd
        def _(pool):
            link = Chain(pool, S("pool_chain"))

            def select(ap, pattern, base, mult, op=ALU.is_ge, fill=0.0):
                return pool.affine_select(out=ap, in_=ap, pattern=pattern, base=base, channel_multiplier=mult,
                                          compare_op=op, fill=fill)

            link(pool.memset(ident[:, :], 0.0))
            select(ident[:, :], [[-1, P]], 0, 1, ALU.not_equal, 1.0).then_inc(S("ident_ready"), 1)
            pool.wait_ge(*at("ident_ready", 1))
            link(pool.memset(shift[:, :, :], 0.0))
            link(select(shift[0:REL, :, :], [[-1, IMG], [1, IMG]], -(KW - 1), 1, ALU.not_equal, 1.0))
            lo, hi = IMG - KW, KW
            link(select(shift[32:33, 0:lo, :], [[1, lo], [-1, IMG]], KW // 2, 0, ALU.is_ge, NEG))
            link(select(shift[32:33, hi:IMG, :], [[-1, IMG - hi], [1, IMG]], KW // 2 - hi, 0, ALU.is_ge, NEG))
            link(pool.memset(rpbT[:, :, :], 0.0))
            pool.memset(rpbT[32:33, :, :], 1.0).then_inc(S("shift_ready"), 1)
            pool.wait_ge(*at("shift_ready", 1))
            link(pool.memset(gavg[:, :], 0.25))
            g = gavg[:, :].rearrange("p (g i) -> p g i", i=4)
            link(select(g, [[-4, P // 4], [0, 4]], 0, 1))
            select(g, [[4, P // 4], [0, 4]], 3, -1).then_inc(S("gavg_ready"), 1)
            pool.wait_ge(*at("gavg_ready", 1))
            link(pool.memset(nhalf[:, :], -0.5))
            link(pool.memset(rmask[:, :, :], NEG))
            for r in range(ROWS):
                link(pool.memset(rmask[32 * r:32 * r + 32, 0, r + 1:r + 1 + KW], 0.0))
            link(pool.memset(rmask[:, 1, ROWS:ROWS + KW], 0.0))
            pool.memset(rmask[:, 2, 1:1 + KW], 0.0).then_inc(S("rmask_ready"), 1)
            pool.wait_ge(*at("rmask_ready", 1))
            for m, nh, hd in ((mask8, NH8, HD8), (mask4, NH4, HD4)):
                link(pool.memset(m[:, :], 1.0))
                link(select(m[:, :], [[-hd, nh]], 0, 1))
                link(select(m[:, :], [[hd, nh]], hd - 1, -1))
            link(pool.memset(vaug[:, :, :, HD8:HD8 + 1], 1.0))
            link(pool.memset(vaug4[:, :, :, HD4:HD4 + 1], 1.0))
            pool.memset(vaug1[:, :, U:U + 1], 1.0).then_inc(S("ones_cols"), 1)
            pool.wait_ge(*at("ones_cols", 1))

            def small_consts():
                link(pool.memset(ones[:, :], 1.0))
                link(pool.memset(upper[:, :], 1.0))
                link(select(upper[:, :], [[1, P]], 0, -1))
                link(pool.memset(band[:, :], 0.0))
                link(select(band[:, :], [[-1, P]], 0, 1, ALU.is_ge, NEG))
                link(select(band[:, :], [[1, P]], RADIUS, -1, ALU.is_ge, NEG))
                link(pool.memset(tril8[:, :, :], 1.0))
                link(select(tril8[:, :, :], [[1, E], [-1, E]], -1, 0))
                for i, v in enumerate((0.0, 10000.0, -10000.0)):
                    link(pool.memset(fills[:, i, :], v))

            def root(i, src, dst, n):
                pool.wait_ge(*at("var_ready", i + 1))
                pool.tensor_tensor(dst, src, nhalf[:, 0:n], ALU.pow).then_inc(S("root_ready"), 1)
                pool.wait_ge(*at("root_ready", i + 1))

            def split_heads(name, src, mask, nh, scores, tiles=T):
                for t in range(tiles):
                    if t == 0:
                        for i in (0, 1):
                            pool.wait_ge(*at("l1_qh" if name == "n1" else f"{name}_q", i + 1))
                    if t >= 2:
                        pool.wait_ge(*at(scores, nh * (t - 1)))
                    pool.tensor_tensor(qm[:, t % 2, 0:nh, :],
                                       src[:, P * t:P * t + P].unsqueeze(1).broadcast_to([P, nh, P]),
                                       mask[:, :].unsqueeze(2).broadcast_to([P, nh, P]),
                                       ALU.mult).then_inc(S(f"{name}_qm"), 1)
                    pool.wait_ge(*at(f"{name}_qm", t + 1))

            root(0, gv[:, :], grs[:, :], 1)
            small_consts()
            split_heads("n0", aT, mask8, NH8, "n0_s")
            pool.wait_ge(*at("n0_sr", HEADS))
            pool.memset(kvpad[:, :, :], 0.0).then_inc(S("kvpad_zero"), 1)
            root(1, gv[:, :], grs[:, :], 1)
            pool.wait_ge(*at("l1_kp", 2))
            pool.wait_ge(*at("l1_vp", 2))
            pool.wait_ge(*at("kvpad_zero", 1))
            for i in range(2):
                pool.tensor_tensor(kvpad[:, 2 + 16 * i:18 + 16 * i, 2:2 + IMG],
                                   halves(bT)[i].rearrange("p (r w) -> p r w", w=IMG),
                                   halves(cT)[i].rearrange("p (r w) -> p r w", w=IMG),
                                   ALU.add).then_inc(S("kvpad_ready"), 1)
            split_heads("n1", aT, mask8, NH8, "n1_s")
            root(2, ve[:, :], rstd[:, :], T)
            for t in range(0, T, 4):
                pool.wait_ge(*at("ln1_norm", t + 4))
                v = bK[:, t:t + 4, :]
                link(pool.tensor_tensor(v, v, row("L1_conv_ln1_g").unsqueeze(1).broadcast_to([P, 4, P]), ALU.mult))
                link(pool.tensor_tensor(v, v, row("L1_conv_ln1_b").unsqueeze(1).broadcast_to([P, 4, P]), ALU.add))
                pool.wait_ge(*at("g_tok", t // 4 + 1))
                pool.tensor_tensor(v, v, cK[:, t:t + 4, :], ALU.add).then_inc(S("xres_ready"), 1)
            root(3, ve[:, :], rstd[:, :], T)
            for t in range(0, T, 4):
                pool.wait_ge(*at("ln2_norm", t + 4))
                v = bK[:, t:t + 4, :]
                link(pool.tensor_tensor(v, v, row("L1_conv_ln2_g").unsqueeze(1).broadcast_to([P, 4, P]), ALU.mult))
                link(pool.tensor_tensor(v, v, row("L1_conv_ln2_b").unsqueeze(1).broadcast_to([P, 4, P]), ALU.add))
                pool.wait_ge(*at("x1_tok", t // 4 + 1))
                pool.tensor_tensor(aK[:, t:t + 4, :], v, aK[:, t:t + 4, :], ALU.add).then_inc(S("x2_ready"), 1)
            root(4, ve[:, :], rstd[:, :], T)
            for t in range(0, T, 4):
                v = aK[:, t:t + 4, :]
                pool.wait_ge(*at("na_norm", t + 4))
                pool.tensor_tensor(v, v, row("L2_attn_bproj").unsqueeze(1).broadcast_to([P, 4, P]),
                                   ALU.add).then_inc(S("xb2_ready"), 1)
            split_heads("n2", aT, mask4, NH4, "n2_s")
            root(5, ve[:, :], rstd[:, :], T)
            root(6, ve[:, :], rstd[:, :], T)
            for e in range(E):
                dst = (bT, cT)[e % 2]
                if e == 0:
                    pool.wait_ge(*at("m2_xT", 2))
                if e >= 2:
                    pool.wait_ge(*at("m2_fc1", 8 * (e - 1)))
                pool.tensor_scalar(dst[:, :], nT[:, :], col("L2_ffn_ln_g", e), col("L2_ffn_ln_b", e),
                                   ALU.mult, ALU.add).then_inc(S("m2_xe"), 1)
            root(7, ve[:, :], rstd[:, :], T)
            for t in range(0, T, 4):
                v = aK[:, t:t + 4, :]
                pool.wait_ge(*at("nc_norm", t + 4))
                link(pool.tensor_tensor(v, v, row("L3_attn_b_o").unsqueeze(1).broadcast_to([P, 4, P]), ALU.add))
                pool.tensor_tensor(v, v, bK[:, t:t + 4, :], ALU.add).then_inc(S("xb3_ready"), 1)
            root(8, ve[:, :], rstd[:, :], T)

        @block.scalar
        def _(act):
            for name, (k, n) in VEC.items():
                src = A[name]
                if len(src.shape) == 1:
                    src = src.rearrange("(a c) -> a c", c=P)
                elif src.shape[1] != P:
                    src = src.rearrange("e (a c) -> (e a) c", c=P)
                act.dma_start(vrows[k:k + n, :], src).then_inc(S("vec_in"), 16)
            act.dma_start(rprows[:, :], A["L0_conv_rpb"].rearrange("h a b -> (h a) b")).then_inc(S("rpb_in"), 16)
            for i, name in enumerate(ROWVEC):
                src = A["L0_conv_qkv_b"][2 * P:3 * P] if i == 0 else A[name]
                act.dma_start(rowv[:, i, :], src.partition_broadcast(P)).then_inc(S("row_in"), 16)
            act.dma_start(rrow[:, 0, :], A["L2_ffn_br"].partition_broadcast(P)).then_inc(S("row_in"), 16)
            act.dma_start(rrow[:, 1, :], A["L3_ffn_gate_b"].partition_broadcast(P)).then_inc(S("row_in"), 16)

            def evac2(dst, banks, ready, done, bias=None):
                for i in range(2):
                    act.wait_ge(*at(ready, i + 1))
                    if bias is None:
                        ins = act.activation(halves(dst)[i], ps[:, banks[i], :], ACT.Copy)
                    else:
                        ins = act.activation(halves(dst)[i], ps[:, banks[i], :], ACT.Identity, bias=bias)
                    ins.then_inc(S(done), 1)

            evac2(xT, (0, 1), "xt_ps", "xT_ready")
            act.wait_ge(*at("w0_ps", 1))
            act.activation(w0[:, :, :], ps[:, 2, :].rearrange("p (a c) -> p a c", a=4), ACT.Copy).then_inc(S("w0_ready"), 1)
            act.wait_ge(*at("vec_ps", 1))
            act.activation(vcols[:, :], ps[:, 3, 0:NVEC], ACT.Copy).then_inc(S("vcols_ready"), 1)
            act.wait_ge(*at("shift_ready", 1))
            act.activation(rpbT[0:REL, :, 1:1 + REL],
                           ps[0:REL, 3, 128:128 + NH8 * REL].rearrange("p (h a) -> p h a", h=NH8),
                           ACT.Copy).then_inc(S("rpbT_ready"), 1)
            act.wait_ge(*at("vcols_ready", 1))
            evac2(bT, (2, 3), "n0_k_ps", "n0_k", col("L0_conv_qkv_b", 1))

            def evac_pT(name, m, w):
                act.wait_ge(*at(f"{name}_pt", m + 1))
                if m >= 4:
                    act.wait_ge(*at(f"{name}_pv", m - 3))
                act.activation(pT[:, m % 4, 0:w], ps[:, 4 + m % 2, 0:w], ACT.Copy).then_inc(S(f"{name}_pta"), 1)

            def o_copy(name, t, bank, rows=P):
                act.wait_ge(*at(f"{name}_ot", t + 1))
                act.activation(oT[0:rows, P * t:P * t + P], ps[0:rows, bank, 0:P], ACT.Copy).then_inc(S(f"{name}_oT"), 1)

            for s in range(HEADS + N0_V + 11):
                n = s - N0_EXP
                if 0 <= n < HEADS:
                    t, h = divmod(n, NH8)
                    act.wait_ge(*at("n0_nmx", t + 1))
                    v = arena_s(t)[:, h, 0:n0_w(n)]
                    act.activation(v, v, ACT.Exp, bias=nmx[:, t, h:h + 1]).then_inc(S("n0_p"), 1)
                m = s - N0_T
                if 0 <= m < HEADS and by_act(m, N0_ACT):
                    evac_pT("n0", m, n0_w(m))
                t, r = divmod(s - N0_V - 10, NH8)
                if r == 0 and 0 <= t < T:
                    o_copy("n0", t, 6 + t % 2)

            evac2(aT, (0, 1), "l1_qp_ps", "l1_qp", col("L1_conv_bq_proj"))
            evac2(cT, (4, 5), "l1_vp_ps", "l1_vp", col("L1_conv_bv_proj"))
            evac2(dT, (2, 3), "l1_kh_ps", "l1_kh", col("L1_conv_bk_a"))
            evac2(eT, (4, 5), "conv_ps", "gT_ready", col("L1_conv_conv_b"))

            for s in range(HEADS + N1_V + 11):
                n = s - N1_EXP
                if 0 <= n < HEADS:
                    act.wait_ge(*at("n1_nmx", n // 2 + 1))
                    if n >= 4:
                        act.wait_ge(*at("n1_pt", n - 3))
                    act.activation(pS[:, n % 4, :], ps[:, n % 4, :], ACT.Exp,
                                   bias=nmx[:, n // 2 % 16, n % 2:n % 2 + 1]).then_inc(S("n1_p"), 1)
                m = s - N1_T
                if 0 <= m < HEADS and by_act(m, N1_ACT):
                    evac_pT("n1", m, HALF)
                t, r = divmod(s - N1_V - 10, NH8)
                if r == 0 and 0 <= t < T:
                    o_copy("n1", t, 6 + t % 2)
            for i in range(2):
                act.wait_ge(*at("gt_ps", i + 1))
                act.activation(cK[:, 4 * i:4 * i + 4, :], ps[:, 4 + i, :].rearrange("p (t c) -> p t c", t=4),
                               ACT.Copy).then_inc(S("g_tok"), 1)
            for i in range(2):
                act.wait_ge(*at("x1t_ps", i + 1))
                act.activation(aK[:, 4 * i:4 * i + 4, :], ps[:, 6 + i, :].rearrange("p (t c) -> p t c", t=4),
                               ACT.Copy).then_inc(S("x1_tok"), 1)

            evac2(nT, (0, 1), "na_tps", "na_T")
            evac2(bT, (4, 5), "n2_k_ps", "n2_k")
            for s in range(T + 4):
                if s < T:
                    act.wait_ge(*at("n2_nmx", s + 1))
                    for h in range(NH4):
                        v = pS[:, s % 4, P * h:P * h + P]
                        act.activation(v, v, ACT.Exp, bias=nmx[:, s, h:h + 1]).then_inc(S("n2_p"), 1)
                if s >= 4:
                    o_copy("n2", s - 4, 6)

            def expert_layer(pre, func):
                act.wait_ge(*at(f"{pre}_lg", 1))
                act.activation(ex[:, :, :], lg[:, :, :], ACT.Exp).then_inc(S(f"{pre}_ex"), 1)
                for e in range(E):
                    for c in range(2 * FC):
                        act.wait_ge(*at(f"{pre}_fc1", 2 * FC * e + c + 1))
                        if e >= 2 and c == 0:
                            act.wait_ge(*at(f"{pre}_fc2", 2 * (e - 1)))
                        act.activation(hid(e)[:, c // 2, HALF * (c % 2):HALF * (c % 2) + HALF], ps[:, c % 4, :], func,
                                       bias=col("L2_ffn_b1" if pre == "m2" else "L3_ffn_b1", FC * e + c // 2)
                                       ).then_inc(S(f"{pre}_h"), 1)
                    if e == 0:
                        for i in range(2):
                            act.wait_ge(*at(f"{pre}_cwt_ps", i + 1))
                            act.activation(cwT[:, HALF * i:HALF * i + HALF], ps[0:E, 4 + i, :],
                                           ACT.Copy).then_inc(S(f"{pre}_cwT"), 1)

            evac2(oT, (0, 1), "nb_tps", "nb_T")
            evac2(nT, (2, 3), "nn_tps", "m2_xT")
            expert_layer("m2", ACT.Gelu)

            evac2(nT, (0, 1), "nc_tps", "nc_T")
            for i in range(2):
                act.wait_ge(*at("n3_k_ps", i + 1))
                act.activation(bT[0:U, HALF * i:HALF * i + HALF], ps[0:U, 4 + i, :], ACT.Copy).then_inc(S("n3_k"), 1)
            for s in range(T + 4):
                if s < T:
                    act.wait_ge(*at("n3_nmx", s + 1))
                    if s >= 2:
                        act.wait_ge(*at("n3_pt", 2 * (s - 1)))
                    act.activation(pS[:, 2 * (s % 2):2 * (s % 2) + 2, :], ps[:, 0:2, :], ACT.Exp,
                                   bias=nmx[:, s, 0:1]).then_inc(S("n3_p"), 1)
                t = s - 1
                if 0 <= t < T:
                    act.wait_ge(*at("n3_pt", 2 * t + 2))
                    if t >= 2:
                        act.wait_ge(*at("n3_pv", t - 1))
                    act.activation(pT[:, 2 * (t % 2) + 1, :], ps[:, 3, :], ACT.Copy).then_inc(S("n3_pta"), 1)
                if s >= 4:
                    o_copy("n3", s - 4, 4 + (s - 4) % 2, U)

            evac2(nT, (0, 1), "nd_tps", "nd_T")
            expert_layer("m3", ACT.Relu)

        @block.tensor
        def _(pe):
            def mm(dst, lhsT, rhs, start=True, stop=True):
                return pe.matmul(dst, lhsT, rhs, start=start, stop=stop, skip_group_check=True)

            def turn4(bank, srcs, cols=P, rows=P):
                for j, src in enumerate(srcs):
                    ins = pe.transpose(ps[0:rows, bank, cols * j:cols * j + cols], src, ident[0:cols, 0:cols])
                return ins

            def product(ready, banks, w, src, rows=P):
                for i in range(2):
                    mm(ps[0:rows, banks[i], :], w, halves(src)[i]).then_inc(S(ready), 1)

            def values(ready, banks, src, w, n):
                for t in range(T):
                    ins = mm(ps[:, banks[t // 4], n * (t % 4):n * (t % 4) + n], src[:, P * t:P * t + P], w)
                    if t % 4 == 3:
                        ins.then_inc(S(ready), 1)

            def tokens_to_channels(ready, banks, src, norm):
                for i in range(2):
                    pe.wait_ge(*at(norm, 4 * i + 4))
                    turn4(banks[i], [src[:, 4 * i + j, :] for j in range(4)]).then_inc(S(ready), 1)

            pe.wait_ge(*at("ident_ready", 1))
            for i in range(2):
                pe.wait_ge(*at("x_in", 64))
                turn4(i, [xK[:, 4 * i + j, :] for j in range(4)]).then_inc(S("xt_ps"), 1)
            pe.wait_ge(*at("w0_in", 32))
            turn4(2, [w0rows[:, j, :] for j in range(4)]).then_inc(S("w0_ps"), 1)
            pe.wait_ge(*at("vec_in", 16 * len(VEC)))
            pe.wait_ge(*at("rpb_in", 16))
            pe.transpose(ps[:, 3, 0:NVEC], vrows[0:NVEC, :], ident[0:NVEC, 0:NVEC])
            pe.transpose(ps[0:REL, 3, 128:128 + NH8 * REL], rprows[:, :],
                         ident[0:NH8 * REL, 0:NH8 * REL]).then_inc(S("vec_ps"), 1)

            def bias_columns(part):
                pe.wait_ge(*at("rpbT_ready", 1))
                if part:
                    pe.wait_ge(*at("tab_ready", 3))
                for jj in range(16):
                    for r in range(ROWS):
                        ins = mm(ps[32 * r:32 * r + 32, 4 + jj // 4, 128 * (jj % 4):128 * (jj % 4) + NH8 * LR],
                                 shift[:, 16 * part + jj, :], rpbT[:, :, 3 - r:3 - r + LR])
                ins.then_inc(S("bias_ps"), 1)

            bias_columns(0)

            def group_average(i, bank):
                if i == 0:
                    pe.wait_ge(*at("gavg_ready", 1))
                    pe.wait_ge(*at("vcols_ready", 1))
                    pe.wait_ge(*at("rpbT_ready", 1))
                pe.wait_ge(*at("gn_stats", i + 1))
                mm(ps[:, bank, 0:2], gavg[:, :], ge[:, :]).then_inc(S("gn_avg"), 1)

            group_average(0, 3)
            pe.wait_ge(*at("w0_ready", 1))
            pe.wait_ge(*at("g0_norm", 2))
            pe.wait_ge(*at("gn_read", 1))
            product("n0_q_ps", (0, 1), w0[:, 0, :], nT)
            product("n0_k_ps", (2, 3), w0[:, 1, :], nT)
            pe.wait_ge(*at("n0_q", 2))
            values("n0_v_ps", (0, 1), nT, w0[:, 2, :], P)
            bias_columns(1)
            pe.wait_ge(*at("n0_k", 2))
            pe.wait_ge(*at("n0_v", 2))
            pe.wait_ge(*at("tab_ready", 6))

            pe.wait_ge(*at("ones_cols", 1))

            def attention(name, scores, s_free, t_lag, v_lag, srcs, values_of, every):
                for s in range(HEADS + v_lag + 10):
                    t, r = divmod(s - v_lag - 9, NH8)
                    if r == 0 and 0 <= t < T:
                        pe.wait_ge(*at(f"{name}_o", t + 1))
                        pe.transpose(ps[:, 6 + t % 2, 0:P], oK[:, t % 2, :], ident[:, :]).then_inc(S(f"{name}_ot"), 1)
                    if s < HEADS:
                        t, h = divmod(s, NH8)
                        if h == 0:
                            pe.wait_ge(*at(f"{name}_qm", t + 1))
                        if s >= 4:
                            pe.wait_ge(*at(s_free, s - 3))
                        scores(t, h, ps[:, s % 4, :]).then_inc(S(f"{name}_s"), 1)
                    m = s - t_lag
                    if 0 <= m < HEADS:
                        pe.wait_ge(*at(f"{name}_p", m + 1))
                        if m >= 2:
                            copied(pe, name, m - 2, every)
                        turn4(4 + m % 2, srcs(m)).then_inc(S(f"{name}_pt"), 1)
                    m = s - v_lag
                    if 0 <= m < HEADS:
                        t, h = divmod(m, NH8)
                        copied(pe, name, m, every)
                        if h == 0 and t >= 2:
                            pe.wait_ge(*at(f"{name}_oT", t - 1))
                        vs = values_of(t, h)
                        for j, v in enumerate(vs):
                            ins = mm(ps[:, 6 + t % 2, 17 * h:17 * h + 17], pT[:, m % 4, P * j:P * j + P], v,
                                     start=j == 0, stop=j == len(vs) - 1)
                        ins.then_inc(S(f"{name}_pv"), 1)

            def n0_scores(t, h, bank):
                return mm(bank[:, 0:P * (n0_hi(t) - n0_lo(t))], qm[:, t % 2, h, :], bT[:, P * n0_lo(t):P * n0_hi(t)])

            attention("n0", n0_scores, "n0_sr", N0_T, N0_V,
                      lambda m: [arena_s(m // NH8)[:, m % NH8, P * j:P * j + P] for j in range(n0_w(m) // P)],
                      lambda t, h: [vaug[:, k, h, :] for k in range(n0_lo(t), n0_hi(t))], N0_ACT)
            pe.wait_ge(*at("n0_oT", T))
            product("n0_proj_ps", (0, 1), w0[:, 3, :], oT)

            group_average(1, 2)
            pe.wait_ge(*at("w1_in", 16 * 7))
            pe.wait_ge(*at("g1_norm", 2))
            product("l1_qp_ps", (0, 1), w1[:, 0, :], nT)
            pe.wait_ge(*at("gn_read", 2))
            product("l1_kp_ps", (2, 3), w1[:, 1, :], nT)
            product("l1_vp_ps", (4, 5), w1[:, 2, :], nT)
            pe.wait_ge(*at("l1_qp", 2))
            product("l1_qh_ps", (6, 7), w1[:, 3, :], aT)
            pe.wait_ge(*at("l1_kp", 2))
            product("l1_kh_ps", (2, 3), w1[:, 4, :], bT)
            pe.wait_ge(*at("l1_vp", 2))
            values("l1_v_ps", (0, 1), cT, w1[:, 5, :], P)
            pe.wait_ge(*at("loc_ready", 1))
            pe.wait_ge(*at("l1_qh", 2))
            mm(ps[0:T, 6, 0:T], loc[:, 0, :], loc[:, 1, :]).then_inc(S("sloc_ps"), 1)
            pe.wait_ge(*at("conv_in", 16))
            pe.wait_ge(*at("kvpad_ready", 2))
            for i in range(2):
                for k in range(25):
                    dy, dx = divmod(k, 5)
                    ins = mm(ps[:, 4 + i, :], convw[:, k, :], kvpad[:, 16 * i + dy:16 * i + dy + 16, dx:dx + IMG],
                             start=k == 0, stop=k == 24)
                ins.then_inc(S("conv_ps"), 1)
            pe.wait_ge(*at("topi_ready", 1))
            pe.wait_ge(*at("l1_kh", 2))
            pe.wait_ge(*at("l1_v", 2))
            pe.wait_ge(*at("gT_ready", 2))
            region = {}

            def n1_scores(t, h, bank):
                if h == 0:
                    for j in range(KV):
                        region[t, j] = pe.value_load(topi[t:t + 1, j:j + 1], min_val=0, max_val=T - 1)
                for j in range(KV):
                    ins = mm(bank[:, P * j:P * j + P], qm[:, t % 2, h, :], dT[:, bass.ds(region[t, j] * P, P)])
                return ins

            def n1_values(t, h):
                return [vaug[:, bass.ds(region[t, j], 1), h, :] for j in range(KV)]

            attention("n1", n1_scores, "n1_p", N1_T, N1_V,
                      lambda m: [pS[:, m % 4, P * j:P * j + P] for j in range(KV)], n1_values, N1_ACT)
            pe.wait_ge(*at("n1_oT", T))
            product("l1_wo_ps", (2, 3), w1[:, 6, :], oT)
            for i in range(2):
                pe.wait_ge(*at("rT_ready", i + 1))
                turn4(i, [halves(nT)[i][:, P * j:P * j + P] for j in range(4)]).then_inc(S("rt_ps"), 1)
            for i in range(2):
                turn4(4 + i, [halves(eT)[i][:, P * j:P * j + P] for j in range(4)]).then_inc(S("gt_ps"), 1)
            for i in range(2):
                turn4(6 + i, [halves(xT)[i][:, P * j:P * j + P] for j in range(4)]).then_inc(S("x1t_ps"), 1)

            pe.wait_ge(*at("ln1_norm", T))
            tokens_to_channels("na_tps", (0, 1), bK, "na_norm")
            pe.wait_ge(*at("w2_in", 32))
            pe.wait_ge(*at("na_T", 2))
            product("n2_q_ps", (2, 3), w2a[:, 0:P], nT)
            product("n2_k_ps", (4, 5), w2a[:, P:2 * P], nT)
            values("n2_v_ps", (6, 7), nT, w2a[:, 2 * P:3 * P], P)
            pe.wait_ge(*at("n2_q", 2))
            pe.wait_ge(*at("n2_k", 2))
            pe.wait_ge(*at("n2_v", 2))
            for s in range(T + 5):
                if s < T:
                    pe.wait_ge(*at("n2_qm", s + 1))
                    if s >= 2:
                        pe.wait_ge(*at("n2_sr", s - 1))
                    for h in range(NH4):
                        mm(ps[:, s % 2, P * h:P * h + P], qm[:, s % 2, h, :],
                           bT[:, P * s:P * s + P]).then_inc(S("n2_s"), 1)
                t = s - 1
                if 0 <= t < T:
                    pe.wait_ge(*at("n2_p", NH4 * (t + 1)))
                    if t >= 2:
                        pe.wait_ge(*at("n2_ptd", t - 1))
                    turn4(2 + t % 2, [pS[:, t % 4, P * h:P * h + P] for h in range(NH4)]).then_inc(S("n2_pt"), 1)
                t = s - 2
                if 0 <= t < T:
                    pe.wait_ge(*at("n2_ptd", t + 1))
                    if t >= 2:
                        pe.wait_ge(*at("n2_o", t - 1))
                    for h in range(NH4):
                        ins = mm(ps[:, 4 + t % 2, 33 * h:33 * h + 33], pT[:, t % 4, P * h:P * h + P], vaug4[:, t, h, :])
                    ins.then_inc(S("n2_pv"), 1)
                t = s - 3
                if 0 <= t < T:
                    pe.wait_ge(*at("n2_o", t + 1))
                    if t >= 1:
                        pe.wait_ge(*at("n2_oT", t))
                    pe.transpose(ps[:, 6, 0:P], oK[:, t % 2, :], ident[:, :]).then_inc(S("n2_ot"), 1)
                t = s - 4
                if 0 <= t < T:
                    pe.wait_ge(*at("n2_oT", t + 1))
                    if t >= 1:
                        pe.wait_ge(*at("n2_add", t))
                    mm(ps[:, 7, 0:P], oT[:, P * t:P * t + P], w2p[:, :]).then_inc(S("n2_proj"), 1)

            def router(pre, k, bank, src):
                if k == 0:
                    pe.wait_ge(*at("rout_in", 32))
                for t in range(T):
                    ins = mm(ps[:, bank, E * t:E * t + E], src[:, P * t:P * t + P], rout[:, k, :])
                ins.then_inc(S(f"{pre}_lg_ps"), 1)

            def experts(pre, x_of, x_ready, w_ready):
                def fc2(e):
                    w_ready(e, 1)
                    for t in range(T):
                        bank = 4 + 2 * (e % 2) + t // 4
                        if t % 4 == 0:
                            if e < 2:
                                pe.wait_ge(*at(f"{pre}_b2", 2))
                            else:
                                pe.wait_ge(*at(f"{pre}_acc", T * (e - 2) + t + 4))
                            pe.wait_ge(*at(f"{pre}_h", 2 * FC * (e + 1)))
                        for c in range(FC):
                            ins = mm(ps[:, bank, P * (t % 4):P * (t % 4) + P], hid(e)[:, c, P * t:P * t + P],
                                     fw2[:, e, c, :], start=c == 0, stop=c == FC - 1)
                        if t % 4 == 3:
                            ins.then_inc(S(f"{pre}_fc2"), 1)

                for e in range(E):
                    x_ready(e)
                    w_ready(e, 0)
                    for c in range(2 * FC):
                        g = 2 * FC * e + c
                        if g >= 4:
                            pe.wait_ge(*at(f"{pre}_h", g - 3))
                        mm(ps[:, c % 4, :], fw1[:, e, P * (c // 2):P * (c // 2) + P],
                           halves(x_of(e))[c % 2]).then_inc(S(f"{pre}_fc1"), 1)
                    if e == 0:
                        pe.wait_ge(*at(f"{pre}_cw", 1))
                        for i in range(2):
                            for j in range(4):
                                ins = pe.transpose(ps[0:E, 4 + i, P * j:P * j + P], cw[:, 4 * i + j, :], ident[:, :])
                            ins.then_inc(S(f"{pre}_cwt_ps"), 1)
                        pe.wait_ge(*at("fb2_in", 32))
                        for i in range(2):
                            pe.wait_ge(*at(f"{pre}_cwT", i + 1))
                            for j in range(4):
                                t = 4 * i + j
                                ins = mm(ps[:, 6 + i, P * j:P * j + P], cwT[:, P * t:P * t + P],
                                         fb2[:, 0 if pre == "m2" else 1, :])
                            ins.then_inc(S(f"{pre}_b2_ps"), 1)
                    else:
                        fc2(e - 1)
                fc2(E - 1)

            tokens_to_channels("nb_tps", (0, 1), bK, "nb_norm")
            tokens_to_channels("nn_tps", (2, 3), cK, "nn_norm")
            pe.wait_ge(*at("nb_T", 2))
            router("m2", 0, 4, oT)
            pe.wait_ge(*at("m2_xT", 2))
            pe.wait_ge(*at("m2_lg", 1))

            def m2_w(e, second):
                pe.wait_ge(*at("fw_in", 32))

            experts("m2", lambda e: (bT, cT)[e % 2], lambda e: pe.wait_ge(*at("m2_xe", e + 1)), m2_w)

            tokens_to_channels("nc_tps", (0, 1), bK, "nc_norm")
            pe.wait_ge(*at("w3_in", 64))
            pe.wait_ge(*at("nc_T", 2))
            product("n3_q_ps", (2, 3), w3q[:, 0, :], nT, U)
            product("n3_k_ps", (4, 5), w3q[:, 1, :], nT, U)
            values("n3_v_ps", (6, 7), nT, w3q[:, 2, :], U)
            pe.wait_ge(*at("n3_q", 2))
            pe.wait_ge(*at("n3_k", 2))
            pe.wait_ge(*at("n3_v", 2))
            for s in range(T + 5):
                if s < T:
                    if s >= 1:
                        pe.wait_ge(*at("n3_p", s))
                    for i in range(2):
                        ins = mm(ps[:, i, :], aT[0:U, P * s:P * s + P], bT[0:U, HALF * i:HALF * i + HALF])
                    ins.then_inc(S("n3_s"), 1)
                t = s - 1
                if 0 <= t < T:
                    pe.wait_ge(*at("n3_p", t + 1))
                    for i in range(2):
                        if t >= 1:
                            pe.wait_ge(*at("n3_pta" if i else "n3_ptd", t))
                        turn4(2 + i, [pS[:, 2 * (t % 2) + i, P * j:P * j + P] for j in range(4)]).then_inc(S("n3_pt"), 1)
                t = s - 2
                if 0 <= t < T:
                    pe.wait_ge(*at("n3_ptd", t + 1))
                    pe.wait_ge(*at("n3_pta", t + 1))
                    if t >= 2:
                        pe.wait_ge(*at("n3_oT", t - 1))
                    for k in range(T):
                        ins = mm(ps[:, 4 + t % 2, 0:U + 1], pT[:, 2 * (t % 2) + k // 4, P * (k % 4):P * (k % 4) + P],
                                 vaug1[:, k, :], start=k == 0, stop=k == T - 1)
                    ins.then_inc(S("n3_pv"), 1)
                t = s - 3
                if 0 <= t < T:
                    pe.wait_ge(*at("n3_o", t + 1))
                    pe.transpose(ps[0:U, 4 + t % 2, 0:P], oK[:, t % 2, 0:U], ident[:, :]).then_inc(S("n3_ot"), 1)
                t = s - 4
                if 0 <= t < T:
                    pe.wait_ge(*at("n3_oT", t + 1))
                    if t >= 2:
                        pe.wait_ge(*at("n3_add", t - 1))
                    mm(ps[:, 6 + t % 2, 0:P], oT[0:U, P * t:P * t + P], w3o[:, :]).then_inc(S("n3_proj"), 1)

            tokens_to_channels("nd_tps", (0, 1), bK, "nd_norm")
            pe.wait_ge(*at("nd_T", 2))
            router("m3", 1, 2, nT)
            pe.wait_ge(*at("m3_hot", 1))
            ng = T * E
            mm(ps[:, 3, 0:ng], upper[:, :], rank[:, :, :], stop=False)
            for d in range(1, T):
                ins = mm(ps[:, 3, E * d:ng], ones[:, :], rank[:, 0:T - d, :], start=False, stop=d == T - 1)
            ins.then_inc(S("m3_pos"), 1)
            pe.wait_ge(*at("m3_pos_read", 1))
            pe.wait_ge(*at("m3_lg", 1))

            def m3_w(e, second):
                pe.wait_ge(*at("fv_in", 2 * 16 * E))

            experts("m3", lambda e: nT, lambda e: None, m3_w)

        @block.vector
        def _(dve):
            link = Chain(dve, S("dve_chain"))
            normed = [0]

            def group_norm(i, bank, norm):
                for k in range(2):
                    ins = dve.bn_stats(st[:, k, :], halves(xT)[k])
                    link(ins)
                link(dve.bn_aggr(mv[:, 0, :], st[:, 0:2, :]))
                link(dve.tensor_copy(ge[:, 0:1], mv[:, 0, 0:1]))
                dve.scalar_tensor_tensor(ge[:, 1:2], mv[:, 0, 0:1], mv[:, 0, 0:1], mv[:, 0, 1:2],
                                         ALU.mult, ALU.add).then_inc(S("gn_stats"), 1)
                dve.wait_ge(*at("gn_avg", i + 1))
                dve.tensor_copy(gm[:, :], ps[:, bank, 0:2]).then_inc(S("gn_read"), 1)
                dve.wait_ge(*at("gn_read", i + 1))
                link(dve.scalar_tensor_tensor(gv[:, :], gm[:, 0:1], gm[:, 0:1], gm[:, 1:2], ALU.mult, ALU.subtract))
                dve.tensor_scalar(gv[:, :], gv[:, :], -1.0, 1e-5, ALU.mult, ALU.add).then_inc(S("var_ready"), 1)
                normed[0] += 1
                dve.wait_ge(*at("root_ready", normed[0]))
                for k in range(2):
                    dve.tensor_scalar(halves(nT)[k], halves(xT)[k], gm[:, 0:1], grs[:, :],
                                      ALU.subtract, ALU.mult).then_inc(S(norm), 1)

            def layer_norm(src, dst, norm, eps=1e-5):
                for t in range(T):
                    ins = dve.bn_stats(st[:, t, :], src(t))
                    ins.then_inc(S(norm + "_st"), 1)
                for t in range(T):
                    dve.wait_ge(*at(norm + "_st", t + 1))
                    ins = dve.bn_aggr(mv[:, t, :], st[:, t, :])
                    ins.then_inc(S(norm + "_mv"), 1)
                dve.wait_ge(*at(norm + "_mv", T))
                dve.tensor_scalar(ve[:, :], mv[:, :, 1], eps, None, ALU.add).then_inc(S("var_ready"), 1)
                normed[0] += 1
                dve.wait_ge(*at("root_ready", normed[0]))
                for t in range(T):
                    dve.tensor_scalar(dst[:, t, :], src(t), mv[:, t, 0:1], rstd[:, t:t + 1],
                                      ALU.subtract, ALU.mult).then_inc(S(norm), 1)

            dve.wait_ge(*at("xT_ready", 2))
            group_norm(0, 3, "g0_norm")
            dve.wait_ge(*at("rmask_ready", 1))

            def bias_tables(part):
                dve.wait_ge(*at("bias_ps", part + 1))
                x = ps[:, 4:8, :].rearrange("p b (q c) -> p (b q) c", c=128)[:, :, 0:NH8 * LR]
                x = x.rearrange("p j (h l) -> p h l j", l=LR)
                for k, (tab, l0, l1) in enumerate(((tab_i, 0, LR), (tab_t, ROWS, LR), (tab_b, 0, 8))):
                    for h in range(0, NH8, 4):
                        ins = dve.tensor_tensor(
                            tab[:, h:h + 4, :, 16 * part:16 * part + 16], x[:, h:h + 4, l0:l1, :],
                            rmask[:, k, l0:l1].unsqueeze(1).unsqueeze(3).broadcast_to([P, 4, l1 - l0, 16]), ALU.add)
                    ins.then_inc(S("tab_ready"), 1)

            bias_tables(0)
            dve.wait_ge(*at("vcols_ready", 1))
            for i in range(2):
                dve.wait_ge(*at("n0_q_ps", i + 1))
                dve.tensor_scalar(halves(aT)[i], ps[:, i, :], col("L0_conv_qkv_b", 0), HD8 ** -0.5,
                                  ALU.add, ALU.mult).then_inc(S("n0_q"), 1)

            def evac_values(ready, done, banks, dst, bias=None):
                for i in range(2):
                    dve.wait_ge(*at(ready, i + 1))
                    d = dst(i)
                    w = d.shape[1] * d.shape[2] * d.shape[3]
                    src = ps[:, banks[i], 0:w].rearrange("p (t h d) -> p t h d", t=4, h=d.shape[2])
                    if bias is None:
                        ins = dve.tensor_copy(d, src)
                    else:
                        ins = dve.tensor_tensor(d, src, bias.rearrange("p (h d) -> p h d", d=HD8).unsqueeze(1)
                                                .broadcast_to(list(d.shape)), ALU.add)
                    ins.then_inc(S(done), 1)

            dve.wait_ge(*at("row_in", 16 * (len(ROWVEC) + 2)))
            evac_values("n0_v_ps", "n0_v", (0, 1), lambda i: vaug[:, 4 * i:4 * i + 4, :, 0:HD8], row("L0_conv_v_b"))
            bias_tables(1)

            def evac_pT(name, m, w):
                dve.wait_ge(*at(f"{name}_pt", m + 1))
                if m >= 4:
                    dve.wait_ge(*at(f"{name}_pv", m - 3))
                dve.tensor_copy(pT[:, m % 4, 0:w], ps[:, 4 + m % 2, 0:w]).then_inc(S(f"{name}_ptd"), 1)

            def normalise(name, t, bank, nh, hd):
                o = ps[:, bank, 0:nh * (hd + 1)].rearrange("p (h d) -> p h d", h=nh)
                if t >= 2:
                    dve.wait_ge(*at(f"{name}_ot", t - 1))
                link(dve.reciprocal(rs[:, t % 2, 0:nh], o[:, :, hd]))
                dve.tensor_tensor(oK[:, t % 2, 0:nh * hd].rearrange("p (h d) -> p h d", h=nh), o[:, :, 0:hd],
                                  rs[:, t % 2, 0:nh].unsqueeze(2).broadcast_to([P, nh, hd]),
                                  ALU.mult).then_inc(S(f"{name}_o"), 1)

            dve.wait_ge(*at("tab_ready", 6))
            for s in range(HEADS + N0_V + 11):
                t, r = divmod(s - N0_V - 8, NH8)
                if r == 0 and 0 <= t < T:
                    dve.wait_ge(*at("n0_pv", NH8 * (t + 1)))
                    normalise("n0", t, 6 + t % 2, NH8, HD8)
                if s < HEADS:
                    t, h = divmod(s, NH8)
                    w = n0_w(s)
                    tab = tab_t if t == 0 else tab_b if t == T - 1 else tab_i
                    dve.wait_ge(*at("n0_s", s + 1))
                    if t >= 3 and h == 0:
                        dve.wait_ge(*at("n0_pt", NH8 * (t - 2)))
                    if t >= 2 and h == 0:
                        dve.wait_ge(*at("n0_nmx", t - 1))
                    dve.tensor_tensor_reduce(arena_s(t)[:, h, 0:w], ps[:, s % 4, 0:w],
                                             tab[:, h, :, :].rearrange("p l j -> p (l j)"), 1.0, -FMAX,
                                             ALU.add, ALU.max, mx[:, t % 2, h:h + 1]).then_inc(S("n0_sr"), 1)
                    if h == NH8 - 1:
                        dve.wait_ge(*at("n0_sr", s + 1))
                        dve.tensor_scalar(nmx[:, t, :], mx[:, t % 2, :], -1.0, None, ALU.mult).then_inc(S("n0_nmx"), 1)
                m = s - N0_T
                if 0 <= m < HEADS and not by_act(m, N0_ACT):
                    evac_pT("n0", m, n0_w(m))
            for i in range(2):
                dve.wait_ge(*at("n0_proj_ps", i + 1))
                dve.scalar_tensor_tensor(halves(xT)[i], ps[:, i, :], col("L0_conv_proj_b"), halves(xT)[i],
                                         ALU.add, ALU.add).then_inc(S("x1T_ready"), 1)
            dve.wait_ge(*at("x1T_ready", 2))

            group_norm(1, 2, "g1_norm")
            for i in range(2):
                dve.wait_ge(*at("l1_kp_ps", i + 1))
                dve.tensor_scalar(halves(bT)[i], ps[:, 2 + i, :], col("L1_conv_bk_proj"), None, ALU.add).then_inc(S("l1_kp"), 1)
            dve.wait_ge(*at("l1_qp", 2))
            dve.wait_ge(*at("l1_kp", 2))
            for i, src in enumerate((aT, bT)):
                dve.tensor_reduce(loc[:, i, :], src[:, :].rearrange("p (t n) -> p t n", t=T), AX.X,
                                  ALU.add).then_inc(S("loc_sum"), 1)
            dve.wait_ge(*at("loc_sum", 2))
            dve.tensor_scalar(loc[:, :, :], loc[:, :, :], 1.0 / P, None, ALU.mult).then_inc(S("loc_ready"), 1)
            for i in range(2):
                dve.wait_ge(*at("l1_qh_ps", i + 1))
                dve.tensor_scalar(halves(aT)[i], ps[:, 6 + i, :], col("L1_conv_bq_a"), HD8 ** -0.5,
                                  ALU.add, ALU.mult).then_inc(S("l1_qh"), 1)
            dve.wait_ge(*at("l1_qh", 2))
            evac_values("l1_v_ps", "l1_v", (0, 1), lambda i: vaug[:, 4 * i:4 * i + 4, :, 0:HD8], row("L1_conv_bv_a"))
            dve.wait_ge(*at("sloc_ps", 1))
            link(dve.tensor_copy(sloc[:, :], ps[0:T, 6, 0:T]))
            link(dve.max(top8[:, :], sloc[:, :]))
            dve.max_index(topi[:, :], top8[:, :], sloc[:, :]).then_inc(S("topi_ready"), 1)

            for s in range(HEADS + N1_V + 11):
                t, r = divmod(s - N1_V - 8, NH8)
                if r == 0 and 0 <= t < T:
                    dve.wait_ge(*at("n1_pv", NH8 * (t + 1)))
                    normalise("n1", t, 6 + t % 2, NH8, HD8)
                if s < HEADS and s % 2 == 1:
                    dve.wait_ge(*at("n1_s", s + 1))
                    k = s // 2
                    if k >= 16:
                        dve.wait_ge(*at("n1_p", 2 * (k - 15)))
                    b = (s - 1) % 4
                    dve.tensor_reduce(nmx[:, k % 16, 0:2], ps[:, b:b + 2, :], AX.X, ALU.max,
                                      negate=True).then_inc(S("n1_nmx"), 1)
                m = s - N1_T
                if 0 <= m < HEADS and not by_act(m, N1_ACT):
                    evac_pT("n1", m, HALF)
            for i in range(2):
                dve.wait_ge(*at("l1_wo_ps", i + 1))
                dve.scalar_tensor_tensor(halves(nT)[i], ps[:, 2 + i, :], col("L1_conv_bo_a"), halves(nT)[i],
                                         ALU.add, ALU.add).then_inc(S("rT_ready"), 1)
            dve.wait_ge(*at("rt_ps", 2))
            layer_norm(lambda t: ps[:, t // 4, P * (t % 4):P * (t % 4) + P], bK, "ln1_norm")
            dve.wait_ge(*at("xres_ready", 2))
            layer_norm(lambda t: bK[:, t, :], bK, "ln2_norm")
            dve.wait_ge(*at("x2_ready", 2))

            layer_norm(lambda t: aK[:, t, :], bK, "na_norm")
            for i in range(2):
                dve.wait_ge(*at("n2_q_ps", i + 1))
                dve.tensor_scalar(halves(aT)[i], ps[:, 2 + i, :], HD4 ** -0.5, None, ALU.mult).then_inc(S("n2_q"), 1)
            evac_values("n2_v_ps", "n2_v", (6, 7), lambda i: vaug4[:, 4 * i:4 * i + 4, :, 0:HD4])
            dve.wait_ge(*at("xb2_ready", 2))
            for s in range(T + 5):
                if s < T:
                    dve.wait_ge(*at("n2_s", NH4 * (s + 1)))
                    if s >= 4:
                        dve.wait_ge(*at("n2_pt", s - 3))
                    v = pS[:, s % 4, :].rearrange("p (h k) -> p h k", h=NH4)
                    dve.tensor_tensor(v, ps[:, s % 2, :].rearrange("p (h k) -> p h k", h=NH4),
                                      band[:, :].unsqueeze(1).broadcast_to([P, NH4, P]), ALU.add).then_inc(S("n2_sr"), 1)
                    dve.wait_ge(*at("n2_sr", s + 1))
                    dve.tensor_reduce(nmx[:, s, 0:NH4], v, AX.X, ALU.max, negate=True).then_inc(S("n2_nmx"), 1)
                t = s - 1
                if 0 <= t < T:
                    dve.wait_ge(*at("n2_pt", t + 1))
                    if t >= 4:
                        dve.wait_ge(*at("n2_pv", t - 3))
                    dve.tensor_copy(pT[:, t % 4, :], ps[:, 2 + t % 2, :]).then_inc(S("n2_ptd"), 1)
                t = s - 2
                if 0 <= t < T:
                    dve.wait_ge(*at("n2_pv", t + 1))
                    normalise("n2", t, 4 + t % 2, NH4, HD4)
                t = s - 4
                if 0 <= t < T:
                    dve.wait_ge(*at("n2_proj", t + 1))
                    dve.tensor_tensor(aK[:, t, :], ps[:, 7, 0:P], aK[:, t, :], ALU.add).then_inc(S("n2_add"), 1)
            dve.wait_ge(*at("n2_add", T))

            def over_experts(v):
                return v.unsqueeze(2).broadcast_to([P, T, E])

            def rank_experts(pre, k, bank):
                dve.wait_ge(*at(f"{pre}_lg_ps", 1))
                link(dve.tensor_tensor(lg[:, :, :], ps[:, bank, 0:T * E].rearrange("p (t e) -> p t e", e=E),
                                       rrow[:, k, :].unsqueeze(1).broadcast_to([P, T, E]), ALU.add))
                link(dve.tensor_reduce(lm[:, :], lg[:, :, :], AX.X, ALU.max))
                dve.tensor_tensor(lg[:, :, :], lg[:, :, :], over_experts(lm[:, :]), ALU.subtract).then_inc(S(f"{pre}_lg"), 1)
                dve.wait_ge(*at(f"{pre}_lg", 1))
                for t in range(T):
                    li = lg[:, t, :].unsqueeze(2).broadcast_to([P, E, E])
                    lj = lg[:, t, :].unsqueeze(1).broadcast_to([P, E, E])
                    dve.tensor_tensor(cmp_[:, t, :, :], lj, li, ALU.is_gt).then_inc(S(f"{pre}_cmp"), 1)
                    dve.tensor_tensor(cm2[:, t, :, :], lj, li, ALU.is_equal).then_inc(S(f"{pre}_cmp"), 1)
                dve.wait_ge(*at(f"{pre}_cmp", 2 * T))
                link(dve.tensor_tensor(cm2[:, :, :, :], cm2[:, :, :, :],
                                       tril8[:, :, :].unsqueeze(1).broadcast_to([P, T, E, E]), ALU.mult))
                link(dve.tensor_tensor(cmp_[:, :, :, :], cmp_[:, :, :, :], cm2[:, :, :, :], ALU.add))
                link(dve.tensor_reduce(rank[:, :, :], cmp_[:, :, :, :], AX.X, ALU.add))

            def accumulate(pre, acc):
                for e in range(E):
                    for t in range(T):
                        if t % 4 == 0:
                            dve.wait_ge(*at(f"{pre}_fc2", 2 * e + t // 4 + 1))
                        if e:
                            dve.wait_ge(*at(f"{pre}_acc", T * (e - 1) + t + 1))
                        dve.scalar_tensor_tensor(acc[:, t, :], ps[:, 4 + 2 * (e % 2) + t // 4, P * (t % 4):P * (t % 4) + P],
                                                 cw[:, t, e:e + 1], acc[:, t, :],
                                                 ALU.mult, ALU.add).then_inc(S(f"{pre}_acc"), 1)

            layer_norm(lambda t: aK[:, t, :], bK, "nb_norm")
            dve.wait_ge(*at("nb_norm", T))
            layer_norm(lambda t: bK[:, t, :], cK, "nn_norm")
            rank_experts("m2", 0, 4)
            dve.wait_ge(*at("m2_ex", 1))
            link(dve.scalar_tensor_tensor(ex[:, :, :], rank[:, :, :], 2.0, ex[:, :, :], ALU.is_lt, ALU.mult))
            link(dve.tensor_reduce(sm[:, :], ex[:, :, :], AX.X, ALU.add))
            link(dve.reciprocal(rsm[:, :], sm[:, :]))
            dve.tensor_tensor(cw[:, :, :], ex[:, :, :], over_experts(rsm[:, :]), ALU.mult).then_inc(S("m2_cw"), 1)
            for i in range(2):
                dve.wait_ge(*at("m2_b2_ps", i + 1))
                v = aK[:, 4 * i:4 * i + 4, :]
                dve.tensor_tensor(v, ps[:, 6 + i, :].rearrange("p (t c) -> p t c", t=4), v, ALU.add).then_inc(S("m2_b2"), 1)
            dve.wait_ge(*at("m2_b2", 2))
            accumulate("m2", aK)
            dve.wait_ge(*at("m2_acc", T * E))

            layer_norm(lambda t: aK[:, t, :], bK, "nc_norm")
            for i in range(2):
                dve.wait_ge(*at("n3_q_ps", i + 1))
                dve.tensor_scalar(aT[0:U, HALF * i:HALF * i + HALF], ps[0:U, 2 + i, :], U ** -0.5, None,
                                  ALU.mult).then_inc(S("n3_q"), 1)
            evac_values("n3_v_ps", "n3_v", (6, 7), lambda i: vaug1[:, 4 * i:4 * i + 4, 0:U].unsqueeze(2))
            dve.wait_ge(*at("xb3_ready", 2))
            for s in range(T + 5):
                if s < T:
                    dve.wait_ge(*at("n3_s", s + 1))
                    dve.tensor_reduce(nmx[:, s, 0:1], ps[:, 0:2, :], AX.XY, ALU.max, negate=True).then_inc(S("n3_nmx"), 1)
                t = s - 1
                if 0 <= t < T:
                    dve.wait_ge(*at("n3_pt", 2 * t + 1))
                    if t >= 2:
                        dve.wait_ge(*at("n3_pv", t - 1))
                    dve.tensor_copy(pT[:, 2 * (t % 2), :], ps[:, 2, :]).then_inc(S("n3_ptd"), 1)
                t = s - 2
                if 0 <= t < T:
                    dve.wait_ge(*at("n3_pv", t + 1))
                    normalise("n3", t, 4 + t % 2, 1, U)
                t = s - 4
                if 0 <= t < T:
                    dve.wait_ge(*at("n3_proj", t + 1))
                    dve.tensor_tensor(aK[:, t, :], ps[:, 6 + t % 2, 0:P], aK[:, t, :], ALU.add).then_inc(S("n3_add"), 1)
            dve.wait_ge(*at("n3_add", T))

            layer_norm(lambda t: aK[:, t, :], bK, "nd_norm")
            rank_experts("m3", 1, 2)
            dve.tensor_scalar(rank[:, :, :], rank[:, :, :], 1.0, None, ALU.is_lt).then_inc(S("m3_hot"), 1)
            dve.wait_ge(*at("m3_hot", 1))
            dve.wait_ge(*at("m3_ex", 1))
            link(dve.tensor_reduce(sm[:, :], ex[:, :, :], AX.X, ALU.add))
            link(dve.reciprocal(rsm[:, :], sm[:, :]))
            link(dve.tensor_tensor(ex[:, :, :], ex[:, :, :], over_experts(rsm[:, :]), ALU.mult))
            link(dve.tensor_tensor(ex[:, :, :], ex[:, :, :], rank[:, :, :], ALU.mult))
            dve.wait_ge(*at("m3_pos", 1))
            dve.scalar_tensor_tensor(cw[:, :, :], ps[:, 3, 0:T * E].rearrange("p (t e) -> p t e", e=E), float(CAP) + 0.5,
                                     ex[:, :, :], ALU.is_lt, ALU.mult).then_inc(S("m3_cw"), 1)
            dve.wait_ge(*at("m3_cw", 1))
            dve.engine_nop().then_inc(S("m3_pos_read"), 1)
            for i in range(2):
                dve.wait_ge(*at("m3_b2_ps", i + 1))
                dve.tensor_copy(cK[:, 4 * i:4 * i + 4, :],
                                ps[:, 6 + i, :].rearrange("p (t c) -> p t c", t=4)).then_inc(S("m3_b2"), 1)
            dve.wait_ge(*at("m3_b2", 2))
            accumulate("m3", cK)
            for t in range(T):
                dve.wait_ge(*at("m3_acc", T * (E - 1) + t + 1))
                y = cK[:, t, :]
                link(dve.tensor_tensor(nanm[:, t, :], y, y, ALU.not_equal))
                link(dve.copy_predicated(y, nanm[:, t, :], fills[:, 0, :]))
                link(dve.tensor_scalar(nanm[:, t, :], y, FMAX, None, ALU.is_gt))
                link(dve.copy_predicated(y, nanm[:, t, :], fills[:, 1, :]))
                link(dve.tensor_scalar(nanm[:, t, :], y, -FMAX, None, ALU.is_lt))
                link(dve.copy_predicated(y, nanm[:, t, :], fills[:, 2, :]))
                dve.tensor_tensor(aK[:, t, :], aK[:, t, :], y, ALU.add).then_inc(S("y_ready"), 1)


def kernel(**inputs):
    import numpy as _np
    import concourse.bacc as _bacc
    from concourse.bass_utils import run_bass_kernel_spmd as _run

    nc = _bacc.Bacc("TRN2", target_bir_lowering=False, num_devices=1)
    arrays, args = {}, {}
    for name, a in inputs.items():
        a = _np.ascontiguousarray(a)
        arrays[f"in_{name}_dram"] = a
        args[name] = nc.dram_tensor(f"in_{name}_dram", a.shape, mybir.dt.from_np(a.dtype), kind="ExternalInput").ap()
    out = nc.dram_tensor("out_0_dram", (1, IMG, IMG, P), F32, kind="ExternalOutput").ap()
    build(nc, args, out)
    r = _run(nc, [arrays], core_ids=[0])
    return r.results[0]["out_0_dram"]
```

```python
from contextlib import ExitStack

import concourse.bass as bass
from concourse import mybir

P = 128
IMG = 32
T = IMG * IMG // P
N = T * P
HALF = 512

F32 = mybir.dt.float32
F32R = mybir.dt.float32r
U32 = mybir.dt.uint32
U8 = mybir.dt.uint8
ALU = mybir.AluOpType
ACT = mybir.ActivationFunctionType
AX = mybir.AxisListType

NEG = -1.0e30
FMAX = 3.4028234e38

NH8, HD8 = 8, 16
NH4, HD4 = 4, 32
KW = 7
REL = 2 * KW - 1
ROWS = P // IMG
LR = 3 * ROWS
KV = 4
HEADS = T * NH8
N0_EXP, N0_T, N0_V = 8, 12, 14
N1_EXP, N1_T, N1_V = 2, 5, 7
O_COPY, O_TURN, O_NORM, O_BACK, O_TURNED, O_PROJECT, O_ADD = 8, 9, 10, 11, 12, 13, 14
N0_ACT, N1_ACT = 4, 2
RADIUS = 32
U = 64
E = 8
FH = 512
FC = FH // P
CAP = -(-5 * N // (4 * E))
SLOTS = E * CAP
SC = SLOTS // P
BIG = 3.0e38
TURNS = ((0, 3), (3, 5), (5, 8), (8, 10))
COMBINE = [(i, k) for part in range(2) for i in range(2) for k in range(SC // 2 * part, SC // 2 * (part + 1))]

VEC = {}
for _name, _cols in (("n0_q_b", 4), ("n0_k_b", 4), ("n1_q_b", 4), ("n1_k_b", 4), ("L0_conv_proj_b", 1),
                     ("L1_conv_bq_proj", 1), ("L1_conv_bk_proj", 1), ("L1_conv_bv_proj", 1),
                     ("L1_conv_conv_b", 1), ("L2_ffn_ln_g", E), ("L2_ffn_ln_b", E), ("L2_ffn_b1", E * FC),
                     ("L3_ffn_b1", E * FC), ("L3_ffn_b2", E)):
    VEC[_name] = (sum(c for _, c in VEC.values()), _cols)
NVEC = sum(c for _, c in VEC.values())

ROWVEC = ["L0_conv_v_b", "L1_conv_bv_a", "L1_conv_bo_a", "L1_conv_ln1_g", "L1_conv_ln1_b", "L1_conv_ln2_g",
          "L1_conv_ln2_b", "L2_attn_bproj", "L3_attn_b_o"]
NROW = len(ROWVEC) * P + 2 * E

KINDS = {
    "turned_ps": [("x1t_ps", 2), ("n1t_ps", 2), ("gt_ps", 2), ("na_tps", 2), ("nb_tps", 2),
                  ("nn_tps", 2), ("nc_tps", 2), ("nd_tps", 2)],
    "product_ps": [("l1_qp_ps", 2), ("l1_kp_ps", 2),
                   ("l1_vp_ps", 2), ("conv_ps", 2), 
                   ("n2_q_ps", 2), ("n2_k_ps", 2), ("n3_q_ps", 2), ("n3_k_ps", 2)],
    "values_ps": [("n0_v_ps", 2), ("l1_v_ps", 2), ("n2_v_ps", 2), ("n3_v_ps", 2)],
    "act_copied": [ ("l1_qp", 2),
                   ("l1_vp", 2), ("gT_ready", 2), ("na_T", 2), ("n2_k", 2),
                   ("nb_T", 2), ("m2_xT", 2), ("nc_T", 2), ("n3_k", 2), ("nd_T", 2)],
    "dve_made": [("n0_v", 2), ("l1_kp", 2), ("loc_sum", 2), ("loc_ready", 1),
                 ("l1_v", 2), ("topi_ready", 1), ("x1_tok", 2), ("n1_tok", 2), ("g_tok", 2), ("n2_q", 2), ("n2_v", 2),
                 ("n3_q", 2), ("n3_v", 2)],
    "normalised": [("g0_norm", 2), ("g1_norm", 2)] + [(f"{x}_norm", T) for x in ("ln1", "ln2", "na", "nb", "nn", "nc", "nd")],
    "norm_stats": [(f"{x}_norm_st", T) for x in ("ln1", "ln2", "na", "nb", "nn", "nc", "nd")],
    "norm_gain": [("ln1_norm_gain", T), ("ln2_norm_gain", T)],
    "norm_mean": [(f"{x}_norm_mv", T) for x in ("ln1", "ln2", "na", "nb", "nn", "nc", "nd")],
    "pool_made": [("kvpad_zero", 1), ("kvpad_ready", 2), ("xb2_ready", 2),
                  ("xb3_ready", 2)],
    "stack_ps": [("n0_st_ps", 16), ("n1_st_ps", 16)],
    "stack_keys": [("n0_xk", 8), ("n1_xk", 8)],
    "stack_queries": [("n0_xq", 8), ("n1_xq", 8)],
    "stack_rounded": [("n0_xh", 16), ("n1_xh", 16)],
    "stacked": [("n0_st", 16), ("n1_st", 16)],
    "values_turned_ps": [("n0_vt", T), ("n1_vt", T)],
    "values_copied": [("n0_vc", T), ("n1_vc", T)],
    "queries_split": [("n0_qm", T), ("n1_qm", T), ("n2_qm", T)],
    "scores_ps": [("n0_s", HEADS), ("n1_s", HEADS), ("n2_s", T * NH4), ("n3_s", T)],
    "scores_read": [("n0_sr", HEADS), ("n2_sr", T)],
    "row_maxima": [("n0_nmx", T), ("n1_nmx", HEADS // 2), ("n2_nmx", T), ("n3_nmx", T)],
    "probabilities": [("n0_p", HEADS), ("n1_p", HEADS), ("n2_p", T * NH4), ("n3_p", T)],
    "turned_p_ps": [("n0_pt", HEADS), ("n1_pt", HEADS), ("n2_pt", T), ("n3_pt", 2 * T)],
    "turned_p_act": [("n0_pta", HEADS // N0_ACT), ("n1_pta", HEADS // N1_ACT), ("n3_pta", T)],
    "turned_p_dve": [("n0_ptd", HEADS - HEADS // N0_ACT), ("n1_ptd", HEADS - HEADS // N1_ACT), ("n2_ptd", T), ("n3_ptd", T)],
    "with_values_ps": [("n0_pv", HEADS // 4), ("n1_pv", HEADS // 4), ("n2_pv", T), ("n3_pv", T)],
    "output": [("n0_o", T), ("n1_o", T), ("n2_o", T), ("n3_o", T)],
    "turned_output_ps": [("n0_ot", T), ("n1_ot", T), ("n2_ot", T), ("n3_ot", T)],
    "turned_output": [("n0_oT", T), ("n1_oT", T), ("n2_oT", T), ("n3_oT", T)],
    "projected_ps": [("n0_proj", T), ("n1_proj", T), ("n2_proj", T), ("n3_proj", T)],
    "residual_added": [("n0_add", T), ("n1_add", T), ("n2_add", T), ("n3_add", T)],
}
for _kind, _count in (("lg_ps", 1), ("lg", 1), ("ex", 1), ("cmp", 2 * T)):
    KINDS["expert_" + _kind] = [(f"m2_{_kind}", _count), (f"m3_{_kind}", _count)]
PLACE = {name: (kind, sum(c for _, c in names[:i])) for kind, names in KINDS.items() for i, (name, _) in enumerate(names)}


class Chain:

    def __init__(self, eng, sem):
        self.eng, self.sem, self.n = eng, sem, 0

    def __call__(self, ins):
        self.n += 1
        ins.then_inc(self.sem, 1)
        self.eng.wait_ge(self.sem, self.n)


def build(nc, A, out):
    with ExitStack() as ctx:
        def sb(name, shape, dt=F32):
            return ctx.enter_context(nc.sbuf_tensor(name, shape, dt))

        sems = {}

        def S(name):
            name = PLACE.get(name, (name, 0))[0]
            if name not in sems:
                sems[name] = ctx.enter_context(nc.semaphore(name))
            return sems[name]

        def at(name, k):
            return S(name), PLACE.get(name, (name, 0))[1] + k

        ps = ctx.enter_context(nc.psum_tensor("ps", [P, 8, HALF], F32))

        ident = sb("ident", [P, P])
        ones = sb("ones", [P, P])
        upper = sb("upper", [P, P])
        band = sb("band", [P, P])
        gavg = sb("gavg", [P, P])
        mask2 = sb("mask2", [P, 2])
        neglo = sb("neglo", [P, 2])
        mask4 = sb("mask4", [P, NH4])
        tril8 = sb("tril8", [P, E, E])
        nhalf = sb("nhalf", [P, 8])
        first = sb("first", [P, 4 * P + NVEC])
        w0 = first[:, 0:4 * P].rearrange("p (a c) -> p a c", a=4)
        vcols = first[:, 4 * P:4 * P + NVEC]
        rows = sb("rows", [P, NROW])
        rrow = rows[:, len(ROWVEC) * P:NROW].rearrange("p (a e) -> p a e", a=2)
        w1 = sb("w1", [P, 7, P])
        convw = sb("convw", [P, 25, P])
        late = sb("late", [P, 4 * P + 3 * U + 2 * E])
        w2a = late[:, 0:3 * P]
        w2p = late[:, 3 * P:4 * P]
        w3q = late[:, 4 * P:4 * P + 3 * U].rearrange("p (a u) -> p a u", a=3)
        rout = late[:, 4 * P + 3 * U:].rearrange("p (a e) -> p a e", a=2)
        w3o = sb("w3o", [U, P])
        fw1 = sb("fw1", [P, E, FH])
        fw2 = sb("fw2", [P, E, FC, P])
        fb2 = sb("fb2", [E, P])
        onesr = sb("onesr", [P, P], F32R)
        rpbT = sb("rpbT", [33, NH8, REL + 2])
        cT = sb("cT", [P, N])
        shift = cT[0:33, :].rearrange("p (a b) -> p a b", a=IMG)
        rmask = sb("rmask", [P, 3, LR])
        arena = sb("arena", [P, 9216])
        tabs = sb("tabs", [P, 7168])
        tab_i = tabs[:, 0:3072].rearrange("p (h l j) -> p h l j", h=NH8, l=LR)
        tab_t = tabs[:, 3072:5120].rearrange("p (h l j) -> p h l j", h=NH8, l=8)
        tab_b = tabs[:, 5120:7168].rearrange("p (h l j) -> p h l j", h=NH8, l=8)

        cmp_ = tabs[:, 0:HALF].rearrange("p (t i j) -> p t i j", t=T, i=E)
        cm2 = tabs[:, HALF:N].rearrange("p (t i j) -> p t i j", t=T, i=E)
        eT = tabs[:, N:2 * N]
        bK = tabs[:, 2 * N:3 * N].rearrange("p (t c) -> p t c", t=T)
        cK = tabs[:, 3 * N:4 * N].rearrange("p (t c) -> p t c", t=T)
        cwT = tabs[0:E, 4 * N:5 * N]
        kvpad = tabs[:, 5 * N:5 * N + (IMG + 4) ** 2].rearrange("p (r w) -> p r w", r=IMG + 4)

        xT = sb("xT", [P, N])
        nT = sb("nT", [P, N])
        aT = sb("aT", [P, N])
        bT = sb("bT", [P, N])
        oT = sb("oT", [P, N])
        aK = sb("aK", [P, T, P])
        xK = aK
        VW = NH8 * (HD8 + 1) + 15
        vaug = sb("vaug", [P, T, VW])
        vfil = tabs[:, 5 * N:5 * N + 2 * KV * VW].rearrange("p (b r c) -> p b r c", b=2, r=KV)
        vaug4 = arena[:, 8 * HALF:8 * HALF + T * NH4 * (HD4 + 1)].rearrange("p (t h d) -> p t h d", t=T, h=NH4)
        vaug1 = tabs[:, 7168 - T * (U + 1):7168].rearrange("p (t d) -> p t d", t=T)
        qst = fw1[:, :, :].rearrange("p e h -> p (e h)").rearrange("p (g n) -> p g n", g=4)
        kr = sb("kr", [P, 4, N], F32R)
        kfil = kr[:, :, :].rearrange("p a n -> p (a n)").rearrange("p (b g n) -> p b g n", b=2, g=4)
        kst = arena[:, 8 * HALF:8 * HALF + 4 * N].rearrange("p (g n) -> p g n", g=4)
        qr = sb("qr", [P, 2, NH8, P], F32R)
        qm = arena[:, 7168:7168 + 2 * NH4 * P].rearrange("p (b h n) -> p b h n", b=2, h=NH4)
        vsb = sb("vsb", [P, 2, P])
        pS8 = arena[:, 0:8 * HALF].rearrange("p (a k) -> p a k", a=8)
        pS = arena[:, 0:4 * HALF].rearrange("p (a k) -> p a k", a=4)
        pT = sb("pT", [P, 8, HALF])
        oK = sb("oK", [P, 2, P])
        mx = sb("mx", [P, 2, 8])
        nmx = sb("nmx", [P, 16, 8])
        rs = sb("rs", [P, 2, 8])
        st = sb("st", [P, T, 6])
        mv = sb("mv", [P, T, 2])
        ge = sb("ge", [P, 2])
        gm = sb("gm", [P, 2])
        gv = sb("gv", [P, 1])
        grs = sb("grs", [P, 1])
        ve = sb("ve", [P, T])
        rstd = sb("rstd", [P, T])
        loc = sb("loc", [P, 2, T])
        sloc = sb("sloc", [T, 8])
        top8 = sb("top8", [T, 8])
        topi = sb("topi", [T, 8], U32)
        lg = sb("lg", [P, T, E])
        lm = sb("lm", [P, T])
        ex = sb("ex", [P, T, E])
        rank = sb("rank", [P, T, E])
        cw = sb("cw", [P, T, E])
        sm = sb("sm", [P, T])
        rsm = sb("rsm", [P, T])
        kept = sb("kept", [P, T, E])
        nanm = sb("nanm", [P, T, P], U8)
        fills = sb("fills", [P, 3, P])

        cflat = convw[:, :, :].rearrange("p k c -> p (k c)")
        places = cflat[:, 0:SLOTS]
        placecol = cflat[:, SLOTS:SLOTS + SC]
        placeoff = cflat[:, SLOTS + SC:SLOTS + SC + E]
        xpart = qr
        krf = kr[:, :, :].rearrange("p a n -> p (a n)")
        slot = sm
        slotd = krf[:, 2 * SLOTS:2 * SLOTS + N].rearrange("p (t n) -> p t n", t=T)
        slotrow = bT
        xg = arena[:, 0:SLOTS]
        yT = arena[:, SLOTS:2 * SLOTS]
        ypart = krf[:, 0:2 * SLOTS].rearrange("p (a k c) -> p a k c", a=2, k=SC)
        qrf = qr[:, :, :, :].rearrange("p a h n -> p (a h n)")

        def hid3(e):
            k = 2 * SLOTS + FC * CAP * (e % 2)
            return arena[:, k:k + FC * CAP].rearrange("p (c n) -> p c n", c=FC)

        def hot(t):
            return krf[:, SLOTS * (t % 2):SLOTS * (t % 2) + SLOTS]

        def hotT(i):
            i %= 6
            return qrf[:, HALF * i:HALF * i + HALF] if i < 4 else krf[:, 2 * SLOTS + HALF * (i - 4):2 * SLOTS + HALF * (i - 3)]

        out_v = out.rearrange("a (t r) w c -> (r w) (a t) c", t=T)

        def row(name):
            k = ROWVEC.index(name) * P
            return rows[:, k:k + P]

        def col(name, i=0):
            k = VEC[name][0] + i
            return vcols[:, k:k + 1]

        def halves(t):
            return t[:, 0:HALF], t[:, HALF:N]

        def n0_lo(t):
            return max(t - 1, 0)

        def n0_hi(t):
            return min(t + 2, T)

        def n0_w(m):
            return P * (n0_hi(m // NH8) - n0_lo(m // NH8))

        def arena_s(t):
            return arena[:, 3072 * (t % 3):3072 * (t % 3) + 3072].rearrange("p (h k) -> p h k", h=NH8)

        def hid(e):
            return arena[:, 4096 * (e % 2):4096 * (e % 2) + 4096].rearrange("p (c n) -> p c n", c=FC)

        def by_act(m, every):
            return m % every == every - 1

        def copied(eng, name, m, every):
            if by_act(m, every):
                eng.wait_ge(*at(f"{name}_pta", (m + 1) // every))
            else:
                eng.wait_ge(*at(f"{name}_ptd", m + 1 - (m + 1) // every))

        block = ctx.enter_context(nc.Block())

        @block.sync
        def _(sp):
            sp.dma_start(xT[:, :], A["xT"]).then_inc(S("x_in"), 16)
            sp.dma_start(first[:, :], A["first"]).then_inc(S("first_in"), 16)
            sp.wait_ge(*at("rpb_zero", 1))
            sp.dma_start(rpbT[0:REL, :, :], A["rpbT"]).then_inc(S("rpb_in"), 16)
            sp.dma_start(rows[:, :], A["rows"].partition_broadcast(P)).then_inc(S("row_in"), 16)
            sp.dma_start(w1[:, :, :], A["w1"]).then_inc(S("w1_in"), 16)
            sp.dma_start(convw[:, :, :], A["convw"]).then_inc(S("conv_in"), 16)
            sp.dma_start(late[:, :], A["late"]).then_inc(S("late_in"), 16)
            sp.dma_start(w3o[:, :], A["w3o"]).then_inc(S("w3_in"), 16)
            sp.dma_start(fb2[:, :], A["fb2"]).then_inc(S("fb2_in"), 16)
            sp.dma_start(fw2[:, :, :, :], A["m2_w2"]).then_inc(S("fw_in"), 16)
            sp.wait_ge(*at("n1_qm", T))
            sp.dma_start(fw1[:, :, :], A["m2_w1"]).then_inc(S("fw_in"), 16)
            for e in range(E):
                sp.wait_ge(*at("m2_fc1", 8 * (e + 1)))
                sp.dma_start(fw1[:, e, :], A["m3_w1"][:, e]).then_inc(S("fv_in"), 16)
                sp.wait_ge(*at("m2_fc2", 2 * (e + 1)))
                sp.dma_start(fw2[:, e, :, :], A["m3_w2"][:, e]).then_inc(S("fv_in"), 16)
            for i in range(2):
                sp.wait_ge(*at("y_ready", i + 1))
                sp.dma_start(out_v[:, 4 * i:4 * i + 4, :], aK[:, 4 * i:4 * i + 4, :]).then_inc(S("y_out"), 16)
            sp.wait_ge(*at("y_out", 2 * 16))

        @block.gpsimd
        def _(pool):
            link = Chain(pool, S("pool_chain"))

            def select(ap, pattern, base, mult, op=ALU.is_ge, fill=0.0):
                return pool.affine_select(out=ap, in_=ap, pattern=pattern, base=base, channel_multiplier=mult,
                                          compare_op=op, fill=fill)

            link(pool.memset(ident[:, :], 0.0))
            select(ident[:, :], [[-1, P]], 0, 1, ALU.not_equal, 1.0).then_inc(S("ident_ready"), 1)
            pool.wait_ge(*at("ident_ready", 1))
            link(pool.memset(shift[:, :, :], 0.0))
            link(select(shift[0:REL, :, :], [[-1, IMG], [1, IMG]], -(KW - 1), 1, ALU.not_equal, 1.0))
            lo, hi = IMG - KW, KW
            link(select(shift[32:33, 0:lo, :], [[1, lo], [-1, IMG]], KW // 2, 0, ALU.is_ge, NEG))
            link(select(shift[32:33, hi:IMG, :], [[-1, IMG - hi], [1, IMG]], KW // 2 - hi, 0, ALU.is_ge, NEG))
            pool.memset(rpbT[:, :, :], 0.0).then_inc(S("rpb_zero"), 1)
            pool.wait_ge(*at("rpb_zero", 1))
            pool.memset(rpbT[32:33, :, :], 1.0).then_inc(S("shift_ready"), 1)
            pool.wait_ge(*at("shift_ready", 1))
            link(pool.memset(gavg[:, :], 0.25))
            g = gavg[:, :].rearrange("p (g i) -> p g i", i=4)
            link(select(g, [[-4, P // 4], [0, 4]], 0, 1))
            select(g, [[4, P // 4], [0, 4]], 3, -1).then_inc(S("gavg_ready"), 1)
            pool.wait_ge(*at("gavg_ready", 1))
            link(pool.memset(nhalf[:, :], -0.5))
            link(pool.memset(rmask[:, :, :], NEG))
            for r in range(ROWS):
                link(pool.memset(rmask[32 * r:32 * r + 32, 0, r + 1:r + 1 + KW], 0.0))
            link(pool.memset(rmask[:, 1, ROWS:ROWS + KW], 0.0))
            pool.memset(rmask[:, 2, 1:1 + KW], 0.0).then_inc(S("rmask_ready"), 1)
            pool.wait_ge(*at("rmask_ready", 1))
            def root(i, src, dst, n):
                pool.wait_ge(*at("var_ready", i + 1))
                pool.tensor_tensor(dst, src, nhalf[:, 0:n], ALU.pow).then_inc(S("root_ready"), 1)
                pool.wait_ge(*at("root_ready", i + 1))

            link(pool.memset(neglo[:, :], 0.0))
            for q in (1, 3):
                link(pool.memset(neglo[32 * q:32 * q + 32, 0:1], -1.0))
            pool.memset(neglo[64:128, 1:2], -1.0).then_inc(S("neglo_ready"), 1)
            pool.wait_ge(*at("neglo_ready", 1))

            def copy(dst, src):
                return pool.tensor_scalar(dst, src, 1.0, 0.0, ALU.mult, ALU.add)

            def round_parts(name):
                for u in range(16):
                    pool.wait_ge(*at(f"{name}_xq" if u % 2 else f"{name}_xk", u // 2 + 1))
                    copy(pT[:, 4 + u % 4, :].bitcast(F32R), pT[:, u % 4, :]).then_inc(S(f"{name}_xh"), 1)
                    pool.wait_ge(*at(f"{name}_xh", u + 1))

            root(0, gv[:, :], grs[:, :], 1)
            link(pool.memset(mask2[:, :], 1.0))
            for q in range(4):
                m = mask2[32 * q:32 * q + 32, :]
                link(select(m, [[-HD8, 2]], 0, 1))
                link(select(m, [[HD8, 2]], HD8 - 1, -1))
            link(pool.memset(mask4[:, :], 1.0))
            link(select(mask4[:, :], [[-HD4, NH4]], 0, 1))
            link(select(mask4[:, :], [[HD4, NH4]], HD4 - 1, -1))
            pool.memset(vaug[:, :, :], 1.0).then_inc(S("ones_cols"), 1)
            pool.wait_ge(*at("ones_cols", 1))

            def small_consts():
                link(pool.memset(ones[:, :], 1.0))
                link(pool.memset(upper[:, :], 1.0))
                link(select(upper[:, :], [[1, P]], 0, -1))
                link(pool.memset(band[:, :], 0.0))
                link(select(band[:, :], [[-1, P]], 0, 1, ALU.is_ge, NEG))
                link(select(band[:, :], [[1, P]], RADIUS, -1, ALU.is_ge, NEG))
                link(pool.memset(tril8[:, :, :], 1.0))
                link(select(tril8[:, :, :], [[1, E], [-1, E]], -1, 0))
                for i, v in enumerate((0.0, 10000.0, -10000.0)):
                    link(pool.memset(fills[:, i, :], v))

            def split_stacks(name):
                for t in range(T):
                    if t == 0:
                        pool.wait_ge(*at(f"{name}_st", 16))
                    if t >= 2:
                        pool.wait_ge(*at(f"{name}_s", NH8 * (t - 1)))
                    pool.tensor_tensor(qr[:, t % 2, :, :].rearrange("p (g a) n -> p g a n", a=2),
                                       qst[:, :, P * t:P * t + P].unsqueeze(2).broadcast_to([P, 4, 2, P]),
                                       mask2[:, :].unsqueeze(1).unsqueeze(3).broadcast_to([P, 4, 2, P]),
                                       ALU.mult).then_inc(S(f"{name}_qm"), 1)
                    pool.wait_ge(*at(f"{name}_qm", t + 1))
                    if name == "n1":
                        if t >= 2:
                            pool.wait_ge(*at("n1_pv", 2 * (t - 1)))
                        for j in range(KV):
                            r = pool.value_load(topi[t:t + 1, j:j + 1], min_val=0, max_val=T - 1)
                            pool.tensor_tensor(vfil[:, t % 2, j:j + 1, :], vaug[:, bass.ds(r, 1), :],
                                               ones[:, 0:1].unsqueeze(2).broadcast_to([P, 1, VW]),
                                               ALU.mult).then_inc(S("v_gathered"), 1)
                            pool.wait_ge(*at("v_gathered", KV * t + j + 1))

            def split_heads(name, src, mask, nh, scores, tiles=T):
                for t in range(tiles):
                    if t == 0:
                        for i in (0, 1):
                            pool.wait_ge(*at(f"{name}_q", i + 1))
                    if t >= 2:
                        pool.wait_ge(*at(scores, nh * (t - 1)))
                    pool.tensor_tensor(qm[:, t % 2, 0:nh, :],
                                       src[:, P * t:P * t + P].unsqueeze(1).broadcast_to([P, nh, P]),
                                       mask[:, :].unsqueeze(2).broadcast_to([P, nh, P]),
                                       ALU.mult).then_inc(S(f"{name}_qm"), 1)
                    pool.wait_ge(*at(f"{name}_qm", t + 1))

            round_parts("n0")
            small_consts()
            split_stacks("n0")
            pool.wait_ge(*at("n0_sr", HEADS))
            pool.memset(kvpad[:, :, :], 0.0).then_inc(S("kvpad_zero"), 1)
            pool.memset(vaug1[:, :, U:U + 1], 1.0).then_inc(S("ones_cols"), 1)
            root(1, gv[:, :], grs[:, :], 1)
            pool.wait_ge(*at("l1_kp", 2))
            pool.wait_ge(*at("l1_vp", 2))
            pool.wait_ge(*at("kvpad_zero", 1))
            for i in range(2):
                pool.tensor_tensor(kvpad[:, 2 + 16 * i:18 + 16 * i, 2:2 + IMG],
                                   halves(bT)[i].rearrange("p (r w) -> p r w", w=IMG),
                                   halves(cT)[i].rearrange("p (r w) -> p r w", w=IMG),
                                   ALU.add).then_inc(S("kvpad_ready"), 1)
            round_parts("n1")
            pool.wait_ge(*at("topi_ready", 1))
            pool.wait_ge(*at("l1_v", 2))
            pool.wait_ge(*at("conv_ps", 2))
            split_stacks("n1")
            pool.wait_ge(*at("k_gathered", KV * T))
            pool.memset(vaug4[:, :, :, HD4:HD4 + 1], 1.0).then_inc(S("ones_cols"), 1)
            pool.wait_ge(*at("ones_cols", 3))
            root(2, ve[:, :], rstd[:, :], T)
            root(3, ve[:, :], rstd[:, :], T)
            root(4, ve[:, :], rstd[:, :], T)
            for t in range(0, T, 4):
                v = aK[:, t:t + 4, :]
                pool.wait_ge(*at("na_norm", t + 4))
                pool.tensor_tensor(v, v, row("L2_attn_bproj").unsqueeze(1).broadcast_to([P, 4, P]),
                                   ALU.add).then_inc(S("xb2_ready"), 1)
            split_heads("n2", aT, mask4, NH4, "n2_s")
            root(5, ve[:, :], rstd[:, :], T)
            root(6, ve[:, :], rstd[:, :], T)
            for e in range(E):
                dst = (bT, cT)[e % 2]
                if e == 0:
                    pool.wait_ge(*at("m2_xT", 2))
                if e >= 2:
                    pool.wait_ge(*at("m2_fc1", 8 * (e - 1)))
                pool.tensor_scalar(dst[:, :], nT[:, :], col("L2_ffn_ln_g", e), col("L2_ffn_ln_b", e),
                                   ALU.mult, ALU.add).then_inc(S("m2_xe"), 1)
            def count(dst, pattern, mult):
                return pool.iota(dst, pattern, base=0, channel_multiplier=mult, allow_small_or_imprecise_dtypes=True)

            count(places, [[1, SLOTS]], 0).then_inc(S("places_ready"), 1)
            count(placecol, [[P, SC]], 1).then_inc(S("places_ready"), 1)
            count(placeoff, [[CAP, E]], 0).then_inc(S("places_ready"), 1)
            copy(onesr[:, :], ones[:, :]).then_inc(S("places_ready"), 1)
            pool.wait_ge(*at("places_ready", 4))
            root(7, ve[:, :], rstd[:, :], T)
            for t in range(0, T, 4):
                v = aK[:, t:t + 4, :]
                pool.wait_ge(*at("nc_norm", t + 4))
                link(pool.tensor_tensor(v, v, row("L3_attn_b_o").unsqueeze(1).broadcast_to([P, 4, P]), ALU.add))
                pool.tensor_tensor(v, v, bK[:, t:t + 4, :], ALU.add).then_inc(S("xb3_ready"), 1)
            root(8, ve[:, :], rstd[:, :], T)
            pool.wait_ge(*at("nd_norm", T))
            pool.wait_ge(*at("x_high", 1))
            pool.tensor_tensor(xpart[:, 1, :, :], bK[:, :, :], xpart[:, 0, :, :].bitcast(F32), ALU.subtract).then_inc(S("x_low"), 1)
            pool.wait_ge(*at("m3_slot", 1))
            pool.tensor_tensor(slotd, ident[:, :].unsqueeze(1).broadcast_to([P, T, P]),
                               slot[:, :].unsqueeze(2).broadcast_to([P, T, P]), ALU.mult).then_inc(S("slot_diagonal"), 1)

        @block.scalar
        def _(act):
            def evac2(dst, banks, ready, done, bias=None):
                for i in range(2):
                    act.wait_ge(*at(ready, i + 1))
                    if bias is None:
                        ins = act.activation(halves(dst)[i], ps[:, banks[i], :], ACT.Copy)
                    else:
                        ins = act.activation(halves(dst)[i], ps[:, banks[i], :], ACT.Identity, bias=bias)
                    ins.then_inc(S(done), 1)

            def stack_keys(name):
                for k in range(8):
                    u = 2 * k
                    act.wait_ge(*at(f"{name}_st_ps", u + 1))
                    if u >= 4:
                        act.wait_ge(*at(f"{name}_st", u - 3))
                    act.activation(pT[:, u % 4, :], ps[:, u % 4, :], ACT.Identity,
                                   bias=col(f"{name}_k_b", k // 2)).then_inc(S(f"{name}_xk"), 1)

            act.wait_ge(*at("first_in", 16))
            stack_keys("n0")

            def evac_pT(name, m, w):
                act.wait_ge(*at(f"{name}_pt", m + 1))
                if m >= 8:
                    act.wait_ge(*at(f"{name}_pv", (m - 8) // 4 + 1))
                act.activation(pT[:, m % 8, 0:w], ps[:, 4 + m % 2, 0:w], ACT.Copy).then_inc(S(f"{name}_pta"), 1)

            def o_copy(name, t, bank, rows=P):
                act.wait_ge(*at(f"{name}_ot", t + 1))
                act.activation(oT[0:rows, P * t:P * t + P], ps[0:rows, bank, 0:P], ACT.Copy).then_inc(S(f"{name}_oT"), 1)

            def output_steps(name, s):
                t, r = divmod(s - O_COPY, NH8)
                if r == 0 and 0 <= t < T:
                    act.wait_ge(*at(f"{name}_pv", 2 * t + 2))
                    act.activation(vsb[:, :, :], ps[:, 6 + t % 2, 0:2 * P].rearrange("p (a n) -> p a n", a=2),
                                   ACT.Copy).then_inc(S(f"{name}_vc"), 1)
                t, r = divmod(s - O_TURNED, NH8)
                if r == 0 and 0 <= t < T:
                    o_copy(name, t, 6 + t % 2)

            for s in range(HEADS + N0_V + 17):
                n = s - N0_EXP
                if 0 <= n < HEADS:
                    t, h = divmod(n, NH8)
                    act.wait_ge(*at("n0_nmx", t + 1))
                    v = arena_s(t)[:, h, 0:n0_w(n)]
                    act.activation(v, v, ACT.Exp, bias=nmx[:, t, h:h + 1]).then_inc(S("n0_p"), 1)
                m = s - N0_T
                if 0 <= m < HEADS and by_act(m, N0_ACT):
                    evac_pT("n0", m, n0_w(m))
                output_steps("n0", s - N0_V)

            evac2(aT, (0, 1), "l1_qp_ps", "l1_qp", col("L1_conv_bq_proj"))
            evac2(cT, (4, 5), "l1_vp_ps", "l1_vp", col("L1_conv_bv_proj"))
            stack_keys("n1")
            evac2(eT, (4, 5), "conv_ps", "gT_ready", col("L1_conv_conv_b"))

            for s in range(HEADS + N1_V + 17):
                n = s - N1_EXP
                if 0 <= n < HEADS:
                    act.wait_ge(*at("n1_nmx", n // 2 + 1))
                    if n >= 8:
                        act.wait_ge(*at("n1_pt", n - 7))
                    act.activation(pS8[:, n % 8, :], ps[:, n % 4, :], ACT.Exp,
                                   bias=nmx[:, n // 2 % 16, n % 2:n % 2 + 1]).then_inc(S("n1_p"), 1)
                m = s - N1_T
                if 0 <= m < HEADS and by_act(m, N1_ACT):
                    evac_pT("n1", m, HALF)
                output_steps("n1", s - N1_V)
            evac2(nT, (0, 1), "na_tps", "na_T")
            evac2(bT, (4, 5), "n2_k_ps", "n2_k")
            for s in range(T + 4):
                if s < T:
                    act.wait_ge(*at("n2_nmx", s + 1))
                    for h in range(NH4):
                        v = pS[:, s % 4, P * h:P * h + P]
                        act.activation(v, v, ACT.Exp, bias=nmx[:, s, h:h + 1]).then_inc(S("n2_p"), 1)
                if s >= 4:
                    o_copy("n2", s - 4, 6)

            def router_exp(pre):
                act.wait_ge(*at(f"{pre}_lg", 1))
                act.activation(ex[:, :, :], lg[:, :, :], ACT.Exp).then_inc(S(f"{pre}_ex"), 1)

            def expert_layer(pre, func):
                router_exp(pre)
                for e in range(E):
                    for c in range(2 * FC):
                        act.wait_ge(*at(f"{pre}_fc1", 2 * FC * e + c + 1))
                        if e >= 2 and c == 0:
                            act.wait_ge(*at(f"{pre}_fc2", 2 * (e - 1)))
                        act.activation(hid(e)[:, c // 2, HALF * (c % 2):HALF * (c % 2) + HALF], ps[:, c % 4, :], func,
                                       bias=col("L2_ffn_b1", FC * e + c // 2)
                                       ).then_inc(S(f"{pre}_h"), 1)
                    if e == 0:
                        for i in range(2):
                            act.wait_ge(*at(f"{pre}_cwt_ps", i + 1))
                            act.activation(cwT[:, HALF * i:HALF * i + HALF], ps[0:E, 4 + i, :],
                                           ACT.Copy).then_inc(S(f"{pre}_cwT"), 1)

            evac2(oT, (0, 1), "nb_tps", "nb_T")
            evac2(nT, (2, 3), "nn_tps", "m2_xT")
            expert_layer("m2", ACT.Gelu)

            evac2(nT, (0, 1), "nc_tps", "nc_T")
            for i in range(2):
                act.wait_ge(*at("n3_k_ps", i + 1))
                act.activation(bT[0:U, HALF * i:HALF * i + HALF], ps[0:U, 4 + i, :], ACT.Copy).then_inc(S("n3_k"), 1)
            for s in range(T + 3):
                if s < T:
                    act.wait_ge(*at("n3_nmx", s + 1))
                    if s >= 2:
                        act.wait_ge(*at("n3_pt", 2 * (s - 1)))
                    act.activation(pS[:, 2 * (s % 2):2 * (s % 2) + 2, :], ps[:, 2 * (s % 2):2 * (s % 2) + 2, :], ACT.Exp,
                                   bias=nmx[:, s, 0:1]).then_inc(S("n3_p"), 1)
                if s >= 3:
                    o_copy("n3", s - 3, 6 + (s - 3) % 2, U)
                t = s - 1
                if 0 <= t < T:
                    act.wait_ge(*at("n3_pt", 2 * t + 2))
                    if t >= 2:
                        act.wait_ge(*at("n3_pv", t - 1))
                    act.activation(pT[:, 2 * (t % 2) + 1, :], ps[:, 5, :], ACT.Copy).then_inc(S("n3_pta"), 1)

            evac2(nT, (0, 1), "nd_tps", "nd_T")
            act.activation(xpart[:, 0, :, :], bK[:, :, :], ACT.Copy).then_inc(S("x_high"), 1)
            router_exp("m3")
            for c in (0, 2):
                act.wait_ge(*at("m3_gathered", T))
                w = min(HALF, SLOTS - HALF * c)
                act.activation(xg[:, HALF * c:HALF * c + w], ps[:, c, 0:w], ACT.Copy).then_inc(S("m3_xg_act"), 1)
            act.wait_ge(*at("slotrow_ps", 1))
            act.activation(slotrow[:, :].rearrange("p (a n) -> p a n", a=2), ps[:, 6:8, :], ACT.Copy).then_inc(S("slotrow"), 1)

            def turned_high(g):
                act.wait_ge(*at("m3_turned_ps", g + 1))
                k0, k1 = TURNS[g]
                act.activation(ypart[:, 0, k0:k1, :], ps[:, 1 + g % 2, 0:P * (k1 - k0)].rearrange("p (k c) -> p k c", c=P),
                               ACT.Copy).then_inc(S("m3_high"), 1)

            for e in range(E):
                for c in range(FC):
                    act.wait_ge(*at("m3_fc1", 2 * e + c // 2 + 1))
                    if e >= 2 and c == 0:
                        act.wait_ge(*at("m3_fc2", e - 1))
                    act.activation(hid3(e)[:, c, :], ps[:, 3 + 2 * (e % 2) + c // 2, CAP * (c % 2):CAP * (c % 2) + CAP],
                                   ACT.Relu, bias=col("L3_ffn_b1", FC * e + c)).then_inc(S("m3_h"), 1)
                if e == E - 2:
                    turned_high(0)
                    turned_high(1)
            turned_high(2)
            turned_high(3)
            for i in range(2):
                act.wait_ge(*at("m3_combined", 15 + 5 * i))
                act.activation(halves(cT)[i], ps[:, 3 + i, :], ACT.Copy).then_inc(S("m3_outT"), 1)

        @block.tensor
        def _(pe):
            def mm(dst, lhsT, rhs, start=True, stop=True):
                return pe.matmul(dst, lhsT, rhs, start=start, stop=stop, skip_group_check=True)

            def turn4(bank, srcs, cols=P, rows=P):
                for j, src in enumerate(srcs):
                    ins = pe.transpose(ps[0:rows, bank, cols * j:cols * j + cols], src, ident[0:cols, 0:cols])
                return ins

            def product(ready, banks, w, src, rows=P):
                for i in range(2):
                    mm(ps[0:rows, banks[i], :], w, halves(src)[i]).then_inc(S(ready), 1)

            def values(ready, banks, src, w, n):
                for t in range(T):
                    ins = mm(ps[:, banks[t // 4], n * (t % 4):n * (t % 4) + n], src[:, P * t:P * t + P], w)
                    if t % 4 == 3:
                        ins.then_inc(S(ready), 1)

            def tokens_to_channels(ready, banks, src, norm):
                for i in range(2):
                    pe.wait_ge(*at(norm, 4 * i + 4))
                    turn4(banks[i], [src[:, 4 * i + j, :] for j in range(4)]).then_inc(S(ready), 1)

            def bias_columns(part):
                if part == 0:
                    pe.wait_ge(*at("shift_ready", 1))
                    pe.wait_ge(*at("rpb_in", 16))
                if part:
                    pe.wait_ge(*at("tab_ready", 3))
                for jj in range(16):
                    for r in range(ROWS):
                        ins = mm(ps[32 * r:32 * r + 32, 4 + jj // 4, 128 * (jj % 4):128 * (jj % 4) + NH8 * LR],
                                 shift[:, 16 * part + jj, :], rpbT[:, :, 3 - r:3 - r + LR])
                ins.then_inc(S("bias_ps"), 1)

            bias_columns(0)

            def group_average(i, bank):
                if i == 0:
                    pe.wait_ge(*at("gavg_ready", 1))
                pe.wait_ge(*at("gn_stats", i + 1))
                mm(ps[:, bank, 0:2], gavg[:, :], ge[:, :]).then_inc(S("gn_avg"), 1)

            group_average(0, 3)
            pe.wait_ge(*at("first_in", 16))
            pe.wait_ge(*at("g0_norm", 2))
            pe.wait_ge(*at("gn_read", 1))

            def stack_products(name, k_src, k_w, q_src, q_w):
                for u in range(16):
                    w, src = (q_w, q_src) if u % 2 else (k_w, k_src)
                    g, i = divmod(u // 2, 2)
                    if u >= 4:
                        pe.wait_ge(*at(f"{name}_xq" if u % 2 else f"{name}_xk", (u - 4) // 2 + 1))
                    for q in range(4):
                        ins = mm(ps[32 * q:32 * q + 32, u % 4, :], w[:, 32 * g:32 * g + 32], halves(src)[i])
                    ins.then_inc(S(f"{name}_st_ps"), 1)

            stack_products("n0", nT, w0[:, 1, :], nT, w0[:, 0, :])
            pe.wait_ge(*at("n0_xk", 8))
            pe.wait_ge(*at("n0_xq", 8))
            values("n0_v_ps", (0, 1), nT, w0[:, 2, :], P)
            bias_columns(1)
            pe.wait_ge(*at("n0_st", 16))
            pe.wait_ge(*at("n0_v", 2))
            pe.wait_ge(*at("tab_ready", 6))

            pe.wait_ge(*at("ones_cols", 1))

            def attention(name, scores, s_free, t_lag, v_lag, srcs, values_of, every, project):
                for s in range(HEADS + v_lag + 17):
                    t, r = divmod(s - v_lag - O_TURN, NH8)
                    if r == 0 and 0 <= t < T:
                        pe.wait_ge(*at(f"{name}_vc", t + 1))
                        for i in range(2):
                            ins = pe.transpose(ps[:, 6 + t % 2, P * i:P * i + P], vsb[:, i, :], ident[:, :])
                        ins.then_inc(S(f"{name}_vt"), 1)
                    t, r = divmod(s - v_lag - O_PROJECT, NH8)
                    if r == 0 and 0 <= t < T:
                        pe.wait_ge(*at(f"{name}_oT", t + 1))
                        project(t, ps[:, 6 + t % 2, 0:P]).then_inc(S(f"{name}_proj"), 1)
                    t, r = divmod(s - v_lag - O_BACK, NH8)
                    if r == 0 and 0 <= t < T:
                        pe.wait_ge(*at(f"{name}_o", t + 1))
                        pe.transpose(ps[:, 6 + t % 2, 0:P], oK[:, t % 2, :], ident[:, :]).then_inc(S(f"{name}_ot"), 1)
                    if s < HEADS:
                        t, h = divmod(s, NH8)
                        if h == 0:
                            pe.wait_ge(*at(f"{name}_qm", t + 1))
                            if name == "n1":
                                pe.wait_ge(*at("k_gathered", KV * (t + 1)))
                        if s >= 4:
                            pe.wait_ge(*at(s_free, s - 3))
                        scores(t, h, ps[:, s % 4, :]).then_inc(S(f"{name}_s"), 1)
                    m = s - t_lag
                    if 0 <= m < HEADS:
                        pe.wait_ge(*at(f"{name}_p", m + 1))
                        if m >= 2:
                            copied(pe, name, m - 2, every)
                        turn4(4 + m % 2, srcs(m)).then_inc(S(f"{name}_pt"), 1)
                    m = s - v_lag
                    if 0 <= m < HEADS and m % 4 == 3:
                        t, h = divmod(m - 3, NH8)
                        for i in range(4):
                            copied(pe, name, m - 3 + i, every)
                        if h == 0 and t >= 2:
                            pe.wait_ge(*at(f"{name}_add", t - 1))
                        if h == 0 and name == "n1":
                            pe.wait_ge(*at("v_gathered", KV * (t + 1)))
                        vs = values_of(t)
                        for j, v in enumerate(vs):
                            for i in range(4):
                                k = (HD8 + 1) * (h + i)
                                ins = mm(ps[32 * i:32 * i + 32, 6 + t % 2, P * (h // 4):P * (h // 4) + P], v[:, k:k + 32],
                                         pT[:, (m - 3 + i) % 8, P * j:P * j + P], start=j == 0, stop=j == len(vs) - 1)
                        ins.then_inc(S(f"{name}_pv"), 1)

            def n0_scores(t, h, bank):
                return mm(bank[:, 0:P * (n0_hi(t) - n0_lo(t))], qr[:, t % 2, h, :], kr[:, h // 2, P * n0_lo(t):P * n0_hi(t)])

            attention("n0", n0_scores, "n0_sr", N0_T, N0_V,
                      lambda m: [arena_s(m // NH8)[:, m % NH8, P * j:P * j + P] for j in range(n0_w(m) // P)],
                      lambda t: [vaug[:, k, :] for k in range(n0_lo(t), n0_hi(t))], N0_ACT,
                      lambda t, bank: mm(bank, w0[:, 3, :], oT[:, P * t:P * t + P]))

            group_average(1, 2)
            pe.wait_ge(*at("w1_in", 16))
            pe.wait_ge(*at("g1_norm", 2))
            product("l1_qp_ps", (0, 1), w1[:, 0, :], nT)
            pe.wait_ge(*at("gn_read", 2))
            product("l1_kp_ps", (2, 3), w1[:, 1, :], nT)
            product("l1_vp_ps", (4, 5), w1[:, 2, :], nT)
            pe.wait_ge(*at("l1_qp", 2))
            pe.wait_ge(*at("l1_kp", 2))
            stack_products("n1", bT, w1[:, 4, :], aT, w1[:, 3, :])
            pe.wait_ge(*at("loc_ready", 1))
            pe.wait_ge(*at("l1_vp", 2))
            mm(ps[0:T, 6, 0:T], loc[:, 0, :], loc[:, 1, :]).then_inc(S("sloc_ps"), 1)
            pe.wait_ge(*at("n1_xk", 8))
            pe.wait_ge(*at("n1_xq", 8))
            values("l1_v_ps", (0, 1), cT, w1[:, 5, :], P)
            pe.wait_ge(*at("l1_v", 2))
            for i in range(2):
                turn4(i, [halves(xT)[i][:, P * j:P * j + P] for j in range(4)]).then_inc(S("x1t_ps"), 1)
            for i in range(2):
                turn4(2 + i, [halves(nT)[i][:, P * j:P * j + P] for j in range(4)]).then_inc(S("n1t_ps"), 1)
            pe.wait_ge(*at("conv_in", 16))
            pe.wait_ge(*at("kvpad_ready", 2))
            for i in range(2):
                for k in range(25):
                    dy, dx = divmod(k, 5)
                    ins = mm(ps[:, 4 + i, :], convw[:, k, :], kvpad[:, 16 * i + dy:16 * i + dy + 16, dx:dx + IMG],
                             start=k == 0, stop=k == 24)
                ins.then_inc(S("conv_ps"), 1)
            pe.wait_ge(*at("topi_ready", 1))
            for i in range(2):
                pe.wait_ge(*at("gT_ready", i + 1))
                turn4(6 + i, [halves(eT)[i][:, P * j:P * j + P] for j in range(4)]).then_inc(S("gt_ps"), 1)
            pe.wait_ge(*at("x1_tok", 2))
            pe.wait_ge(*at("n1_tok", 2))
            pe.wait_ge(*at("g_tok", 2))

            def n1_scores(t, h, bank):
                return mm(bank, qr[:, t % 2, h, :], kfil[:, t % 2, h // 2, :])

            attention("n1", n1_scores, "n1_p", N1_T, N1_V,
                      lambda m: [pS8[:, m % 8, P * j:P * j + P] for j in range(KV)], lambda t: [vfil[:, t % 2, j, :] for j in range(KV)], N1_ACT,
                      lambda t, bank: mm(bank, oT[:, P * t:P * t + P], w1[:, 6, :]))

            tokens_to_channels("na_tps", (0, 1), bK, "na_norm")
            pe.wait_ge(*at("late_in", 16))
            pe.wait_ge(*at("na_T", 2))
            product("n2_q_ps", (2, 3), w2a[:, 0:P], nT)
            product("n2_k_ps", (4, 5), w2a[:, P:2 * P], nT)
            values("n2_v_ps", (6, 7), nT, w2a[:, 2 * P:3 * P], P)
            pe.wait_ge(*at("n2_q", 2))
            pe.wait_ge(*at("n2_k", 2))
            pe.wait_ge(*at("n2_v", 2))
            for s in range(T + 5):
                if s < T:
                    pe.wait_ge(*at("n2_qm", s + 1))
                    if s >= 2:
                        pe.wait_ge(*at("n2_sr", s - 1))
                    for h in range(NH4):
                        mm(ps[:, s % 2, P * h:P * h + P], qm[:, s % 2, h, :],
                           bT[:, P * s:P * s + P]).then_inc(S("n2_s"), 1)
                t = s - 1
                if 0 <= t < T:
                    pe.wait_ge(*at("n2_p", NH4 * (t + 1)))
                    if t >= 2:
                        pe.wait_ge(*at("n2_ptd", t - 1))
                    turn4(2 + t % 2, [pS[:, t % 4, P * h:P * h + P] for h in range(NH4)]).then_inc(S("n2_pt"), 1)
                t = s - 2
                if 0 <= t < T:
                    pe.wait_ge(*at("n2_ptd", t + 1))
                    if t >= 2:
                        pe.wait_ge(*at("n2_o", t - 1))
                    for h in range(NH4):
                        ins = mm(ps[:, 4 + t % 2, 33 * h:33 * h + 33], pT[:, t % 4, P * h:P * h + P], vaug4[:, t, h, :])
                    ins.then_inc(S("n2_pv"), 1)
                t = s - 3
                if 0 <= t < T:
                    pe.wait_ge(*at("n2_o", t + 1))
                    if t >= 1:
                        pe.wait_ge(*at("n2_oT", t))
                    pe.transpose(ps[:, 6, 0:P], oK[:, t % 2, :], ident[:, :]).then_inc(S("n2_ot"), 1)
                t = s - 4
                if 0 <= t < T:
                    pe.wait_ge(*at("n2_oT", t + 1))
                    if t >= 1:
                        pe.wait_ge(*at("n2_add", t))
                    mm(ps[:, 7, 0:P], oT[:, P * t:P * t + P], w2p[:, :]).then_inc(S("n2_proj"), 1)

            def router(pre, k, bank, src):
                for t in range(T):
                    ins = mm(ps[:, bank, E * t:E * t + E], src[:, P * t:P * t + P], rout[:, k, :])
                ins.then_inc(S(f"{pre}_lg_ps"), 1)

            def experts(pre, x_of, x_ready, w_ready):
                def fc2(e):
                    w_ready(e, 1)
                    for t in range(T):
                        bank = 4 + 2 * (e % 2) + t // 4
                        if t % 4 == 0:
                            if e < 2:
                                pe.wait_ge(*at(f"{pre}_b2", 2))
                            else:
                                pe.wait_ge(*at(f"{pre}_acc", T * (e - 2) + t + 4))
                            pe.wait_ge(*at(f"{pre}_h", 2 * FC * (e + 1)))
                        for c in range(FC):
                            ins = mm(ps[:, bank, P * (t % 4):P * (t % 4) + P], hid(e)[:, c, P * t:P * t + P],
                                     fw2[:, e, c, :], start=c == 0, stop=c == FC - 1)
                        if t % 4 == 3:
                            ins.then_inc(S(f"{pre}_fc2"), 1)

                for e in range(E):
                    x_ready(e)
                    w_ready(e, 0)
                    for c in range(2 * FC):
                        g = 2 * FC * e + c
                        if g >= 4:
                            pe.wait_ge(*at(f"{pre}_h", g - 3))
                        mm(ps[:, c % 4, :], fw1[:, e, P * (c // 2):P * (c // 2) + P],
                           halves(x_of(e))[c % 2]).then_inc(S(f"{pre}_fc1"), 1)
                    if e == 0:
                        pe.wait_ge(*at(f"{pre}_cw", 1))
                        for i in range(2):
                            for j in range(4):
                                ins = pe.transpose(ps[0:E, 4 + i, P * j:P * j + P], cw[:, 4 * i + j, :], ident[:, :])
                            ins.then_inc(S(f"{pre}_cwt_ps"), 1)
                        pe.wait_ge(*at("fb2_in", 16))
                        for i in range(2):
                            pe.wait_ge(*at(f"{pre}_cwT", i + 1))
                            for j in range(4):
                                t = 4 * i + j
                                ins = mm(ps[:, 6 + i, P * j:P * j + P], cwT[:, P * t:P * t + P],
                                         fb2[:, :])
                            ins.then_inc(S(f"{pre}_b2_ps"), 1)
                    else:
                        fc2(e - 1)
                fc2(E - 1)

            tokens_to_channels("nb_tps", (0, 1), bK, "nb_norm")
            tokens_to_channels("nn_tps", (2, 3), cK, "nn_norm")
            pe.wait_ge(*at("nb_T", 2))
            router("m2", 0, 4, oT)
            pe.wait_ge(*at("m2_xT", 2))
            pe.wait_ge(*at("m2_lg", 1))

            def m2_w(e, second):
                pe.wait_ge(*at("fw_in", 32))

            experts("m2", lambda e: (bT, cT)[e % 2], lambda e: pe.wait_ge(*at("m2_xe", e + 1)), m2_w)

            tokens_to_channels("nc_tps", (0, 1), bK, "nc_norm")
            pe.wait_ge(*at("w3_in", 16))
            pe.wait_ge(*at("nc_T", 2))
            product("n3_q_ps", (2, 3), w3q[:, 0, :], nT, U)
            product("n3_k_ps", (4, 5), w3q[:, 1, :], nT, U)
            values("n3_v_ps", (6, 7), nT, w3q[:, 2, :], U)
            pe.wait_ge(*at("n3_q", 2))
            pe.wait_ge(*at("n3_k", 2))
            pe.wait_ge(*at("n3_v", 2))
            for s in range(T + 4):
                if s < T:
                    if s >= 2:
                        pe.wait_ge(*at("n3_p", s - 1))
                    for i in range(2):
                        ins = mm(ps[:, 2 * (s % 2) + i, :], aT[0:U, P * s:P * s + P], bT[0:U, HALF * i:HALF * i + HALF])
                    ins.then_inc(S("n3_s"), 1)
                t = s - 2
                if 0 <= t < T:
                    pe.wait_ge(*at("n3_ptd", t + 1))
                    pe.wait_ge(*at("n3_pta", t + 1))
                    if t >= 2:
                        pe.wait_ge(*at("n3_add", t - 1))
                    for k in range(T):
                        ins = mm(ps[:, 6 + t % 2, 0:U + 1], pT[:, 2 * (t % 2) + k // 4, P * (k % 4):P * (k % 4) + P],
                                 vaug1[:, k, :], start=k == 0, stop=k == T - 1)
                    ins.then_inc(S("n3_pv"), 1)
                t = s - 3
                if 0 <= t < T:
                    pe.wait_ge(*at("n3_o", t + 1))
                    pe.transpose(ps[0:U, 6 + t % 2, 0:P], oK[:, t % 2, 0:U], ident[:, :]).then_inc(S("n3_ot"), 1)
                t = s - 1
                if 0 <= t < T:
                    pe.wait_ge(*at("n3_p", t + 1))
                    for i in range(2):
                        if t >= 1:
                            pe.wait_ge(*at("n3_pta" if i else "n3_ptd", t))
                        turn4(4 + i, [pS[:, 2 * (t % 2) + i, P * j:P * j + P] for j in range(4)]).then_inc(S("n3_pt"), 1)
                t = s - 3
                if 0 <= t < T:
                    pe.wait_ge(*at("n3_oT", t + 1))
                    mm(ps[:, 6 + t % 2, 0:P], oT[0:U, P * t:P * t + P], w3o[:, :]).then_inc(S("n3_proj"), 1)

            tokens_to_channels("nd_tps", (0, 1), bK, "nd_norm")
            pe.wait_ge(*at("nd_T", 2))
            router("m3", 1, 2, nT)
            pe.wait_ge(*at("m3_hot", 1))
            ng = T * E
            mm(ps[:, 3, 0:ng], upper[:, :], rank[:, :, :], stop=False)
            for d in range(1, T):
                ins = mm(ps[:, 3, E * d:ng], ones[:, :], rank[:, 0:T - d, :], start=False, stop=d == T - 1)
            ins.then_inc(S("m3_pos"), 1)
            pe.wait_ge(*at("x_high", 1))
            pe.wait_ge(*at("x_low", 1))
            cuts = [(c, HALF * c, min(HALF * c + HALF, SLOTS)) for c in range(3)]
            for t in range(T):
                pe.wait_ge(*at("m3_hot_ready", t + 1))
                for a in range(2):
                    for c, k0, k1 in cuts:
                        ins = mm(ps[:, c, 0:k1 - k0], xpart[:, a, t, :], hot(t)[:, k0:k1],
                                 start=t == 0 and a == 0, stop=t == T - 1 and a == 1)
                ins.then_inc(S("m3_gathered"), 1)
            pe.wait_ge(*at("slot_diagonal", 1))
            pe.wait_ge(*at("places_ready", 4))
            for i in range(2):
                ins = mm(ps[:, 6 + i, :], onesr[:, :], slotd[:, 4 * i:4 * i + 4, :])
            ins.then_inc(S("slotrow_ps"), 1)

            def m3_fc2(e):
                pe.wait_ge(*at("m3_h", FC * (e + 1)))
                if e >= 2:
                    pe.wait_ge(*at("m3_y", e - 1))
                for c in range(FC):
                    ins = mm(ps[:, 0 if e % 2 else 7, 0:CAP], fw2[:, e, c, :], hid3(e)[:, c, :], start=c == 0, stop=c == FC - 1)
                ins.then_inc(S("m3_fc2"), 1)

            def m3_turn(g):
                k0, k1 = TURNS[g]
                pe.wait_ge(*at("m3_clean", g // 2 + 1))
                if g >= 2:
                    pe.wait_ge(*at("m3_low", g - 1))
                turn4(1 + g % 2, [yT[:, P * k:P * k + P] for k in range(k0, k1)]).then_inc(S("m3_turned_ps"), 1)

            def m3_combine(part):
                for j in range(SC):
                    n = SC * part + j
                    i, k = COMBINE[n]
                    g = [k < k1 for _, k1 in TURNS].index(True)
                    pe.wait_ge(*at("m3_high", g + 1))
                    pe.wait_ge(*at("m3_low", g + 1))
                    pe.wait_ge(*at("m3_hotT", n + 1))
                    for a in range(2):
                        ins = mm(ps[:, 3 + i, :], ypart[:, a, k, :], hotT(n), start=k == 0 and a == 0, stop=k == SC - 1 and a == 1)
                    ins.then_inc(S("m3_combined"), 1)

            pe.wait_ge(*at("fv_in", 2 * 16 * E))
            for e in range(E):
                if e == 0:
                    pe.wait_ge(*at("m3_xg_act", 2))
                    pe.wait_ge(*at("m3_xg_dve", 1))
                    pe.wait_ge(*at("slotrow", 1))
                if e >= 2:
                    pe.wait_ge(*at("m3_h", FC * (e - 1)))
                for c in range(FC):
                    ins = mm(ps[:, 3 + 2 * (e % 2) + c // 2, CAP * (c % 2):CAP * (c % 2) + CAP], fw1[:, e, P * c:P * c + P],
                             xg[:, CAP * e:CAP * e + CAP])
                    if c % 2:
                        ins.then_inc(S("m3_fc1"), 1)
                if e:
                    m3_fc2(e - 1)
                if e == E - 2:
                    m3_turn(0)
                    m3_turn(1)
            m3_fc2(E - 1)
            m3_combine(0)
            m3_turn(2)
            m3_turn(3)
            m3_combine(1)
            for i in range(2):
                pe.wait_ge(*at("m3_outT", i + 1))
                turn4(5 + i, [halves(cT)[i][:, P * j:P * j + P] for j in range(4)]).then_inc(S("m3_out_ps"), 1)

        @block.vector
        def _(dve):
            link = Chain(dve, S("dve_chain"))
            normed = [0]

            def group_norm(i, bank, norm):
                for k in range(2):
                    ins = dve.bn_stats(st[:, k, :], halves(xT)[k])
                    link(ins)
                link(dve.bn_aggr(mv[:, 0, :], st[:, 0:2, :]))
                link(dve.tensor_copy(ge[:, 0:1], mv[:, 0, 0:1]))
                dve.scalar_tensor_tensor(ge[:, 1:2], mv[:, 0, 0:1], mv[:, 0, 0:1], mv[:, 0, 1:2],
                                         ALU.mult, ALU.add).then_inc(S("gn_stats"), 1)
                dve.wait_ge(*at("gn_avg", i + 1))
                dve.tensor_copy(gm[:, :], ps[:, bank, 0:2]).then_inc(S("gn_read"), 1)
                dve.wait_ge(*at("gn_read", i + 1))
                link(dve.scalar_tensor_tensor(gv[:, :], gm[:, 0:1], gm[:, 0:1], gm[:, 1:2], ALU.mult, ALU.subtract))
                dve.tensor_scalar(gv[:, :], gv[:, :], -1.0, 1e-5, ALU.mult, ALU.add).then_inc(S("var_ready"), 1)
                normed[0] += 1
                dve.wait_ge(*at("root_ready", normed[0]))
                for k in range(2):
                    dve.tensor_scalar(halves(nT)[k], halves(xT)[k], gm[:, 0:1], grs[:, :],
                                      ALU.subtract, ALU.mult).then_inc(S(norm), 1)

            def token_stats(src, norm):
                for t in range(T):
                    dve.bn_stats(st[:, t, :], src[:, t, :]).then_inc(S(norm + "_st"), 1)
                for t in range(T):
                    dve.wait_ge(*at(norm + "_st", t + 1))
                    dve.bn_aggr(mv[:, t, :], st[:, t, :]).then_inc(S(norm + "_mv"), 1)
                dve.wait_ge(*at(norm + "_mv", T))
                dve.tensor_scalar(ve[:, :], mv[:, :, 1], 1e-5, None, ALU.add).then_inc(S("var_ready"), 1)

            def root_of_variance():
                normed[0] += 1
                dve.wait_ge(*at("root_ready", normed[0]))

            def layer_norm(src, dst, norm):
                token_stats(src, norm)
                root_of_variance()
                for t in range(T):
                    dve.tensor_scalar(dst[:, t, :], src[:, t, :], mv[:, t, 0:1], rstd[:, t:t + 1],
                                      ALU.subtract, ALU.mult).then_inc(S(norm), 1)

            dve.wait_ge(*at("x_in", 16))
            group_norm(0, 3, "g0_norm")
            dve.wait_ge(*at("rmask_ready", 1))

            def bias_tables(part):
                dve.wait_ge(*at("bias_ps", part + 1))
                x = ps[:, 4:8, :].rearrange("p b (q c) -> p (b q) c", c=128)[:, :, 0:NH8 * LR]
                x = x.rearrange("p j (h l) -> p h l j", l=LR)
                for k, (tab, l0, l1) in enumerate(((tab_i, 0, LR), (tab_t, ROWS, LR), (tab_b, 0, 8))):
                    for h in range(0, NH8, 4):
                        ins = dve.tensor_tensor(
                            tab[:, h:h + 4, :, 16 * part:16 * part + 16], x[:, h:h + 4, l0:l1, :],
                            rmask[:, k, l0:l1].unsqueeze(1).unsqueeze(3).broadcast_to([P, 4, l1 - l0, 16]), ALU.add)
                    ins.then_inc(S("tab_ready"), 1)

            bias_tables(0)

            def stack_queries(name):
                for u in range(16 + 3):
                    if u < 16 and u % 2:
                        dve.wait_ge(*at(f"{name}_st_ps", u + 1))
                        if u >= 4:
                            dve.wait_ge(*at(f"{name}_st", u - 3))
                        dve.tensor_scalar(pT[:, u % 4, :], ps[:, u % 4, :], col(f"{name}_q_b", u // 4), HD8 ** -0.5,
                                          ALU.add, ALU.mult).then_inc(S(f"{name}_xq"), 1)
                    v = u - 3
                    if v >= 0:
                        g, i = divmod(v // 2, 2)
                        dst = qst if v % 2 else kr if name == "n0" else kst
                        dve.wait_ge(*at(f"{name}_xh", v + 1))
                        dve.scalar_tensor_tensor(dst[:, g, HALF * i:HALF * i + HALF], pT[:, 4 + v % 4, :],
                                                 neglo[:, 1 - v % 2:2 - v % 2], pT[:, v % 4, :],
                                                 ALU.mult, ALU.add).then_inc(S(f"{name}_st"), 1)

            dve.wait_ge(*at("first_in", 16))
            dve.wait_ge(*at("neglo_ready", 1))
            stack_queries("n0")

            def evac_values(ready, done, banks, dst, bias=None):
                for i in range(2):
                    dve.wait_ge(*at(ready, i + 1))
                    d = dst(i)
                    w = d.shape[1] * d.shape[2] * d.shape[3]
                    src = ps[:, banks[i], 0:w].rearrange("p (t h d) -> p t h d", t=4, h=d.shape[2])
                    if bias is None:
                        ins = dve.tensor_copy(d, src)
                    else:
                        ins = dve.tensor_tensor(d, src, bias.rearrange("p (h d) -> p h d", d=HD8).unsqueeze(1)
                                                .broadcast_to(list(d.shape)), ALU.add)
                    ins.then_inc(S(done), 1)

            dve.wait_ge(*at("row_in", 16))
            def vaug_heads(i):
                v = vaug[:, 4 * i:4 * i + 4, 0:NH8 * (HD8 + 1)]
                return v.rearrange("p t (h d) -> p t h d", h=NH8)[:, :, :, 0:HD8]

            dve.wait_ge(*at("ones_cols", 1))
            evac_values("n0_v_ps", "n0_v", (0, 1), vaug_heads, row("L0_conv_v_b"))
            bias_tables(1)

            def evac_pT(name, m, w):
                dve.wait_ge(*at(f"{name}_pt", m + 1))
                if m >= 8:
                    dve.wait_ge(*at(f"{name}_pv", (m - 8) // 4 + 1))
                dve.tensor_copy(pT[:, m % 8, 0:w], ps[:, 4 + m % 2, 0:w]).then_inc(S(f"{name}_ptd"), 1)

            def normalise(name, t, bank, nh, hd, step=None):
                step = step or hd + 1
                o = ps[:, bank, 0:nh * step].rearrange("p (h d) -> p h d", h=nh)
                if t >= 2:
                    dve.wait_ge(*at(f"{name}_ot", t - 1))
                link(dve.reciprocal(rs[:, t % 2, 0:nh], o[:, :, hd]))
                dve.tensor_tensor(oK[:, t % 2, 0:nh * hd].rearrange("p (h d) -> p h d", h=nh), o[:, :, 0:hd],
                                  rs[:, t % 2, 0:nh].unsqueeze(2).broadcast_to([P, nh, hd]),
                                  ALU.mult).then_inc(S(f"{name}_o"), 1)

            dve.wait_ge(*at("tab_ready", 6))
            for s in range(HEADS + N0_V + 17):
                t, r = divmod(s - N0_V - O_ADD, NH8)
                if r == 0 and 0 <= t < T:
                    dve.wait_ge(*at("n0_proj", t + 1))
                    v = xT[:, P * t:P * t + P]
                    dve.scalar_tensor_tensor(v, ps[:, 6 + t % 2, 0:P], col("L0_conv_proj_b"), v,
                                             ALU.add, ALU.add).then_inc(S("n0_add"), 1)
                t, r = divmod(s - N0_V - O_NORM, NH8)
                if r == 0 and 0 <= t < T:
                    dve.wait_ge(*at("n0_vt", t + 1))
                    normalise("n0", t, 6 + t % 2, NH8, HD8, 32)
                if s < HEADS:
                    t, h = divmod(s, NH8)
                    w = n0_w(s)
                    tab = tab_t if t == 0 else tab_b if t == T - 1 else tab_i
                    dve.wait_ge(*at("n0_s", s + 1))
                    if t >= 3 and h == 0:
                        dve.wait_ge(*at("n0_pt", NH8 * (t - 2)))
                    if t >= 2 and h == 0:
                        dve.wait_ge(*at("n0_nmx", t - 1))
                    dve.tensor_tensor_reduce(arena_s(t)[:, h, 0:w], ps[:, s % 4, 0:w],
                                             tab[:, h, :, :].rearrange("p l j -> p (l j)"), 1.0, -FMAX,
                                             ALU.add, ALU.max, mx[:, t % 2, h:h + 1]).then_inc(S("n0_sr"), 1)
                    if h == NH8 - 1:
                        dve.wait_ge(*at("n0_sr", s + 1))
                        dve.tensor_scalar(nmx[:, t, :], mx[:, t % 2, :], -1.0, None, ALU.mult).then_inc(S("n0_nmx"), 1)
                m = s - N0_T
                if 0 <= m < HEADS and not by_act(m, N0_ACT):
                    evac_pT("n0", m, n0_w(m))
            dve.wait_ge(*at("n0_add", T))

            group_norm(1, 2, "g1_norm")
            for i in range(2):
                dve.wait_ge(*at("l1_kp_ps", i + 1))
                dve.tensor_scalar(halves(bT)[i], ps[:, 2 + i, :], col("L1_conv_bk_proj"), None, ALU.add).then_inc(S("l1_kp"), 1)
            dve.wait_ge(*at("l1_qp", 2))
            dve.wait_ge(*at("l1_kp", 2))
            for i, src in enumerate((aT, bT)):
                dve.tensor_reduce(loc[:, i, :], src[:, :].rearrange("p (t n) -> p t n", t=T), AX.X,
                                  ALU.add).then_inc(S("loc_sum"), 1)
            dve.wait_ge(*at("loc_sum", 2))
            dve.tensor_scalar(loc[:, :, :], loc[:, :, :], 1.0 / P, None, ALU.mult).then_inc(S("loc_ready"), 1)
            stack_queries("n1")
            evac_values("l1_v_ps", "l1_v", (0, 1), vaug_heads, row("L1_conv_bv_a"))
            dve.wait_ge(*at("sloc_ps", 1))
            link(dve.tensor_copy(sloc[:, :], ps[0:T, 6, 0:T]))
            link(dve.max(top8[:, :], sloc[:, :]))
            dve.max_index(topi[:, :], top8[:, :], sloc[:, :]).then_inc(S("topi_ready"), 1)
            dve.wait_ge(*at("topi_ready", 1))
            for ready, done, bank, dst, bias in (("x1t_ps", "x1_tok", 0, aK, "L1_conv_ln2_b"),
                                                 ("n1t_ps", "n1_tok", 2, bK, "L1_conv_bo_a"),
                                                 ("gt_ps", "g_tok", 6, cK, "L1_conv_ln1_b")):
                for i in range(2):
                    dve.wait_ge(*at(ready, i + 1))
                    dve.tensor_tensor(dst[:, 4 * i:4 * i + 4, :], ps[:, bank + i, :].rearrange("p (t c) -> p t c", t=4),
                                      row(bias).unsqueeze(1).broadcast_to([P, 4, P]), ALU.add).then_inc(S(done), 1)

            def gather_keys(t, j):
                if t >= 2:
                    dve.wait_ge(*at("n1_s", NH8 * (t - 1)))
                r = dve.value_load(topi[t:t + 1, j:j + 1], min_val=0, max_val=T - 1)
                dve.tensor_copy(kfil[:, t % 2, :, P * j:P * j + P],
                                kst[:, :, bass.ds(r * P, P)]).then_inc(S("k_gathered"), 1)

            for j in range(KV):
                gather_keys(0, j)
            for s in range(HEADS + N1_V + 17):
                t, r = divmod(s + NH8 - 2, NH8)
                if r < KV and 0 < t < T:
                    gather_keys(t, r)
                t, r = divmod(s - N1_V - O_ADD, NH8)
                if r == 0 and 0 <= t < T:
                    dve.wait_ge(*at("n1_proj", t + 1))
                    dve.tensor_tensor(bK[:, t, :], ps[:, 6 + t % 2, 0:P], bK[:, t, :], ALU.add).then_inc(S("n1_add"), 1)
                t, r = divmod(s - N1_V - O_NORM, NH8)
                if r == 0 and 0 <= t < T:
                    dve.wait_ge(*at("n1_vt", t + 1))
                    normalise("n1", t, 6 + t % 2, NH8, HD8, 32)
                if s < HEADS and s % 2 == 1:
                    dve.wait_ge(*at("n1_s", s + 1))
                    k = s // 2
                    if k >= 16:
                        dve.wait_ge(*at("n1_p", 2 * (k - 15)))
                    b = (s - 1) % 4
                    dve.tensor_reduce(nmx[:, k % 16, 0:2], ps[:, b:b + 2, :], AX.X, ALU.max,
                                      negate=True).then_inc(S("n1_nmx"), 1)
                m = s - N1_T
                if 0 <= m < HEADS and not by_act(m, N1_ACT):
                    evac_pT("n1", m, HALF)
            dve.wait_ge(*at("n1_add", T))

            def gained_norm(src, row_name, plus, dst, norm):
                token_stats(src, norm)
                for t in range(T):
                    dve.scalar_tensor_tensor(src[:, t, :], src[:, t, :], mv[:, t, 0:1], row(row_name),
                                             ALU.subtract, ALU.mult).then_inc(S(norm + "_gain"), 1)
                root_of_variance()
                for t in range(T):
                    dve.wait_ge(*at(norm + "_gain", t + 1))
                    dve.scalar_tensor_tensor(dst[:, t, :], src[:, t, :], rstd[:, t:t + 1], plus[:, t, :],
                                             ALU.mult, ALU.add).then_inc(S(norm), 1)

            gained_norm(bK, "L1_conv_ln1_g", cK, cK, "ln1_norm")
            dve.wait_ge(*at("ln1_norm", T))
            gained_norm(cK, "L1_conv_ln2_g", aK, aK, "ln2_norm")
            dve.wait_ge(*at("ln2_norm", T))

            layer_norm(aK, bK, "na_norm")
            for i in range(2):
                dve.wait_ge(*at("n2_q_ps", i + 1))
                dve.tensor_scalar(halves(aT)[i], ps[:, 2 + i, :], HD4 ** -0.5, None, ALU.mult).then_inc(S("n2_q"), 1)
            dve.wait_ge(*at("ones_cols", 3))
            evac_values("n2_v_ps", "n2_v", (6, 7), lambda i: vaug4[:, 4 * i:4 * i + 4, :, 0:HD4])
            dve.wait_ge(*at("xb2_ready", 2))
            for s in range(T + 5):
                if s < T:
                    dve.wait_ge(*at("n2_s", NH4 * (s + 1)))
                    if s >= 4:
                        dve.wait_ge(*at("n2_pt", s - 3))
                    v = pS[:, s % 4, :].rearrange("p (h k) -> p h k", h=NH4)
                    dve.tensor_tensor(v, ps[:, s % 2, :].rearrange("p (h k) -> p h k", h=NH4),
                                      band[:, :].unsqueeze(1).broadcast_to([P, NH4, P]), ALU.add).then_inc(S("n2_sr"), 1)
                    dve.wait_ge(*at("n2_sr", s + 1))
                    dve.tensor_reduce(nmx[:, s, 0:NH4], v, AX.X, ALU.max, negate=True).then_inc(S("n2_nmx"), 1)
                t = s - 1
                if 0 <= t < T:
                    dve.wait_ge(*at("n2_pt", t + 1))
                    if t >= 4:
                        dve.wait_ge(*at("n2_pv", t - 3))
                    dve.tensor_copy(pT[:, t % 4, :], ps[:, 2 + t % 2, :]).then_inc(S("n2_ptd"), 1)
                t = s - 2
                if 0 <= t < T:
                    dve.wait_ge(*at("n2_pv", t + 1))
                    normalise("n2", t, 4 + t % 2, NH4, HD4)
                t = s - 4
                if 0 <= t < T:
                    dve.wait_ge(*at("n2_proj", t + 1))
                    dve.tensor_tensor(aK[:, t, :], ps[:, 7, 0:P], aK[:, t, :], ALU.add).then_inc(S("n2_add"), 1)
            dve.wait_ge(*at("n2_add", T))

            def over_experts(v):
                return v.unsqueeze(2).broadcast_to([P, T, E])

            def rank_experts(pre, k, bank):
                dve.wait_ge(*at(f"{pre}_lg_ps", 1))
                link(dve.tensor_tensor(lg[:, :, :], ps[:, bank, 0:T * E].rearrange("p (t e) -> p t e", e=E),
                                       rrow[:, k, :].unsqueeze(1).broadcast_to([P, T, E]), ALU.add))
                link(dve.tensor_reduce(lm[:, :], lg[:, :, :], AX.X, ALU.max))
                dve.tensor_tensor(lg[:, :, :], lg[:, :, :], over_experts(lm[:, :]), ALU.subtract).then_inc(S(f"{pre}_lg"), 1)
                dve.wait_ge(*at(f"{pre}_lg", 1))
                for t in range(T):
                    li = lg[:, t, :].unsqueeze(2).broadcast_to([P, E, E])
                    lj = lg[:, t, :].unsqueeze(1).broadcast_to([P, E, E])
                    dve.tensor_tensor(cmp_[:, t, :, :], lj, li, ALU.is_gt).then_inc(S(f"{pre}_cmp"), 1)
                    dve.tensor_tensor(cm2[:, t, :, :], lj, li, ALU.is_equal).then_inc(S(f"{pre}_cmp"), 1)
                dve.wait_ge(*at(f"{pre}_cmp", 2 * T))
                link(dve.tensor_tensor(cm2[:, :, :, :], cm2[:, :, :, :],
                                       tril8[:, :, :].unsqueeze(1).broadcast_to([P, T, E, E]), ALU.mult))
                link(dve.tensor_tensor(cmp_[:, :, :, :], cmp_[:, :, :, :], cm2[:, :, :, :], ALU.add))
                link(dve.tensor_reduce(rank[:, :, :], cmp_[:, :, :, :], AX.X, ALU.add))

            def accumulate(pre, acc):
                for e in range(E):
                    for t in range(T):
                        if t % 4 == 0:
                            dve.wait_ge(*at(f"{pre}_fc2", 2 * e + t // 4 + 1))
                        if e:
                            dve.wait_ge(*at(f"{pre}_acc", T * (e - 1) + t + 1))
                        dve.scalar_tensor_tensor(acc[:, t, :], ps[:, 4 + 2 * (e % 2) + t // 4, P * (t % 4):P * (t % 4) + P],
                                                 cw[:, t, e:e + 1], acc[:, t, :],
                                                 ALU.mult, ALU.add).then_inc(S(f"{pre}_acc"), 1)

            layer_norm(aK, bK, "nb_norm")
            dve.wait_ge(*at("nb_norm", T))
            layer_norm(bK, cK, "nn_norm")
            rank_experts("m2", 0, 4)
            dve.wait_ge(*at("m2_ex", 1))
            link(dve.scalar_tensor_tensor(ex[:, :, :], rank[:, :, :], 2.0, ex[:, :, :], ALU.is_lt, ALU.mult))
            link(dve.tensor_reduce(sm[:, :], ex[:, :, :], AX.X, ALU.add))
            link(dve.reciprocal(rsm[:, :], sm[:, :]))
            dve.tensor_tensor(cw[:, :, :], ex[:, :, :], over_experts(rsm[:, :]), ALU.mult).then_inc(S("m2_cw"), 1)
            for i in range(2):
                dve.wait_ge(*at("m2_b2_ps", i + 1))
                v = aK[:, 4 * i:4 * i + 4, :]
                dve.tensor_tensor(v, ps[:, 6 + i, :].rearrange("p (t c) -> p t c", t=4), v, ALU.add).then_inc(S("m2_b2"), 1)
            dve.wait_ge(*at("m2_b2", 2))
            accumulate("m2", aK)
            dve.wait_ge(*at("m2_acc", T * E))

            layer_norm(aK, bK, "nc_norm")
            for i in range(2):
                dve.wait_ge(*at("n3_q_ps", i + 1))
                dve.tensor_scalar(aT[0:U, HALF * i:HALF * i + HALF], ps[0:U, 2 + i, :], U ** -0.5, None,
                                  ALU.mult).then_inc(S("n3_q"), 1)
            evac_values("n3_v_ps", "n3_v", (6, 7), lambda i: vaug1[:, 4 * i:4 * i + 4, 0:U].unsqueeze(2))
            dve.wait_ge(*at("xb3_ready", 2))
            for s in range(T + 3):
                if s < T:
                    dve.wait_ge(*at("n3_s", s + 1))
                    dve.tensor_reduce(nmx[:, s, 0:1], ps[:, 2 * (s % 2):2 * (s % 2) + 2, :], AX.XY, ALU.max,
                                      negate=True).then_inc(S("n3_nmx"), 1)
                t = s - 2
                if 0 <= t < T:
                    dve.wait_ge(*at("n3_pv", t + 1))
                    normalise("n3", t, 6 + t % 2, 1, U)
                t = s - 1
                if 0 <= t < T:
                    dve.wait_ge(*at("n3_pt", 2 * t + 1))
                    if t >= 2:
                        dve.wait_ge(*at("n3_pv", t - 1))
                    dve.tensor_copy(pT[:, 2 * (t % 2), :], ps[:, 4, :]).then_inc(S("n3_ptd"), 1)
                t = s - 3
                if 0 <= t < T:
                    dve.wait_ge(*at("n3_proj", t + 1))
                    dve.tensor_tensor(aK[:, t, :], ps[:, 6 + t % 2, 0:P], aK[:, t, :], ALU.add).then_inc(S("n3_add"), 1)
            dve.wait_ge(*at("n3_add", T))

            layer_norm(aK, bK, "nd_norm")
            rank_experts("m3", 1, 2)
            dve.tensor_scalar(rank[:, :, :], rank[:, :, :], 1.0, None, ALU.is_lt).then_inc(S("m3_hot"), 1)
            dve.wait_ge(*at("m3_hot", 1))
            dve.wait_ge(*at("m3_ex", 1))
            link(dve.tensor_reduce(sm[:, :], ex[:, :, :], AX.X, ALU.add))
            link(dve.reciprocal(rsm[:, :], sm[:, :]))
            dve.wait_ge(*at("m3_pos", 1))
            dve.wait_ge(*at("places_ready", 4))
            pos = ps[:, 3, 0:T * E].rearrange("p (t e) -> p t e", e=E)
            link(dve.scalar_tensor_tensor(cw[:, :, :], pos, float(CAP) + 0.5, rank[:, :, :], ALU.is_lt, ALU.mult))
            link(dve.tensor_tensor(ex[:, :, :], pos, placeoff.unsqueeze(1).broadcast_to([P, T, E]), ALU.add))
            link(dve.tensor_tensor(ex[:, :, :], ex[:, :, :], cw[:, :, :], ALU.mult))
            link(dve.tensor_reduce(slot[:, :], ex[:, :, :], AX.X, ALU.add))
            dve.tensor_scalar(slot[:, :], slot[:, :], -1.0, None, ALU.add).then_inc(S("m3_slot"), 1)
            dve.wait_ge(*at("m3_slot", 1))
            for t in range(T):
                if t >= 2:
                    dve.wait_ge(*at("m3_gathered", t - 1))
                dve.tensor_scalar(hot(t), places, slot[:, t:t + 1], None, ALU.is_equal).then_inc(S("m3_hot_ready"), 1)
            dve.wait_ge(*at("m3_gathered", T))
            dve.tensor_copy(xg[:, HALF:2 * HALF], ps[:, 1, :]).then_inc(S("m3_xg_dve"), 1)
            dve.wait_ge(*at("slotrow", 1))

            def hot_turned(n):
                i, k = COMBINE[n]
                if n >= 6:
                    dve.wait_ge(*at("m3_combined", n - 5))
                dve.tensor_scalar(hotT(n), halves(slotrow)[i], placecol[:, k:k + 1], None,
                                  ALU.is_equal).then_inc(S("m3_hotT"), 1)

            def turned_low(g):
                dve.wait_ge(*at("m3_high", g + 1))
                k0, k1 = TURNS[g]
                dve.tensor_tensor(ypart[:, 1, k0:k1, :], ps[:, 1 + g % 2, 0:P * (k1 - k0)].rearrange("p (k c) -> p k c", c=P),
                                  ypart[:, 0, k0:k1, :].bitcast(F32), ALU.subtract).then_inc(S("m3_low"), 1)

            made = 0
            for e in range(E):
                if made < 6:
                    hot_turned(made)
                    made += 1
                dve.wait_ge(*at("m3_fc2", e + 1))
                dve.tensor_scalar(yT[:, CAP * e:CAP * e + CAP], ps[:, 0 if e % 2 else 7, 0:CAP], col("L3_ffn_b2", e), 0.5,
                                  ALU.add, ALU.mult).then_inc(S("m3_y"), 1)
                if e % 4 == 3:
                    v = yT[:, CAP * (e - 3):CAP * (e + 1)].rearrange("p (k c) -> p k c", c=P)
                    m = nanm[:, 0:SC // 2, :]
                    dve.wait_ge(*at("m3_y", e + 1))
                    link(dve.tensor_tensor(m, v, v, ALU.not_equal))
                    link(dve.copy_predicated(v, m, fills[:, 0:1, :].broadcast_to([P, SC // 2, P])))
                    dve.tensor_scalar(v, v, BIG, -BIG, ALU.min, ALU.max).then_inc(S("m3_clean"), 1)
                if e == E - 2:
                    turned_low(0)
                    turned_low(1)
            for n in range(made, 12):
                hot_turned(n)
            turned_low(2)
            turned_low(3)
            for n in range(12, 2 * SC):
                hot_turned(n)
            for i in range(2):
                dve.wait_ge(*at("m3_out_ps", i + 1))
                y, m, r = (v[:, 4 * i:4 * i + 4, :] for v in (cK, nanm, aK))

                def fill(k):
                    return fills[:, k:k + 1, :].broadcast_to([P, 4, P])
                link(dve.scalar_tensor_tensor(y, ps[:, 5 + i, :].rearrange("p (t c) -> p t c", c=P), 2.0,
                                              rsm[:, 4 * i:4 * i + 4].unsqueeze(2).broadcast_to([P, 4, P]),
                                              ALU.mult, ALU.mult))
                link(dve.tensor_tensor(m, y, y, ALU.not_equal))
                link(dve.copy_predicated(y, m, fill(0)))
                link(dve.tensor_scalar(m, y, FMAX, None, ALU.is_gt))
                link(dve.copy_predicated(y, m, fill(1)))
                link(dve.tensor_scalar(m, y, -FMAX, None, ALU.is_lt))
                link(dve.copy_predicated(y, m, fill(2)))
                dve.tensor_tensor(r, r, y, ALU.add).then_inc(S("y_ready"), 1)


def kernel(**inputs):
    import numpy as _np
    import concourse.bacc as _bacc
    from concourse.bass_utils import run_bass_kernel_spmd as _run

    a = {name: _np.asarray(v) for name, v in inputs.items()}

    def experts_first(w):
        return w.transpose(1, 0, 2)

    def experts_second(w):
        return w.reshape(E, FC, P, P).transpose(2, 0, 1, 3)

    def stacked(b):
        return _np.tile(b.reshape(4, 32), (1, 4)).reshape(4 * P)

    a["n0_q_b"], a["n0_k_b"] = stacked(a["L0_conv_qkv_b"][:P]), stacked(a["L0_conv_qkv_b"][P:2 * P])
    a["n1_q_b"], a["n1_k_b"] = stacked(a["L1_conv_bq_a"]), stacked(a["L1_conv_bk_a"])
    qkv = a["L0_conv_qkv_w"].reshape(3, P, P)
    laid = {
        "xT": a["x"].reshape(N, P).T,
        "first": _np.concatenate([qkv[0].T, qkv[1].T, qkv[2].T, a["L0_conv_proj_w"].T]
                                 + [a[name].reshape(-1, P).T for name in VEC], axis=1),
        "rpbT": _np.pad(a["L0_conv_rpb"].transpose(2, 0, 1), ((0, 0), (0, 0), (1, 1))),
        "rows": _np.concatenate([a["L0_conv_qkv_b"][2 * P:]] + [a[name] for name in ROWVEC[1:]]
                                + [a["L2_ffn_br"], a["L3_ffn_gate_b"]]),
        "w1": _np.stack([a["L1_conv_" + name] for name in
                         ("wq_proj", "wk_proj", "wv_proj", "wq_a", "wk_a", "wv_a", "wo_a")], axis=1),
        "convw": a["L1_conv_conv_w"].reshape(25, P, P).transpose(1, 0, 2),
        "late": _np.concatenate([a["L2_attn_Wqkv"], a["L2_attn_Wproj"], a["L3_attn_W_q"], a["L3_attn_W_k"],
                                 a["L3_attn_W_v"], a["L2_ffn_Wr"], a["L3_ffn_gate_w"]], axis=1),
        "w3o": a["L3_attn_W_o"],
        "fb2": a["L2_ffn_b2"],
        "m2_w1": experts_first(a["L2_ffn_W1"]), "m2_w2": experts_second(a["L2_ffn_W2"]),
        "m3_w1": experts_first(a["L3_ffn_w1"]), "m3_w2": experts_second(a["L3_ffn_w2"]),
    }
    nc = _bacc.Bacc("TRN2", target_bir_lowering=False, num_devices=1)
    arrays, args = {}, {}
    for name, v in laid.items():
        v = _np.ascontiguousarray(v)
        arrays[f"in_{name}_dram"] = v
        args[name] = nc.dram_tensor(f"in_{name}_dram", v.shape, mybir.dt.from_np(v.dtype), kind="ExternalInput").ap()
    out = nc.dram_tensor("out_0_dram", (1, IMG, IMG, P), F32, kind="ExternalOutput").ap()
    build(nc, args, out)
    r = _run(nc, [arrays], core_ids=[0])
    return r.results[0]["out_0_dram"]
```

```python
from contextlib import ExitStack

import concourse.bass as bass
from concourse import mybir

P = 128
IMG = 32
T = IMG * IMG // P
N = T * P
HALF = 512

F32 = mybir.dt.float32
F32R = mybir.dt.float32r
U32 = mybir.dt.uint32
U8 = mybir.dt.uint8
ALU = mybir.AluOpType
ACT = mybir.ActivationFunctionType
AX = mybir.AxisListType

NEG = -1.0e30
FMAX = 3.4028234e38

NH8, HD8 = 8, 16
NH4, HD4 = 4, 32
KW = 7
REL = 2 * KW - 1
ROWS = P // IMG
LR = 3 * ROWS
KV = 4
HEADS = T * NH8
N0_EXP, N0_T, N0_V = 5, 8, 10
N1_EXP, N1_T, N1_V = 2, 5, 7
O_COPY, O_TURN, O_NORM, O_BACK, O_TURNED, O_PROJECT, O_ADD = 8, 9, 10, 11, 12, 13, 14
N0_S, N1_S = 4, 3
CONV_START, CONV_COPY, CONV_TURN, CONV_ADD = (0, 33), (26, 59), (28, 61), (29, 62)
N0_ACT, N1_ACT = 2, 2
RADIUS = 32
U = 64
E = 8
FH = 512
FC = FH // P
CAP = -(-5 * N // (4 * E))
SLOTS = E * CAP
SC = SLOTS // P
BIG = 3.0e38
TURNS = ((0, 3), (3, 5), (5, 8), (8, 10))
COMBINE = [(i, k) for part in range(2) for i in range(2) for k in range(SC // 2 * part, SC // 2 * (part + 1))]


def by_act(m, every):
    return (m % every == every - 1) if every > 0 else (m % -every != -every - 1)


def act_copies(n, every):
    return n // every if every > 0 else n - n // -every


VEC = {}
for _name, _cols in (("n0_q_b", 4), ("n0_k_b", 4), ("n1_q_b", 4), ("n1_k_b", 4), ("L0_conv_proj_b", 1),
                     ("L1_conv_bq_proj", 1), ("L1_conv_bk_proj", 1), ("L1_conv_bv_proj", 1),
                     ("L1_conv_conv_b", 1), ("L2_ffn_ln_g", E), ("L2_ffn_ln_b", E), ("L2_ffn_b1", E * FC),
                     ("L3_ffn_b1", E * FC), ("L3_ffn_b2", E)):
    VEC[_name] = (sum(c for _, c in VEC.values()), _cols)
NVEC = sum(c for _, c in VEC.values())

ROWVEC = ["L0_conv_v_b", "L1_conv_bv_a", "L1_conv_bo_a", "L1_conv_ln1_g", "L1_conv_ln1_b", "L1_conv_ln2_g",
          "L1_conv_ln2_b", "L2_attn_bproj", "L3_attn_b_o"]
NROW = len(ROWVEC) * P + 2 * E

PASSES = ((0, 0), (0, 1), (1, 0))

NORMS = ["ln1", "ln2", "na", "nb", "nn", "nc", "nd"]

KINDS = {
    "turned_ps": [("x1t_ps", 2), ("n1t_ps", 2), ("gt_ps", 2), ("nb_tps", 2),
                  ("nn_tps", 2), ("nd_tps", 2)],
    "product_ps": [("l1_qp_ps", 2), ("l1_kp_ps", 2),
                   ("l1_vp_ps", 2), ("conv_ps", 2)],
    "values_ps": [("n0_v_ps", 2), ("l1_v_ps", 2)],
    "act_copied": [ ("l1_qp", 2),
                   ("l1_vp", 2), ("gT_ready", 2),
                   ("nb_T", 2), ("m2_xT", 2), ("nd_T", 2)],
    "dve_made": [("n0_v", 2), ("l1_kp", 2), ("loc_sum", 2), ("loc_ready", 1),
                 ("topi_ready", 1), ("l1_v", 2), ("x1_tok", 2), ("n1_tok", 2), ("g_tok", 2)],
    "normalised": [("g0_norm", 2), ("g1_norm", 2)],
    "pool_made": [("kvpad_zero", 1), ("kvpad_ready", 2), ("xb2_ready", 2),
                  ("xb3_ready", 2)],
    "stack_ps": [("n0_st_ps", 16), ("n1_st_ps", 16)],
    "stack_parts": [("n0_x", 16), ("n1_x", 16)],
    "stack_rounded": [("n0_xh", 16), ("n1_xh", 16)],
    "stacked": [("n0_st", 16), ("n1_st", 16)],
    "values_turned_ps": [("n0_vt", T), ("n1_vt", T)],
    "values_copied": [("n0_vc", T), ("n1_vc", T)],
    "queries_split": [("n0_qm", T), ("n1_qm", T), ("n2_qm", T)],
    "scores_ps": [("n0_s", HEADS), ("n1_s", HEADS), ("n2_s", T * NH4), ("n3_s", T)],
    "scores_read": [("n0_sr", HEADS), ("n2_sr", T)],
    "row_maxima": [("n0_nmx", 2 * T), ("n1_nmx", HEADS), ("n2_nmx", T), ("n3_nmx", T)],
    "probabilities": [("n0_p", HEADS), ("n1_p", HEADS), ("n2_p", T * NH4), ("n3_p", T)],
    "turned_p_ps": [("n0_pt", HEADS), ("n1_pt", HEADS), ("n2_pt", T), ("n3_pt", 2 * T)],
    "turned_p_act": [("n0_pta", act_copies(HEADS, N0_ACT)), ("n1_pta", act_copies(HEADS, N1_ACT)), ("n2_pta", T), ("n3_pta", T)],
    "turned_p_dve": [("n0_ptd", HEADS - act_copies(HEADS, N0_ACT)), ("n1_ptd", HEADS - act_copies(HEADS, N1_ACT)), ("n3_ptd", T)],
    "with_values_ps": [("n0_pv", HEADS // 4), ("n1_pv", HEADS // 4), ("n2_pv", T), ("n3_pv", T)],
    "output": [("n0_o", T), ("n1_o", T), ("n2_o", T), ("n3_o", T)],
    "turned_output_ps": [("n0_ot", T), ("n1_ot", T), ("n2_ot", T), ("n3_ot", T)],
    "turned_output": [("n0_oT", T), ("n1_oT", T), ("n2_oT", T), ("n3_oT", T)],
    "projected_ps": [("n0_proj", T), ("n1_proj", T), ("n2_proj", T), ("n3_proj", T)],
    "residual_added": [("n0_add", T), ("n1_add", T), ("n2_add", T), ("n3_add", T)],
}
for _kind, _count in (("lg_ps", 2), ("lg", 1), ("ex", 1)):
    KINDS["expert_" + _kind] = [(f"m2_{_kind}", _count), (f"m3_{_kind}", _count)]
for _group in (("ln1", "nb", "nc", "nd"), ("ln2", "nn")):
    for _suffix, _count in (("norm", T), ("norm_st", T), ("norm_mv", T), ("var", 2), ("root", 2)):
        KINDS[f"{_group[0]}_{_suffix}_and_later"] = [(f"{x}_{_suffix}", _count) for x in _group]
for _suffix in ("q_ps", "k_ps", "v_ps", "q", "k", "v"):
    KINDS["attention_" + _suffix] = [(f"{x}_{_suffix}", 2) for x in ("n2", "n3")]
KINDS["attention_tps"] = [("na_tps", 2), ("nc_tps", 2)]
KINDS["attention_T"] = [("na_T", 2), ("nc_T", 2)]
PLACE = {name: (kind, sum(c for _, c in names[:i])) for kind, names in KINDS.items() for i, (name, _) in enumerate(names)}


class Chain:

    def __init__(self, eng, sem):
        self.eng, self.sem, self.n = eng, sem, 0

    def __call__(self, ins):
        self.n += 1
        ins.then_inc(self.sem, 1)
        self.eng.wait_ge(self.sem, self.n)


def build(nc, A, out):
    with ExitStack() as ctx:
        def over(name, shape):
            with nc.sbuf_tensor(name, shape, F32R) as tensor:
                return tensor

        def sb(name, shape, dt=F32):
            return ctx.enter_context(nc.sbuf_tensor(name, shape, dt))

        sems = {}

        def S(name):
            name = PLACE.get(name, (name, 0))[0]
            if name not in sems:
                sems[name] = ctx.enter_context(nc.semaphore(name))
            return sems[name]

        def at(name, k):
            return S(name), PLACE.get(name, (name, 0))[1] + k

        ps = ctx.enter_context(nc.psum_tensor("ps", [P, 8, HALF], F32))

        ident = sb("ident", [P, P])
        ones = sb("ones", [P, P])
        upper = sb("upper", [P, P])
        band = sb("band", [P, P])
        gavg = sb("gavg", [P, P])
        mask2 = sb("mask2", [P, 2])
        neglo = sb("neglo", [P, 2])
        mask4 = sb("mask4", [P, NH4])
        tril8 = sb("tril8", [P, E, E])
        qbias = sb("qbias", [P, 2, 4])
        nhalf = sb("nhalf", [P, 8])
        first = sb("first", [P, 4 * P + NVEC])
        w0 = first[:, 0:4 * P].rearrange("p (a c) -> p a c", a=4)
        vcols = first[:, 4 * P:4 * P + NVEC]
        rows = sb("rows", [P, NROW])
        rrow = rows[:, len(ROWVEC) * P:NROW].rearrange("p (a e) -> p a e", a=2)
        w1 = sb("w1", [P, 7, P])
        convw_low = over("convw_low", [P, 25, P])
        convw = sb("convw", [P, 25, P])
        late = sb("late", [P, 4 * P + 3 * U + 2 * E])
        w2a = late[:, 0:3 * P]
        w2p = late[:, 3 * P:4 * P]
        w3q = late[:, 4 * P:4 * P + 3 * U].rearrange("p (a u) -> p a u", a=3)
        rout = late[:, 4 * P + 3 * U:].rearrange("p (a e) -> p a e", a=2)
        w3o = sb("w3o", [U, P])
        fw1 = sb("fw1", [P, E, FH])
        convw_high = over("convw_high", [P, 25, P])
        fw2 = sb("fw2", [P, E, FC, P])
        fb2 = sb("fb2", [E, P])
        onesr = sb("onesr", [P, P], F32R)
        rpbT = sb("rpbT", [33, NH8, REL + 2])
        cT = sb("cT", [P, N])
        shift = cT[0:33, :].rearrange("p (a b) -> p a b", a=IMG)
        rmask = sb("rmask", [P, 3, LR])
        arena = sb("arena", [P, 9216])
        tabs_parts = over("tabs_parts", [P, 7168])
        tabs = sb("tabs", [P, 7168])
        tab_i = tabs[:, 0:3072].rearrange("p (h l j) -> p h l j", h=NH8, l=LR)
        tab_t = tabs[:, 3072:5120].rearrange("p (h l j) -> p h l j", h=NH8, l=8)
        tab_b = tabs[:, 5120:7168].rearrange("p (h l j) -> p h l j", h=NH8, l=8)

        cmp_ = tabs[:, 0:HALF].rearrange("p (t i j) -> p t i j", t=T, i=E)
        cm2 = tabs[:, HALF:N].rearrange("p (t i j) -> p t i j", t=T, i=E)
        eT = tabs[:, 4 * N:5 * N]
        bK = tabs[:, 2 * N:3 * N].rearrange("p (t c) -> p t c", t=T)
        cK = tabs[:, 3 * N:4 * N].rearrange("p (t c) -> p t c", t=T)
        cwT = tabs[0:E, 4 * N:5 * N]
        kvpad = tabs[:, 5 * N:5 * N + (IMG + 4) ** 2].rearrange("p (r w) -> p r w", r=IMG + 4)

        xT = sb("xT", [P, N])
        nT = sb("nT", [P, N])
        KVP = (IMG + 4) ** 2
        kv_high = over("kv_high", [P, KVP])
        aT = sb("aT", [P, N])
        bT = sb("bT", [P, N])
        kv_low = tabs_parts[:, 5 * N:5 * N + KVP]
        kv_parts = [v.rearrange("p (r w) -> p r w", r=IMG + 4) for v in (kv_high[:, :], kv_low)]
        convw_parts = (convw_high, convw_low)
        oT = sb("oT", [P, N])
        aK = sb("aK", [P, T, P])
        VW = NH8 * (HD8 + 1) + 15
        vaug = sb("vaug", [P, T, VW])
        vfil = tabs[:, 0:2 * KV * VW].rearrange("p (b r c) -> p b r c", b=2, r=KV)
        vaug4 = arena[:, 8 * HALF:8 * HALF + T * NH4 * (HD4 + 1)].rearrange("p (t h d) -> p t h d", t=T, h=NH4)
        vaug1 = tabs[:, 7168 - T * (U + 1):7168].rearrange("p (t d) -> p t d", t=T)
        qst = fw1[:, :, :].rearrange("p e h -> p (e h)").rearrange("p (g n) -> p g n", g=4)
        kr = sb("kr", [P, 4, N], F32R)
        kfil = kr[:, :, :].rearrange("p a n -> p (a n)").rearrange("p (b g n) -> p b g n", b=2, g=4)
        kst = arena[:, 8 * HALF:8 * HALF + 4 * N].rearrange("p (g n) -> p g n", g=4)
        qr = sb("qr", [P, 2, NH8, P], F32R)
        qm = arena[:, 7168:7168 + 2 * NH4 * P].rearrange("p (b h n) -> p b h n", b=2, h=NH4)
        vsb = sb("vsb", [P, 2, P])
        pS8 = arena[:, 0:8 * HALF].rearrange("p (a k) -> p a k", a=8)
        pS = arena[:, 0:4 * HALF].rearrange("p (a k) -> p a k", a=4)
        pT = sb("pT", [P, 8, HALF])
        oK = sb("oK", [P, 2, P])
        mx = sb("mx", [P, 2, 8])
        nmx = sb("nmx", [P, 16, 8])
        rs = sb("rs", [P, 2, 8])
        st = sb("st", [P, 3, T, 6])
        mv = sb("mv", [P, 3, T, 2])
        ge = sb("ge", [P, 2])
        gm = sb("gm", [P, 2])
        gv = sb("gv", [P, 1])
        grs = sb("grs", [P, 1])
        ve = sb("ve", [P, 3, T])
        rstd = sb("rstd", [P, 3, T])
        loc = sb("loc", [P, 2, T])
        sloc = sb("sloc", [T, 8])
        top8 = sb("top8", [T, 8])
        topi = sb("topi", [T, 8], U32)
        lg = sb("lg", [P, T, E])
        lm = sb("lm", [P, T])
        ex = sb("ex", [P, T, E])
        rank = sb("rank", [P, T, E])
        cw = sb("cw", [P, T, E])
        sm = sb("sm", [P, T])
        rsm = sb("rsm", [P, T])
        kept = sb("kept", [P, T, E])
        before = sb("before", [P, T, E])
        before2 = sb("before2", [P, T, E])
        lmask = sb("lmask", [P, T], U8)
        nanm = sb("nanm", [P, T, P], U8)
        fills = sb("fills", [P, 1, P])

        xpart2 = kr[:, :, :].rearrange("p (b a) n -> p b a n", b=2)
        wpart2 = qr[:, :, :, :].rearrange("p b (a c) n -> p b a (c n)", a=2)

        cflat = convw[:, :, :].rearrange("p k c -> p (k c)")
        places = cflat[:, 0:SLOTS]
        placecol = cflat[:, SLOTS:SLOTS + SC]
        placeoff = cflat[:, SLOTS + SC:SLOTS + SC + E]
        xpart = qr
        krf = kr[:, :, :].rearrange("p a n -> p (a n)")
        slot = sm
        slotd = krf[:, 2 * SLOTS:2 * SLOTS + N].rearrange("p (t n) -> p t n", t=T)
        slotrow = bT
        xg = arena[:, 0:SLOTS]
        yT = arena[:, SLOTS:2 * SLOTS]
        ypart = krf[:, 0:2 * SLOTS].rearrange("p (a k c) -> p a k c", a=2, k=SC)
        qrf = qr[:, :, :, :].rearrange("p a h n -> p (a h n)")

        def hid3(e):
            k = 2 * SLOTS + FC * CAP * (e % 2)
            return arena[:, k:k + FC * CAP].rearrange("p (c n) -> p c n", c=FC)

        def hot(t):
            return krf[:, SLOTS * (t % 2):SLOTS * (t % 2) + SLOTS]

        def hotT(i):
            i %= 6
            return qrf[:, HALF * i:HALF * i + HALF] if i < 4 else krf[:, 2 * SLOTS + HALF * (i - 4):2 * SLOTS + HALF * (i - 3)]

        out_v = out.rearrange("a (t r) w c -> (r w) (a t) c", t=T)

        def row(name):
            k = ROWVEC.index(name) * P
            return rows[:, k:k + P]

        def col(name, i=0):
            k = VEC[name][0] + i
            return vcols[:, k:k + 1]

        def halves(t):
            return t[:, 0:HALF], t[:, HALF:N]

        def n0_lo(t):
            return max(t - 1, 0)

        def n0_hi(t):
            return min(t + 2, T)

        def n0_w(m):
            return P * (n0_hi(m // NH8) - n0_lo(m // NH8))

        def arena_s(t):
            return arena[:, 3072 * (t % 3):3072 * (t % 3) + 3072].rearrange("p (h k) -> p h k", h=NH8)

        def hid(e):
            return arena[:, 4096 * (e % 2):4096 * (e % 2) + 4096].rearrange("p (c n) -> p c n", c=FC)

        def copied(eng, name, m, every):
            if by_act(m, every):
                eng.wait_ge(*at(f"{name}_pta", act_copies(m + 1, every)))
            else:
                eng.wait_ge(*at(f"{name}_ptd", m + 1 - act_copies(m + 1, every)))

        block = ctx.enter_context(nc.Block())

        @block.sync
        def _(sp):
            sp.dma_start(xT[:, :], A["xT"]).then_inc(S("x_in"), 16)
            sp.dma_start(first[:, :], A["first"]).then_inc(S("first_in"), 16)
            sp.wait_ge(*at("rpb_zero", 1))
            sp.dma_start(rpbT[0:REL, :, :], A["rpbT"]).then_inc(S("rpb_in"), 16)
            sp.dma_start(rows[:, :], A["rows"].partition_broadcast(P)).then_inc(S("row_in"), 16)
            sp.dma_start(w1[:, :, :], A["w1"]).then_inc(S("w1_in"), 16)
            sp.dma_start(convw[:, :, :], A["convw"]).then_inc(S("conv_in"), 16)
            sp.dma_start(late[:, :], A["late"]).then_inc(S("late_in"), 16)
            sp.dma_start(w3o[:, :], A["w3o"]).then_inc(S("w3_in"), 16)
            sp.dma_start(fb2[:, :], A["fb2"]).then_inc(S("fb2_in"), 16)
            sp.wait_ge(*at("conv_ps", 2))
            sp.dma_start(fw2[:, :, :, :], A["m2_w2"]).then_inc(S("fw_in"), 16)
            sp.wait_ge(*at("n1_qm", T))
            sp.dma_start(fw1[:, :, :], A["m2_w1"]).then_inc(S("fw_in"), 16)
            for e in range(E):
                sp.wait_ge(*at("m2_w_high", e + 1))
                sp.wait_ge(*at("m2_w_low", e + 1))
                sp.dma_start(fw1[:, e, :], A["m3_w1"][:, e]).then_inc(S("fv_in"), 16)
                sp.wait_ge(*at("m2_fc2", 2 * (e + 1)))
                sp.dma_start(fw2[:, e, :, :], A["m3_w2"][:, e]).then_inc(S("fv_in"), 16)
            for i in range(2):
                sp.wait_ge(*at(f"y_ready_{i}", 1))
                sp.dma_start(out_v[:, 4 * i:4 * i + 4, :], aK[:, 4 * i:4 * i + 4, :]).then_inc(S("y_out"), 16)
            sp.wait_ge(*at("y_out", 2 * 16))

        @block.gpsimd
        def _(pool):
            link = Chain(pool, S("pool_chain"))

            def select(ap, pattern, base, mult, op=ALU.is_ge, fill=0.0):
                return pool.affine_select(out=ap, in_=ap, pattern=pattern, base=base, channel_multiplier=mult,
                                          compare_op=op, fill=fill)

            pool.memset(rpbT[:, :, :], 0.0).then_inc(S("rpb_zero"), 1)
            link(pool.memset(gavg[:, :], 0.25))
            g = gavg[:, :].rearrange("p (g i) -> p g i", i=4)
            link(select(g, [[-4, P // 4], [0, 4]], 0, 1))
            select(g, [[4, P // 4], [0, 4]], 3, -1).then_inc(S("gavg_ready"), 1)
            link(pool.memset(shift[:, :, :], 0.0))
            link(select(shift[0:REL, :, :], [[-1, IMG], [1, IMG]], -(KW - 1), 1, ALU.not_equal, 1.0))
            lo, hi = IMG - KW, KW
            link(select(shift[32:33, 0:lo, :], [[1, lo], [-1, IMG]], KW // 2, 0, ALU.is_ge, NEG))
            link(select(shift[32:33, hi:IMG, :], [[-1, IMG - hi], [1, IMG]], KW // 2 - hi, 0, ALU.is_ge, NEG))
            pool.wait_ge(*at("rpb_zero", 1))
            pool.memset(rpbT[32:33, :, :], 1.0).then_inc(S("shift_ready"), 1)
            pool.wait_ge(*at("shift_ready", 1))
            link(pool.memset(ident[:, :], 0.0))
            select(ident[:, :], [[-1, P]], 0, 1, ALU.not_equal, 1.0).then_inc(S("ident_ready"), 1)
            pool.wait_ge(*at("ident_ready", 1))
            link(pool.memset(nhalf[:, :], -0.5))
            link(pool.memset(rmask[:, :, :], NEG))
            for r in range(ROWS):
                link(pool.memset(rmask[32 * r:32 * r + 32, 0, r + 1:r + 1 + KW], 0.0))
            link(pool.memset(rmask[:, 1, ROWS:ROWS + KW], 0.0))
            pool.memset(rmask[:, 2, 1:1 + KW], 0.0).then_inc(S("rmask_ready"), 1)
            pool.wait_ge(*at("rmask_ready", 1))
            def root(name, i, src, dst, n):
                pool.wait_ge(*at(f"{name}_var", i + 1))
                pool.tensor_tensor(dst, src, nhalf[:, 0:n], ALU.pow).then_inc(S(f"{name}_root"), 1)
                pool.wait_ge(*at(f"{name}_root", i + 1))

            def token_root(name, i):
                k = NORMS.index(name) % 3
                root(name, i, ve[:, k, 4 * i:4 * i + 4], rstd[:, k, 4 * i:4 * i + 4], 4)

            def token_roots(name):
                token_root(name, 0)
                token_root(name, 1)

            link(pool.memset(neglo[:, :], 0.0))
            for q in (1, 3):
                link(pool.memset(neglo[32 * q:32 * q + 32, 0:1], -1.0))
            pool.memset(neglo[64:128, 1:2], -1.0).then_inc(S("neglo_ready"), 1)
            pool.wait_ge(*at("neglo_ready", 1))

            def copy(dst, src):
                return pool.tensor_scalar(dst, src, 1.0, 0.0, ALU.mult, ALU.add)

            def round_parts(name):
                for u in range(16):
                    pool.wait_ge(*at(f"{name}_x", u + 1))
                    copy(pT[:, 4 + u % 4, :].bitcast(F32R), pT[:, u % 4, :]).then_inc(S(f"{name}_xh"), 1)
                    pool.wait_ge(*at(f"{name}_xh", u + 1))

            root("g", 0, gv[:, :], grs[:, :], 1)
            pool.wait_ge(*at("first_in", 16))
            for layer, name in enumerate(("n0_q_b", "n1_q_b")):
                k = VEC[name][0]
                pool.tensor_scalar(qbias[:, layer, :], vcols[:, k:k + 4], HD8 ** -0.5, 0.0,
                                   ALU.mult, ALU.add).then_inc(S("q_bias"), 1)
            link(pool.memset(mask2[:, :], 1.0))
            for q in range(4):
                m = mask2[32 * q:32 * q + 32, :]
                link(select(m, [[-HD8, 2]], 0, 1))
                link(select(m, [[HD8, 2]], HD8 - 1, -1))
            link(pool.memset(mask4[:, :], 1.0))
            link(select(mask4[:, :], [[-HD4, NH4]], 0, 1))
            link(select(mask4[:, :], [[HD4, NH4]], HD4 - 1, -1))
            pool.memset(vaug[:, :, :], 1.0).then_inc(S("ones_cols"), 1)
            pool.wait_ge(*at("ones_cols", 1))

            def small_consts():
                link(pool.memset(ones[:, :], 1.0))
                link(pool.memset(upper[:, :], 1.0))
                link(select(upper[:, :], [[1, P]], 0, -1))
                link(pool.memset(band[:, :], 0.0))
                link(select(band[:, :], [[-1, P]], 0, 1, ALU.is_ge, NEG))
                link(select(band[:, :], [[1, P]], RADIUS, -1, ALU.is_ge, NEG))
                link(pool.memset(tril8[:, :, :], 1.0))
                link(select(tril8[:, :, :], [[1, E], [-1, E]], -1, 0))
                link(pool.memset(fills[:, :, :], 0.0))

            def split_stacks(name):
                for t in range(T):
                    if t == 0:
                        pool.wait_ge(*at(f"{name}_st", 16))
                    if name == "n1" and t == T - 1:
                        token_root("ln1", 0)
                    if t >= 2:
                        pool.wait_ge(*at(f"{name}_s", NH8 * (t - 1)))
                    pool.tensor_tensor(qr[:, t % 2, :, :].rearrange("p (g a) n -> p g a n", a=2),
                                       qst[:, :, P * t:P * t + P].unsqueeze(2).broadcast_to([P, 4, 2, P]),
                                       mask2[:, :].unsqueeze(1).unsqueeze(3).broadcast_to([P, 4, 2, P]),
                                       ALU.mult).then_inc(S(f"{name}_qm"), 1)
                    pool.wait_ge(*at(f"{name}_qm", t + 1))
                    if name == "n1":
                        if t >= 2:
                            pool.wait_ge(*at("n1_pv", 2 * (t - 1)))
                        if t == 0:
                            pool.wait_ge(*at("topi_ready", 1))
                            pool.wait_ge(*at("l1_v", 2))
                        for j in range(KV):
                            r = pool.value_load(topi[t:t + 1, j:j + 1], min_val=0, max_val=T - 1)
                            pool.tensor_tensor(vfil[:, t % 2, j:j + 1, :], vaug[:, bass.ds(r, 1), :],
                                               ones[:, 0:1].unsqueeze(2).broadcast_to([P, 1, VW]),
                                               ALU.mult).then_inc(S("v_gathered"), 1)
                            pool.wait_ge(*at("v_gathered", KV * t + j + 1))

            def add_bias(i):
                v = aK[:, 4 * i:4 * i + 4, :]
                pool.wait_ge(*at("na_norm", 4 * i + 4))
                pool.tensor_tensor(v, v, row("L2_attn_bproj").unsqueeze(1).broadcast_to([P, 4, P]),
                                   ALU.add).then_inc(S("xb2_ready"), 1)

            def split_heads(name, src, mask, nh, scores, tiles=T):
                for t in range(tiles):
                    if t == 2:
                        add_bias(1)
                    if t % 4 == 0:
                        pool.wait_ge(*at(f"{name}_q", t // 4 + 1))
                    if t >= 2:
                        pool.wait_ge(*at(scores, nh * (t - 1)))
                    pool.tensor_tensor(qm[:, t % 2, 0:nh, :],
                                       src[:, P * t:P * t + P].unsqueeze(1).broadcast_to([P, nh, P]),
                                       mask[:, :].unsqueeze(2).broadcast_to([P, nh, P]),
                                       ALU.mult).then_inc(S(f"{name}_qm"), 1)
                    pool.wait_ge(*at(f"{name}_qm", t + 1))

            round_parts("n0")
            small_consts()
            split_stacks("n0")
            pool.wait_ge(*at("conv_w_high", 1))
            pool.tensor_tensor(convw_low[:, :, :], convw[:, :, :], convw_high[:, :, :].bitcast(F32),
                               ALU.subtract).then_inc(S("conv_w_low"), 1)
            pool.wait_ge(*at("n0_sr", HEADS))
            pool.memset(kvpad[:, :, :], 0.0).then_inc(S("kvpad_zero"), 1)
            pool.memset(vaug1[:, :, U:U + 1], 1.0).then_inc(S("ones_cols"), 1)
            root("g", 1, gv[:, :], grs[:, :], 1)
            pool.wait_ge(*at("l1_kp", 2))
            pool.wait_ge(*at("l1_vp", 2))
            pool.wait_ge(*at("kvpad_zero", 1))
            for i in range(2):
                pool.tensor_tensor(kvpad[:, 2 + 16 * i:18 + 16 * i, 2:2 + IMG],
                                   halves(bT)[i].rearrange("p (r w) -> p r w", w=IMG),
                                   halves(cT)[i].rearrange("p (r w) -> p r w", w=IMG),
                                   ALU.add).then_inc(S("kvpad_ready"), 1)
            round_parts("n1")
            pool.wait_ge(*at("kv_high", 1))
            pool.tensor_tensor(kv_low, kvpad.rearrange("p r w -> p (r w)"), kv_high[:, :].bitcast(F32),
                               ALU.subtract).then_inc(S("kv_low"), 1)
            split_stacks("n1")
            token_root("ln2", 0)
            pool.wait_ge(*at("k_gathered", KV * T))
            pool.memset(vaug4[:, :, :, HD4:HD4 + 1], 1.0).then_inc(S("ones_cols"), 1)
            pool.wait_ge(*at("ones_cols", 3))
            token_root("na", 0)
            add_bias(0)
            for name in ("ln1", "ln2", "na"):
                token_root(name, 1)
            split_heads("n2", aT, mask4, NH4, "n2_s")

            def w_high(e):
                if e == 0:
                    pool.wait_ge(*at("fw_in", 32))
                if e >= 2:
                    pool.wait_ge(*at("m2_fc1", 8 * (e - 1)))
                copy(wpart2[:, e % 2, 0, :], fw1[:, e, :]).then_inc(S("m2_w_high"), 1)

            w_high(0)
            w_high(1)
            token_roots("nb")
            token_roots("nn")
            for e in range(E):
                dst = (bT, cT)[e % 2]
                if e == 0:
                    pool.wait_ge(*at("m2_xT", 2))
                if e >= 2:
                    pool.wait_ge(*at("m2_x_low", e - 1))
                pool.tensor_scalar(dst[:, :], nT[:, :], col("L2_ffn_ln_g", e), col("L2_ffn_ln_b", e),
                                   ALU.mult, ALU.add).then_inc(S("m2_xe"), 1)
                if 1 <= e < E - 1:
                    w_high(e + 1)
            def count(dst, pattern, mult):
                return pool.iota(dst, pattern, base=0, channel_multiplier=mult, allow_small_or_imprecise_dtypes=True)

            count(places, [[1, SLOTS]], 0).then_inc(S("places_ready"), 1)
            count(placecol, [[P, SC]], 1).then_inc(S("places_ready"), 1)
            count(placeoff, [[CAP, E]], 0).then_inc(S("places_ready"), 1)
            copy(onesr[:, :], ones[:, :]).then_inc(S("places_ready"), 1)
            pool.wait_ge(*at("places_ready", 4))
            token_roots("nc")
            for t in range(0, T, 4):
                v = aK[:, t:t + 4, :]
                pool.wait_ge(*at("nc_norm", t + 4))
                link(pool.tensor_tensor(v, v, row("L3_attn_b_o").unsqueeze(1).broadcast_to([P, 4, P]), ALU.add))
                pool.tensor_tensor(v, v, bK[:, t:t + 4, :], ALU.add).then_inc(S("xb3_ready"), 1)
            token_roots("nd")
            pool.wait_ge(*at("nd_norm", T))
            pool.wait_ge(*at("x_high", 1))
            pool.tensor_tensor(xpart[:, 1, :, :], bK[:, :, :], xpart[:, 0, :, :].bitcast(F32), ALU.subtract).then_inc(S("x_low"), 1)
            pool.wait_ge(*at("m3_slot", 1))
            pool.tensor_tensor(slotd, ident[:, :].unsqueeze(1).broadcast_to([P, T, P]),
                               slot[:, :].unsqueeze(2).broadcast_to([P, T, P]), ALU.mult).then_inc(S("slot_diagonal"), 1)
            pool.wait_ge(*at("y_clean", 1))
            pool.tensor_tensor(aK[:, 0:4, :], aK[:, 0:4, :], cK[:, 0:4, :], ALU.add).then_inc(S("y_ready_0"), 1)

        @block.scalar
        def _(act):
            def evac2(dst, banks, ready, done, bias=None):
                for i in range(2):
                    act.wait_ge(*at(ready, i + 1))
                    if bias is None:
                        ins = act.activation(halves(dst)[i], ps[:, banks[i], :], ACT.Copy)
                    else:
                        ins = act.activation(halves(dst)[i], ps[:, banks[i], :], ACT.Identity, bias=bias)
                    ins.then_inc(S(done), 1)

            def turned_half(dst, bank, ready, done, i, rows=P):
                act.wait_ge(*at(ready, i + 1))
                act.activation(halves(dst)[i][0:rows], ps[0:rows, bank + i, :], ACT.Copy).then_inc(S(done), 1)

            def stack_parts(name, layer):
                for u in range(16):
                    act.wait_ge(*at(f"{name}_st_ps", u + 1))
                    if u >= 4:
                        act.wait_ge(*at(f"{name}_st", u - 3))
                    k = u // 4
                    bias = qbias[:, layer, k:k + 1] if u % 2 else col(f"{name}_k_b", k)
                    act.activation(pT[:, u % 4, :], ps[:, u % 4, :], ACT.Identity, bias=bias,
                                   scale=HD8 ** -0.5 if u % 2 else 1.0).then_inc(S(f"{name}_x"), 1)

            act.wait_ge(*at("first_in", 16))
            act.wait_ge(*at("q_bias", 2))
            stack_parts("n0", 0)

            def evac_pT(name, m, w):
                act.wait_ge(*at(f"{name}_pt", m + 1))
                if m >= 8:
                    act.wait_ge(*at(f"{name}_pv", (m - 8) // 4 + 1))
                act.activation(pT[:, m % 8, 0:w], ps[:, 4 + m % 2, 0:w], ACT.Copy).then_inc(S(f"{name}_pta"), 1)

            def o_copy(name, t, bank, rows=P):
                act.wait_ge(*at(f"{name}_ot", t + 1))
                act.activation(oT[0:rows, P * t:P * t + P], ps[0:rows, bank, 0:P], ACT.Copy).then_inc(S(f"{name}_oT"), 1)

            def output_steps(name, s):
                t, r = divmod(s - O_COPY, NH8)
                if r == 0 and 0 <= t < T:
                    act.wait_ge(*at(f"{name}_pv", 2 * t + 2))
                    act.activation(vsb[:, :, :], ps[:, 6 + t % 2, 0:2 * P].rearrange("p (a n) -> p a n", a=2),
                                   ACT.Copy).then_inc(S(f"{name}_vc"), 1)
                t, r = divmod(s - O_TURNED, NH8)
                if r == 0 and 0 <= t < T:
                    o_copy(name, t, 6 + t % 2)

            act.wait_ge(*at("conv_in", 16))
            act.activation(convw_high[:, :, :], convw[:, :, :], ACT.Copy).then_inc(S("conv_w_high"), 1)

            for s in range(HEADS + N0_V + 17):
                n = s - N0_EXP
                if 0 <= n < HEADS:
                    t, h = divmod(n, NH8)
                    act.wait_ge(*at("n0_nmx", n // 4 + 1))
                    v = arena_s(t)[:, h, 0:n0_w(n)]
                    act.activation(v, v, ACT.Exp, bias=nmx[:, t, h:h + 1]).then_inc(S("n0_p"), 1)
                m = s - N0_T
                if 0 <= m < HEADS and by_act(m, N0_ACT):
                    evac_pT("n0", m, n0_w(m))
                output_steps("n0", s - N0_V)

            evac2(aT, (0, 1), "l1_qp_ps", "l1_qp", col("L1_conv_bq_proj"))
            evac2(cT, (4, 5), "l1_vp_ps", "l1_vp", col("L1_conv_bv_proj"))
            stack_parts("n1", 1)
            act.wait_ge(*at("kvpad_ready", 2))
            act.wait_ge(*at("loc_sum", 2))
            act.activation(kv_high[:, :], kvpad.rearrange("p r w -> p (r w)"), ACT.Copy).then_inc(S("kv_high"), 1)

            def conv_out(i):
                act.wait_ge(*at("conv_ps", i + 1))
                act.activation(halves(eT)[i], ps[:, 3, :], ACT.Identity, bias=col("L1_conv_conv_b")).then_inc(S("gT_ready"), 1)

            for s in range(HEADS + N1_V + 17):
                n = s - N1_EXP
                if 0 <= n < HEADS:
                    act.wait_ge(*at("n1_nmx", n + 1))
                    if n >= 8:
                        act.wait_ge(*at("n1_pt", n - 7))
                    act.activation(pS8[:, n % 8, :], ps[:, n % N1_S, :], ACT.Exp,
                                   bias=nmx[:, n // NH8, n % NH8:n % NH8 + 1]).then_inc(S("n1_p"), 1)
                m = s - N1_T
                if 0 <= m < HEADS and by_act(m, N1_ACT):
                    evac_pT("n1", m, HALF)
                if s in CONV_COPY:
                    conv_out(CONV_COPY.index(s))
                output_steps("n1", s - N1_V)
            for i in range(2):
                turned_half(nT, 0, "na_tps", "na_T", i)
                turned_half(bT, 4, "n2_k_ps", "n2_k", i)
            for s in range(T + 6):
                if s < T:
                    act.wait_ge(*at("n2_nmx", s + 1))
                    for h in range(NH4):
                        v = pS[:, s % 4, P * h:P * h + P]
                        act.activation(v, v, ACT.Exp, bias=nmx[:, s, h:h + 1]).then_inc(S("n2_p"), 1)
                t = s - 4
                if 0 <= t < T:
                    o_copy("n2", t, 6)
                t = s - 2
                if 0 <= t < T:
                    act.wait_ge(*at("n2_pt", t + 1))
                    if t >= 4:
                        act.wait_ge(*at("n2_pv", t - 3))
                    act.activation(pT[:, t % 4, :], ps[:, 2 + t % 2, :], ACT.Copy).then_inc(S("n2_pta"), 1)

            def router_exp(pre):
                act.wait_ge(*at(f"{pre}_lg", 1))
                act.activation(ex[:, :, :], lg[:, :, :], ACT.Exp).then_inc(S(f"{pre}_ex"), 1)

            def expert_layer(pre, func):
                def x_high(e):
                    if e >= 2:
                        act.wait_ge(*at("m2_fc1", 8 * (e - 1)))
                    act.activation(xpart2[:, e % 2, 0, :], nT[:, :], ACT.Identity, bias=col("L2_ffn_ln_b", e),
                                   scale=col("L2_ffn_ln_g", e)).then_inc(S("m2_x_high"), 1)

                act.wait_ge(*at("m2_xT", 2))
                x_high(0)
                x_high(1)
                router_exp(pre)
                for e in range(E):
                    if 1 <= e < E - 1:
                        x_high(e + 1)
                    for c in range(2 * FC):
                        act.wait_ge(*at(f"{pre}_fc1", 2 * FC * e + c + 1))
                        if e >= 2 and c == 0:
                            act.wait_ge(*at(f"{pre}_fc2", 2 * (e - 1)))
                        act.activation(hid(e)[:, c // 2, HALF * (c % 2):HALF * (c % 2) + HALF], ps[:, c % 4, :], func,
                                       bias=col("L2_ffn_b1", FC * e + c // 2)
                                       ).then_inc(S(f"{pre}_h"), 1)
                    if e == 0:
                        for i in range(2):
                            act.wait_ge(*at(f"{pre}_cwt_ps", i + 1))
                            act.activation(cwT[:, HALF * i:HALF * i + HALF], ps[0:E, 4 + i, :],
                                           ACT.Copy).then_inc(S(f"{pre}_cwT"), 1)

            evac2(oT, (0, 1), "nb_tps", "nb_T")
            evac2(nT, (2, 3), "nn_tps", "m2_xT")
            expert_layer("m2", ACT.Gelu)

            for i in range(2):
                turned_half(nT, 0, "nc_tps", "nc_T", i)
            for i in range(2):
                act.wait_ge(*at("n3_q_ps", i + 1))
                act.activation(halves(bT)[i][0:U], ps[U:2 * U, 2 + i, :], ACT.Copy).then_inc(S("n3_k"), 1)
            for s in range(T + 3):
                if s < T:
                    act.wait_ge(*at("n3_nmx", s + 1))
                    if s >= 2:
                        act.wait_ge(*at("n3_pt", 2 * (s - 1)))
                    act.activation(pS[:, 2 * (s % 2):2 * (s % 2) + 2, :], ps[:, 2 * (s % 2):2 * (s % 2) + 2, :], ACT.Exp,
                                   bias=nmx[:, s, 0:1]).then_inc(S("n3_p"), 1)
                if s >= 3:
                    o_copy("n3", s - 3, 6 + (s - 3) % 2, U)
                t = s - 1
                if 0 <= t < T:
                    act.wait_ge(*at("n3_pt", 2 * t + 2))
                    if t >= 2:
                        act.wait_ge(*at("n3_pv", t - 1))
                    act.activation(pT[:, 2 * (t % 2) + 1, :], ps[:, 5, :], ACT.Copy).then_inc(S("n3_pta"), 1)

            evac2(nT, (0, 1), "nd_tps", "nd_T")
            act.activation(xpart[:, 0, :, :], bK[:, :, :], ACT.Copy).then_inc(S("x_high"), 1)
            router_exp("m3")
            act.wait_ge(*at("m3_gathered", T))
            for c in (0, 2):
                w = min(HALF, SLOTS - HALF * c)
                act.activation(xg[:, HALF * c:HALF * c + w], ps[:, c, 0:w], ACT.Copy).then_inc(S("m3_xg_act"), 1)
                if c == 0:
                    act.wait_ge(*at("slotrow_ps", 1))
                    act.activation(slotrow[:, :].rearrange("p (a n) -> p a n", a=2), ps[:, 6:8, :],
                                   ACT.Copy).then_inc(S("slotrow"), 1)

            def turned_high(g):
                act.wait_ge(*at("m3_turned_ps", g + 1))
                k0, k1 = TURNS[g]
                act.activation(ypart[:, 0, k0:k1, :], ps[:, 1 + g % 2, 0:P * (k1 - k0)].rearrange("p (k c) -> p k c", c=P),
                               ACT.Copy).then_inc(S("m3_high"), 1)

            for e in range(E):
                for c in range(FC):
                    act.wait_ge(*at("m3_fc1", 2 * e + c // 2 + 1))
                    if e >= 2 and c == 0:
                        act.wait_ge(*at("m3_fc2", e - 1))
                    act.activation(hid3(e)[:, c, :], ps[:, 3 + 2 * (e % 2) + c // 2, CAP * (c % 2):CAP * (c % 2) + CAP],
                                   ACT.Relu, bias=col("L3_ffn_b1", FC * e + c)).then_inc(S("m3_h"), 1)
                if e == E - 2:
                    turned_high(0)
                    turned_high(1)
            turned_high(2)
            turned_high(3)
            for i in range(2):
                act.wait_ge(*at("m3_combined", 15 + 5 * i))
                act.activation(halves(cT)[i], ps[:, 3 + i, :], ACT.Copy).then_inc(S("m3_outT"), 1)

        @block.tensor
        def _(pe):
            def mm(dst, lhsT, rhs, start=True, stop=True):
                return pe.matmul(dst, lhsT, rhs, start=start, stop=stop, skip_group_check=True)

            def turn4(bank, srcs, cols=P, rows=P):
                for j, src in enumerate(srcs):
                    ins = pe.transpose(ps[0:rows, bank, cols * j:cols * j + cols], src, ident[0:cols, 0:cols])
                return ins

            def product(ready, banks, w, src, rows=P):
                for i in range(2):
                    mm(ps[0:rows, banks[i], :], w, halves(src)[i]).then_inc(S(ready), 1)

            def values(ready, banks, src, w, n):
                for t in range(T):
                    ins = mm(ps[:, banks[t // 4], n * (t % 4):n * (t % 4) + n], src[:, P * t:P * t + P], w)
                    if t % 4 == 3:
                        ins.then_inc(S(ready), 1)

            def tokens_to_channels(ready, banks, src, norm):
                for i in range(2):
                    pe.wait_ge(*at(norm, 4 * i + 4))
                    turn4(banks[i], [src[:, 4 * i + j, :] for j in range(4)]).then_inc(S(ready), 1)

            def bias_columns(part):
                if part == 0:
                    pe.wait_ge(*at("shift_ready", 1))
                    pe.wait_ge(*at("rpb_in", 16))
                if part:
                    pe.wait_ge(*at("tab_ready", 3))
                for jj in range(16):
                    for r in range(ROWS):
                        ins = mm(ps[32 * r:32 * r + 32, 4 + jj // 4, 128 * (jj % 4):128 * (jj % 4) + NH8 * LR],
                                 shift[:, 16 * part + jj, :], rpbT[:, :, 3 - r:3 - r + LR])
                ins.then_inc(S("bias_ps"), 1)

            def group_average(i, bank):
                if i == 0:
                    pe.wait_ge(*at("gavg_ready", 1))
                pe.wait_ge(*at("gn_stats", i + 1))
                mm(ps[:, bank, 0:2], gavg[:, :], ge[:, :]).then_inc(S("gn_avg"), 1)

            group_average(0, 3)
            bias_columns(0)
            pe.wait_ge(*at("first_in", 16))
            pe.wait_ge(*at("g0_norm", 2))
            pe.wait_ge(*at("gn_read", 1))

            def stack_products(name, k_src, k_w, q_src, q_w):
                for u in range(16):
                    w, src = (q_w, q_src) if u % 2 else (k_w, k_src)
                    g, i = divmod(u // 2, 2)
                    if name == "n1" and u == 10:
                        pe.wait_ge(*at("loc_ready", 1))
                        mm(ps[0:T, 6, 0:T], loc[:, 0, :], loc[:, 1, :]).then_inc(S("sloc_ps"), 1)
                    if u >= 4:
                        pe.wait_ge(*at(f"{name}_x", u - 3))
                    for q in range(4):
                        ins = mm(ps[32 * q:32 * q + 32, u % 4, :], w[:, 32 * g:32 * g + 32], halves(src)[i])
                    ins.then_inc(S(f"{name}_st_ps"), 1)

            stack_products("n0", nT, w0[:, 1, :], nT, w0[:, 0, :])
            bias_columns(1)
            pe.wait_ge(*at("n0_x", 16))
            values("n0_v_ps", (0, 1), nT, w0[:, 2, :], P)
            pe.wait_ge(*at("n0_st", 16))
            pe.wait_ge(*at("n0_v", 2))
            pe.wait_ge(*at("tab_ready", 6))

            pe.wait_ge(*at("ones_cols", 1))

            def attention(name, scores, banks, s_free, t_lag, v_lag, srcs, values_of, every, project):
                for s in range(HEADS + v_lag + 17):
                    t, r = divmod(s - v_lag - O_TURN, NH8)
                    if r == 0 and 0 <= t < T:
                        pe.wait_ge(*at(f"{name}_vc", t + 1))
                        for i in range(2):
                            ins = pe.transpose(ps[:, 6 + t % 2, P * i:P * i + P], vsb[:, i, :], ident[:, :])
                        ins.then_inc(S(f"{name}_vt"), 1)
                    t, r = divmod(s - v_lag - O_PROJECT, NH8)
                    if r == 0 and 0 <= t < T:
                        pe.wait_ge(*at(f"{name}_oT", t + 1))
                        project(t, ps[:, 6 + t % 2, 0:P]).then_inc(S(f"{name}_proj"), 1)
                    t, r = divmod(s - v_lag - O_BACK, NH8)
                    if r == 0 and 0 <= t < T:
                        pe.wait_ge(*at(f"{name}_o", t + 1))
                        pe.transpose(ps[:, 6 + t % 2, 0:P], oK[:, t % 2, :], ident[:, :]).then_inc(S(f"{name}_ot"), 1)
                    if s < HEADS:
                        t, h = divmod(s, NH8)
                        if h == 0:
                            pe.wait_ge(*at(f"{name}_qm", t + 1))
                            if name == "n1":
                                pe.wait_ge(*at("k_gathered", KV * (t + 1)))
                        if s >= banks:
                            pe.wait_ge(*at(s_free, s - banks + 1))
                        scores(t, h, ps[:, s % banks, :]).then_inc(S(f"{name}_s"), 1)
                        if name == "n1":
                            for i in range(2):
                                if 0 <= s - CONV_START[i] < 25:
                                    conv_tap(i, s - CONV_START[i])
                                if s == CONV_TURN[i]:
                                    pe.wait_ge(*at("gT_ready", i + 1))
                                    turn4(3, [halves(eT)[i][:, P * j:P * j + P] for j in range(4)]).then_inc(S("gt_ps"), 1)
                    m = s - t_lag
                    if 0 <= m < HEADS:
                        pe.wait_ge(*at(f"{name}_p", m + 1))
                        if name == "n1" and m == 0:
                            pe.wait_ge(*at("x1_tok", 2))
                        if m >= 2:
                            copied(pe, name, m - 2, every)
                        turn4(4 + m % 2, srcs(m)).then_inc(S(f"{name}_pt"), 1)
                    m = s - v_lag
                    if 0 <= m < HEADS and m % 4 == 3:
                        t, h = divmod(m - 3, NH8)
                        for i in range(4):
                            copied(pe, name, m - 3 + i, every)
                        if h == 0 and t >= 2:
                            pe.wait_ge(*at(f"{name}_add", t - 1))
                        if h == 0 and name == "n1" and t == 0:
                            pe.wait_ge(*at("n1_tok", 2))
                        if h == 0 and name == "n1":
                            pe.wait_ge(*at("v_gathered", KV * (t + 1)))
                        vs = values_of(t)
                        for j, v in enumerate(vs):
                            for i in range(4):
                                k = (HD8 + 1) * (h + i)
                                ins = mm(ps[32 * i:32 * i + 32, 6 + t % 2, P * (h // 4):P * (h // 4) + P], v[:, k:k + 32],
                                         pT[:, (m - 3 + i) % 8, P * j:P * j + P], start=j == 0, stop=j == len(vs) - 1)
                        ins.then_inc(S(f"{name}_pv"), 1)

            def n0_scores(t, h, bank):
                return mm(bank[:, 0:P * (n0_hi(t) - n0_lo(t))], qr[:, t % 2, h, :], kr[:, h // 2, P * n0_lo(t):P * n0_hi(t)])

            attention("n0", n0_scores, N0_S, "n0_sr", N0_T, N0_V,
                      lambda m: [arena_s(m // NH8)[:, m % NH8, P * j:P * j + P] for j in range(n0_w(m) // P)],
                      lambda t: [vaug[:, k, :] for k in range(n0_lo(t), n0_hi(t))], N0_ACT,
                      lambda t, bank: mm(bank, w0[:, 3, :], oT[:, P * t:P * t + P]))

            group_average(1, 2)
            pe.wait_ge(*at("w1_in", 16))
            pe.wait_ge(*at("g1_norm", 2))
            product("l1_qp_ps", (0, 1), w1[:, 0, :], nT)
            pe.wait_ge(*at("gn_read", 2))
            product("l1_kp_ps", (2, 3), w1[:, 1, :], nT)
            product("l1_vp_ps", (4, 5), w1[:, 2, :], nT)
            pe.wait_ge(*at("l1_qp", 2))
            pe.wait_ge(*at("l1_kp", 2))
            stack_products("n1", bT, w1[:, 4, :], aT, w1[:, 3, :])
            pe.wait_ge(*at("l1_vp", 2))
            pe.wait_ge(*at("n1_x", 16))
            values("l1_v_ps", (0, 1), cT, w1[:, 5, :], P)
            for i in range(2):
                turn4(4 + i, [halves(xT)[i][:, P * j:P * j + P] for j in range(4)]).then_inc(S("x1t_ps"), 1)
            pe.wait_ge(*at("topi_ready", 1))
            for i in range(2):
                turn4(6 + i, [halves(nT)[i][:, P * j:P * j + P] for j in range(4)]).then_inc(S("n1t_ps"), 1)
            pe.wait_ge(*at("l1_v", 2))
            for name in ("conv_w_high", "conv_w_low", "kv_high", "kv_low"):
                pe.wait_ge(*at(name, 1))
            pe.wait_ge(*at("topi_ready", 1))

            def conv_tap(i, k):
                if k == 0 and i:
                    pe.wait_ge(*at("g_tok", 1))
                dy, dx = divmod(k, 5)
                for j, (a, b) in enumerate(PASSES):
                    ins = mm(ps[:, 3, :], convw_parts[a][:, k, :], kv_parts[b][:, 16 * i + dy:16 * i + dy + 16, dx:dx + IMG],
                             start=k == 0 and j == 0, stop=k == 24 and j == 2)
                if k == 24:
                    ins.then_inc(S("conv_ps"), 1)


            def n1_scores(t, h, bank):
                return mm(bank, qr[:, t % 2, h, :], kfil[:, t % 2, h // 2, :])

            attention("n1", n1_scores, N1_S, "n1_p", N1_T, N1_V,
                      lambda m: [pS8[:, m % 8, P * j:P * j + P] for j in range(KV)], lambda t: [vfil[:, t % 2, j, :] for j in range(KV)], N1_ACT,
                      lambda t, bank: mm(bank, oT[:, P * t:P * t + P], w1[:, 6, :]))

            def channels_half(norm, i):
                pe.wait_ge(*at(f"{norm}_norm", 4 * i + 4))
                turn4(i, [bK[:, 4 * i + j, :] for j in range(4)]).then_inc(S(f"{norm}_tps"), 1)

            def values_half(name, i, wv, n):
                for j in range(4):
                    ins = mm(ps[:, 6 + i, n * j:n * j + n], halves(nT)[i][:, P * j:P * j + P], wv)
                ins.then_inc(S(f"{name}_v_ps"), 1)

            pe.wait_ge(*at("g_tok", 2))
            pe.wait_ge(*at("n1_add", T))
            pe.wait_ge(*at("late_in", 16))
            for i in range(2):
                channels_half("na", i)
                pe.wait_ge(*at("na_T", i + 1))
                mm(ps[:, 2 + i, :], w2a[:, 0:P], halves(nT)[i]).then_inc(S("n2_q_ps"), 1)
                mm(ps[:, 4 + i, :], w2a[:, P:2 * P], halves(nT)[i]).then_inc(S("n2_k_ps"), 1)
                values_half("n2", i, w2a[:, 2 * P:3 * P], P)
            pe.wait_ge(*at("n2_q", 2))
            pe.wait_ge(*at("n2_k", 2))
            pe.wait_ge(*at("n2_v", 2))
            for s in range(T + 6):
                if s < T:
                    pe.wait_ge(*at("n2_qm", s + 1))
                    if s >= 2:
                        pe.wait_ge(*at("n2_sr", s - 1))
                    for h in range(NH4):
                        mm(ps[:, s % 2, P * h:P * h + P], qm[:, s % 2, h, :],
                           bT[:, P * s:P * s + P]).then_inc(S("n2_s"), 1)
                t = s - 4
                if 0 <= t < T:
                    pe.wait_ge(*at("n2_o", t + 1))
                    if t >= 1:
                        pe.wait_ge(*at("n2_oT", t))
                    pe.transpose(ps[:, 6, 0:P], oK[:, t % 2, :], ident[:, :]).then_inc(S("n2_ot"), 1)
                t = s - 2
                if 0 <= t < T:
                    pe.wait_ge(*at("n2_p", NH4 * (t + 1)))
                    if t >= 2:
                        pe.wait_ge(*at("n2_pta", t - 1))
                    turn4(2 + t % 2, [pS[:, t % 4, P * h:P * h + P] for h in range(NH4)]).then_inc(S("n2_pt"), 1)
                t = s - 3
                if 0 <= t < T:
                    pe.wait_ge(*at("n2_pta", t + 1))
                    if t >= 2:
                        pe.wait_ge(*at("n2_o", t - 1))
                    for h in range(NH4):
                        ins = mm(ps[:, 4 + t % 2, 33 * h:33 * h + 33], pT[:, t % 4, P * h:P * h + P], vaug4[:, t, h, :])
                    ins.then_inc(S("n2_pv"), 1)
                t = s - 5
                if 0 <= t < T:
                    pe.wait_ge(*at("n2_oT", t + 1))
                    if t >= 1:
                        pe.wait_ge(*at("n2_add", t))
                    mm(ps[:, 7, 0:P], oT[:, P * t:P * t + P], w2p[:, :]).then_inc(S("n2_proj"), 1)

            def router(pre, k, bank, src, ready, tiles):
                for t in tiles:
                    if t % 4 == 0:
                        pe.wait_ge(*at(ready, t // 4 + 1))
                    ins = mm(ps[:, bank, E * t:E * t + E], src[:, P * t:P * t + P], rout[:, k, :])
                    if t % 4 == 3:
                        ins.then_inc(S(f"{pre}_lg_ps"), 1)

            def experts(pre, x_ready, w_ready):
                def fc2(e):
                    w_ready(e, 1)
                    for t in range(T):
                        bank = 4 + 2 * (e % 2) + t // 4
                        if t % 4 == 0:
                            if e < 2:
                                pe.wait_ge(*at(f"{pre}_b2", 2))
                            else:
                                pe.wait_ge(*at(f"{pre}_acc", T * (e - 2) + t + 4))
                            pe.wait_ge(*at(f"{pre}_h", 2 * FC * (e + 1)))
                        for c in range(FC):
                            ins = mm(ps[:, bank, P * (t % 4):P * (t % 4) + P], hid(e)[:, c, P * t:P * t + P],
                                     fw2[:, e, c, :], start=c == 0, stop=c == FC - 1)
                        if t % 4 == 3:
                            ins.then_inc(S(f"{pre}_fc2"), 1)

                def second_biases():
                    pe.wait_ge(*at("fb2_in", 16))
                    for i in range(2):
                        pe.wait_ge(*at(f"{pre}_cwT", i + 1))
                        for j in range(4):
                            t = 4 * i + j
                            ins = mm(ps[:, 6 + i, P * j:P * j + P], cwT[:, P * t:P * t + P], fb2[:, :])
                        ins.then_inc(S(f"{pre}_b2_ps"), 1)

                for e in range(E):
                    x_ready(e)
                    w_ready(e, 0)
                    for c in range(2 * FC):
                        g = 2 * FC * e + c
                        if g == 2 * FC + 4:
                            second_biases()
                        if g >= 4:
                            pe.wait_ge(*at(f"{pre}_h", g - 3))
                        for k, (a, b) in enumerate(PASSES):
                            ins = mm(ps[:, c % 4, :], wpart2[:, e % 2, a, P * (c // 2):P * (c // 2) + P],
                                     halves(xpart2[:, e % 2, b, :])[c % 2], start=k == 0, stop=k == 2)
                        ins.then_inc(S(f"{pre}_fc1"), 1)
                    if e == 0:
                        pe.wait_ge(*at(f"{pre}_cw", 1))
                        for i in range(2):
                            for j in range(4):
                                ins = pe.transpose(ps[0:E, 4 + i, P * j:P * j + P], cw[:, 4 * i + j, :], ident[:, :])
                            ins.then_inc(S(f"{pre}_cwt_ps"), 1)
                    if e:
                        fc2(e - 1)
                fc2(E - 1)

            tokens_to_channels("nb_tps", (0, 1), bK, "nb_norm")
            router("m2", 0, 4, oT, "nb_T", range(0, 4))
            tokens_to_channels("nn_tps", (2, 3), cK, "nn_norm")
            router("m2", 0, 4, oT, "nb_T", range(4, T))
            pe.wait_ge(*at("m2_xT", 2))

            def m2_w(e, second):
                pe.wait_ge(*at("fw_in", 32))

            def m2_parts(e):
                for name in ("m2_x_high", "m2_x_low", "m2_w_high", "m2_w_low"):
                    pe.wait_ge(*at(name, e + 1))

            experts("m2", m2_parts, m2_w)

            pe.wait_ge(*at("w3_in", 16))
            pe.wait_ge(*at("m2_acc", T * E))
            channels_half("nc", 0)
            channels_half("nc", 1)
            for i in range(2):
                pe.wait_ge(*at("nc_T", i + 1))
                mm(ps[:, 2 + i, :], w3q[:, 0:2, :].rearrange("p a u -> p (a u)"), halves(nT)[i]).then_inc(S("n3_q_ps"), 1)
            for i in range(2):
                values_half("n3", i, w3q[:, 2, :], U)
            pe.wait_ge(*at("n3_q", 2))
            pe.wait_ge(*at("n3_k", 2))
            pe.wait_ge(*at("n3_v", 2))
            for s in range(T + 4):
                if s < T:
                    if s >= 2:
                        pe.wait_ge(*at("n3_p", s - 1))
                    for i in range(2):
                        ins = mm(ps[:, 2 * (s % 2) + i, :], aT[0:U, P * s:P * s + P], bT[0:U, HALF * i:HALF * i + HALF])
                    ins.then_inc(S("n3_s"), 1)
                t = s - 2
                if 0 <= t < T:
                    pe.wait_ge(*at("n3_ptd", t + 1))
                    pe.wait_ge(*at("n3_pta", t + 1))
                    if t >= 2:
                        pe.wait_ge(*at("n3_add", t - 1))
                    for k in range(T):
                        ins = mm(ps[:, 6 + t % 2, 0:U + 1], pT[:, 2 * (t % 2) + k // 4, P * (k % 4):P * (k % 4) + P],
                                 vaug1[:, k, :], start=k == 0, stop=k == T - 1)
                    ins.then_inc(S("n3_pv"), 1)
                t = s - 3
                if 0 <= t < T:
                    pe.wait_ge(*at("n3_o", t + 1))
                    pe.transpose(ps[0:U, 6 + t % 2, 0:P], oK[:, t % 2, 0:U], ident[:, :]).then_inc(S("n3_ot"), 1)
                t = s - 1
                if 0 <= t < T:
                    pe.wait_ge(*at("n3_p", t + 1))
                    for i in range(2):
                        if t >= 1:
                            pe.wait_ge(*at("n3_pta" if i else "n3_ptd", t))
                        turn4(4 + i, [pS[:, 2 * (t % 2) + i, P * j:P * j + P] for j in range(4)]).then_inc(S("n3_pt"), 1)
                t = s - 3
                if 0 <= t < T:
                    pe.wait_ge(*at("n3_oT", t + 1))
                    mm(ps[:, 6 + t % 2, 0:P], oT[0:U, P * t:P * t + P], w3o[:, :]).then_inc(S("n3_proj"), 1)

            tokens_to_channels("nd_tps", (0, 1), bK, "nd_norm")
            router("m3", 1, 2, nT, "nd_T", range(T))
            pe.wait_ge(*at("m3_hot", 1))
            mm(ps[:, 3, 0:T * E], upper[:, :], rank[:, :, :], stop=False)
            pe.wait_ge(*at("m3_before", 2))
            mm(ps[:, 3, E:T * E], ones[:, :], before[:, 0:T - 1, :], start=False).then_inc(S("m3_pos"), 1)
            pe.wait_ge(*at("x_high", 1))
            pe.wait_ge(*at("x_low", 1))
            cuts = [(c, HALF * c, min(HALF * c + HALF, SLOTS)) for c in range(3)]
            for t in range(T):
                pe.wait_ge(*at("m3_hot_ready", t + 1))
                for a in range(2):
                    for c, k0, k1 in cuts:
                        ins = mm(ps[:, c, 0:k1 - k0], xpart[:, a, t, :], hot(t)[:, k0:k1],
                                 start=t == 0 and a == 0, stop=t == T - 1 and a == 1)
                ins.then_inc(S("m3_gathered"), 1)
            pe.wait_ge(*at("slot_diagonal", 1))
            pe.wait_ge(*at("places_ready", 4))
            for i in range(2):
                ins = mm(ps[:, 6 + i, :], onesr[:, :], slotd[:, 4 * i:4 * i + 4, :])
            ins.then_inc(S("slotrow_ps"), 1)

            def m3_fc2(e):
                pe.wait_ge(*at("m3_h", FC * (e + 1)))
                if e >= 2:
                    pe.wait_ge(*at("m3_y", e - 1))
                for c in range(FC):
                    ins = mm(ps[:, 0 if e % 2 else 7, 0:CAP], fw2[:, e, c, :], hid3(e)[:, c, :], start=c == 0, stop=c == FC - 1)
                ins.then_inc(S("m3_fc2"), 1)

            def m3_turn(g):
                k0, k1 = TURNS[g]
                pe.wait_ge(*at("m3_clean", g // 2 + 1))
                if g >= 2:
                    pe.wait_ge(*at("m3_low", g - 1))
                turn4(1 + g % 2, [yT[:, P * k:P * k + P] for k in range(k0, k1)]).then_inc(S("m3_turned_ps"), 1)

            def m3_out_turn(i):
                pe.wait_ge(*at("m3_outT", i + 1))
                turn4(5 + i, [halves(cT)[i][:, P * j:P * j + P] for j in range(4)]).then_inc(S("m3_out_ps"), 1)

            def m3_combine(part):
                for j in range(SC):
                    n = SC * part + j
                    i, k = COMBINE[n]
                    g = [k < k1 for _, k1 in TURNS].index(True)
                    pe.wait_ge(*at("m3_high", g + 1))
                    pe.wait_ge(*at("m3_low", g + 1))
                    pe.wait_ge(*at("m3_hotT", n + 1))
                    for a in range(2):
                        ins = mm(ps[:, 3 + i, :], ypart[:, a, k, :], hotT(n), start=k == 0 and a == 0, stop=k == SC - 1 and a == 1)
                    ins.then_inc(S("m3_combined"), 1)
                    if n == 2 * SC - 3:
                        m3_out_turn(0)

            pe.wait_ge(*at("fv_in", 2 * 16 * E))
            for e in range(E):
                if e == 0:
                    pe.wait_ge(*at("m3_xg_act", 1))
                if e == 1:
                    pe.wait_ge(*at("slotrow", 1))
                if e == 3:
                    pe.wait_ge(*at("m3_xg_dve", 1))
                if e == 6:
                    pe.wait_ge(*at("m3_xg_act", 2))
                if e >= 2:
                    pe.wait_ge(*at("m3_h", FC * (e - 1)))
                for c in range(FC):
                    ins = mm(ps[:, 3 + 2 * (e % 2) + c // 2, CAP * (c % 2):CAP * (c % 2) + CAP], fw1[:, e, P * c:P * c + P],
                             xg[:, CAP * e:CAP * e + CAP])
                    if c % 2:
                        ins.then_inc(S("m3_fc1"), 1)
                if e:
                    m3_fc2(e - 1)
                if e == E - 2:
                    m3_turn(0)
                    m3_turn(1)
            m3_fc2(E - 1)
            m3_combine(0)
            m3_turn(2)
            m3_turn(3)
            m3_combine(1)
            m3_out_turn(1)

        @block.vector
        def _(dve):
            link = Chain(dve, S("dve_chain"))

            def group_norm(i, bank, norm):
                for k in range(2):
                    ins = dve.bn_stats(st[:, 0, k, :], halves(xT)[k])
                    link(ins)
                link(dve.bn_aggr(mv[:, 0, 0, :], st[:, 0, 0:2, :]))
                link(dve.tensor_copy(ge[:, 0:1], mv[:, 0, 0, 0:1]))
                dve.scalar_tensor_tensor(ge[:, 1:2], mv[:, 0, 0, 0:1], mv[:, 0, 0, 0:1], mv[:, 0, 0, 1:2],
                                         ALU.mult, ALU.add).then_inc(S("gn_stats"), 1)
                dve.wait_ge(*at("gn_avg", i + 1))
                dve.tensor_copy(gm[:, :], ps[:, bank, 0:2]).then_inc(S("gn_read"), 1)
                dve.wait_ge(*at("gn_read", i + 1))
                link(dve.scalar_tensor_tensor(gv[:, :], gm[:, 0:1], gm[:, 0:1], gm[:, 1:2], ALU.mult, ALU.subtract))
                dve.tensor_scalar(gv[:, :], gv[:, :], -1.0, 1e-5, ALU.mult, ALU.add).then_inc(S("g_var"), 1)
                dve.wait_ge(*at("g_root", i + 1))
                for k in range(2):
                    dve.tensor_scalar(halves(nT)[k], halves(xT)[k], gm[:, 0:1], grs[:, :],
                                      ALU.subtract, ALU.mult).then_inc(S(norm), 1)

            def stats_of(name, src, t):
                dve.bn_stats(st[:, NORMS.index(name) % 3, t, :], src[:, t, :]).then_inc(S(f"{name}_norm_st"), 1)

            def mean_of(name, t):
                k = NORMS.index(name) % 3
                dve.wait_ge(*at(f"{name}_norm_st", t + 1))
                dve.bn_aggr(mv[:, k, t, :], st[:, k, t, :]).then_inc(S(f"{name}_norm_mv"), 1)
                if t % 4 == 3:
                    dve.wait_ge(*at(f"{name}_norm_mv", t + 1))
                    dve.tensor_scalar(ve[:, k, t - 3:t + 1], mv[:, k, t - 3:t + 1, 1], 1e-5, None,
                                      ALU.add).then_inc(S(f"{name}_var"), 1)

            def normalise_tile(name, src, dst, t):
                k = NORMS.index(name) % 3
                dve.wait_ge(*at(f"{name}_root", t // 4 + 1))
                dve.tensor_scalar(dst[:, t, :], src[:, t, :], mv[:, k, t, 0:1], rstd[:, k, t:t + 1],
                                  ALU.subtract, ALU.mult).then_inc(S(f"{name}_norm"), 1)

            def half_stats(name, src, i, before):
                dve.wait_ge(*at(f"{before}_norm", 4 * i + 4))
                for t in range(4 * i, 4 * i + 4):
                    stats_of(name, src, t)
                for t in range(4 * i, 4 * i + 4):
                    mean_of(name, t)

            def normalise_half(name, src, dst, i):
                for t in range(4 * i, 4 * i + 4):
                    normalise_tile(name, src, dst, t)

            dve.wait_ge(*at("x_in", 16))
            group_norm(0, 3, "g0_norm")
            dve.wait_ge(*at("rmask_ready", 1))

            def bias_tables(part):
                dve.wait_ge(*at("bias_ps", part + 1))
                x = ps[:, 4:8, :].rearrange("p b (q c) -> p (b q) c", c=128)[:, :, 0:NH8 * LR]
                x = x.rearrange("p j (h l) -> p h l j", l=LR)
                for k, (tab, l0, l1) in enumerate(((tab_i, 0, LR), (tab_t, ROWS, LR), (tab_b, 0, 8))):
                    for h in range(0, NH8, 4):
                        ins = dve.tensor_tensor(
                            tab[:, h:h + 4, :, 16 * part:16 * part + 16], x[:, h:h + 4, l0:l1, :],
                            rmask[:, k, l0:l1].unsqueeze(1).unsqueeze(3).broadcast_to([P, 4, l1 - l0, 16]), ALU.add)
                    ins.then_inc(S("tab_ready"), 1)

            bias_tables(0)

            def pick_regions():
                dve.wait_ge(*at("sloc_ps", 1))
                link(dve.tensor_copy(sloc[:, :], ps[0:T, 6, 0:T]))
                link(dve.max(top8[:, :], sloc[:, :]))
                dve.max_index(topi[:, :], top8[:, :], sloc[:, :]).then_inc(S("topi_ready"), 1)
                dve.wait_ge(*at("topi_ready", 1))

            def stack_lows(name):
                for v in range(16):
                    if name == "n1" and v == 12:
                        pick_regions()
                    g, i = divmod(v // 2, 2)
                    dst = qst if v % 2 else kr if name == "n0" else kst
                    dve.wait_ge(*at(f"{name}_xh", v + 1))
                    dve.scalar_tensor_tensor(dst[:, g, HALF * i:HALF * i + HALF], pT[:, 4 + v % 4, :],
                                             neglo[:, 1 - v % 2:2 - v % 2], pT[:, v % 4, :],
                                             ALU.mult, ALU.add).then_inc(S(f"{name}_st"), 1)

            dve.wait_ge(*at("first_in", 16))
            dve.wait_ge(*at("neglo_ready", 1))
            stack_lows("n0")

            def evac_values(ready, done, banks, dst, bias=None, halves_of=(0, 1)):
                for i in halves_of:
                    dve.wait_ge(*at(ready, i + 1))
                    d = dst(i)
                    w = d.shape[1] * d.shape[2] * d.shape[3]
                    src = ps[:, banks[i], 0:w].rearrange("p (t h d) -> p t h d", t=4, h=d.shape[2])
                    if bias is None:
                        ins = dve.tensor_copy(d, src)
                    else:
                        ins = dve.tensor_tensor(d, src, bias.rearrange("p (h d) -> p h d", d=HD8).unsqueeze(1)
                                                .broadcast_to(list(d.shape)), ALU.add)
                    ins.then_inc(S(done), 1)

            dve.wait_ge(*at("row_in", 16))
            def vaug_heads(i):
                v = vaug[:, 4 * i:4 * i + 4, 0:NH8 * (HD8 + 1)]
                return v.rearrange("p t (h d) -> p t h d", h=NH8)[:, :, :, 0:HD8]

            dve.wait_ge(*at("ones_cols", 1))
            bias_tables(1)
            evac_values("n0_v_ps", "n0_v", (0, 1), vaug_heads, row("L0_conv_v_b"))

            def evac_pT(name, m, w):
                dve.wait_ge(*at(f"{name}_pt", m + 1))
                if m >= 8:
                    dve.wait_ge(*at(f"{name}_pv", (m - 8) // 4 + 1))
                dve.tensor_copy(pT[:, m % 8, 0:w], ps[:, 4 + m % 2, 0:w]).then_inc(S(f"{name}_ptd"), 1)

            def normalise(name, t, bank, nh, hd, step=None):
                step = step or hd + 1
                o = ps[:, bank, 0:nh * step].rearrange("p (h d) -> p h d", h=nh)
                if t >= 2:
                    dve.wait_ge(*at(f"{name}_ot", t - 1))
                link(dve.reciprocal(rs[:, t % 2, 0:nh], o[:, :, hd]))
                dve.tensor_tensor(oK[:, t % 2, 0:nh * hd].rearrange("p (h d) -> p h d", h=nh), o[:, :, 0:hd],
                                  rs[:, t % 2, 0:nh].unsqueeze(2).broadcast_to([P, nh, hd]),
                                  ALU.mult).then_inc(S(f"{name}_o"), 1)

            dve.wait_ge(*at("tab_ready", 6))
            for s in range(HEADS + N0_V + 17):
                t, r = divmod(s - N0_V - O_ADD, NH8)
                if r == 0 and 0 <= t < T:
                    dve.wait_ge(*at("n0_proj", t + 1))
                    v = xT[:, P * t:P * t + P]
                    dve.scalar_tensor_tensor(v, ps[:, 6 + t % 2, 0:P], col("L0_conv_proj_b"), v,
                                             ALU.add, ALU.add).then_inc(S("n0_add"), 1)
                t, r = divmod(s - N0_V - O_NORM, NH8)
                if r == 0 and 0 <= t < T:
                    dve.wait_ge(*at("n0_vt", t + 1))
                    normalise("n0", t, 6 + t % 2, NH8, HD8, 32)
                if s < HEADS:
                    t, h = divmod(s, NH8)
                    w = n0_w(s)
                    tab = tab_t if t == 0 else tab_b if t == T - 1 else tab_i
                    dve.wait_ge(*at("n0_s", s + 1))
                    if t >= 3 and h == 0:
                        dve.wait_ge(*at("n0_pt", NH8 * (t - 2)))
                    if t >= 2 and h == 0:
                        dve.wait_ge(*at("n0_nmx", 2 * (t - 1)))
                    dve.tensor_tensor_reduce(arena_s(t)[:, h, 0:w], ps[:, s % 4, 0:w],
                                             tab[:, h, :, :].rearrange("p l j -> p (l j)"), 1.0, -FMAX,
                                             ALU.add, ALU.max, mx[:, t % 2, h:h + 1]).then_inc(S("n0_sr"), 1)
                    if h % 4 == 3:
                        dve.wait_ge(*at("n0_sr", s + 1))
                        dve.tensor_scalar(nmx[:, t, h - 3:h + 1], mx[:, t % 2, h - 3:h + 1], -1.0, None, ALU.mult).then_inc(S("n0_nmx"), 1)
                m = s - N0_T
                if 0 <= m < HEADS and not by_act(m, N0_ACT):
                    evac_pT("n0", m, n0_w(m))
            dve.wait_ge(*at("n0_add", T))

            group_norm(1, 2, "g1_norm")
            for i in range(2):
                dve.wait_ge(*at("l1_kp_ps", i + 1))
                dve.tensor_scalar(halves(bT)[i], ps[:, 2 + i, :], col("L1_conv_bk_proj"), None, ALU.add).then_inc(S("l1_kp"), 1)
            dve.wait_ge(*at("l1_qp", 2))
            dve.wait_ge(*at("l1_kp", 2))
            for i, src in enumerate((aT, bT)):
                dve.tensor_reduce(loc[:, i, :], src[:, :].rearrange("p (t n) -> p t n", t=T), AX.X,
                                  ALU.add).then_inc(S("loc_sum"), 1)
            dve.wait_ge(*at("loc_sum", 2))
            dve.tensor_scalar(loc[:, :, :], loc[:, :, :], 1.0 / P, None, ALU.mult).then_inc(S("loc_ready"), 1)
            stack_lows("n1")
            def residual(ready, done, banks, dst, bias, halves_of=(0, 1)):
                for i in halves_of:
                    dve.wait_ge(*at(ready, i + 1))
                    dve.tensor_tensor(dst[:, 4 * i:4 * i + 4, :], ps[:, banks[i], :].rearrange("p (t c) -> p t c", t=4),
                                      row(bias).unsqueeze(1).broadcast_to([P, 4, P]), ALU.add).then_inc(S(done), 1)


            def gather_keys(t, j):
                if t >= 2:
                    dve.wait_ge(*at("n1_s", NH8 * (t - 1)))
                r = dve.value_load(topi[t:t + 1, j:j + 1], min_val=0, max_val=T - 1)
                dve.tensor_copy(kfil[:, t % 2, :, P * j:P * j + P],
                                kst[:, :, bass.ds(r * P, P)]).then_inc(S("k_gathered"), 1)

            def gain_tile(name, src, gain, t):
                dve.wait_ge(*at(f"{name}_norm_mv", t + 1))
                dve.scalar_tensor_tensor(src[:, t, :], src[:, t, :], mv[:, NORMS.index(name) % 3, t, 0:1], row(gain),
                                         ALU.subtract, ALU.mult).then_inc(S(f"{name}_norm_gain"), 1)

            def add_tile(name, src, plus, t):
                dve.wait_ge(*at(f"{name}_root", t // 4 + 1))
                dve.wait_ge(*at(f"{name}_norm_gain", t + 1))
                dve.scalar_tensor_tensor(plus[:, t, :], src[:, t, :], rstd[:, NORMS.index(name) % 3, t:t + 1], plus[:, t, :],
                                         ALU.mult, ALU.add).then_inc(S(f"{name}_norm"), 1)

            def early_norms(s):
                def tile(first):
                    return s - first if first <= s < first + 4 else None
                if (t := tile(48)) is not None:
                    gain_tile("ln1", bK, "L1_conv_ln1_g", t)
                if (t := tile(50)) is not None:
                    dve.wait_ge(*at("g_tok", 1))
                    add_tile("ln1", bK, cK, t)
                if (t := tile(51)) is not None:
                    dve.wait_ge(*at("ln1_norm", t + 1))
                    stats_of("ln2", cK, t)
                if (t := tile(52)) is not None:
                    mean_of("ln2", t)
                if (t := tile(53)) is not None:
                    gain_tile("ln2", cK, "L1_conv_ln2_g", t)
                if (t := tile(57)) is not None:
                    add_tile("ln2", cK, aK, t)
                if (t := tile(58)) is not None:
                    dve.wait_ge(*at("ln2_norm", t + 1))
                    stats_of("na", aK, t)
                if (t := tile(59)) is not None:
                    mean_of("na", t)
                if (t := tile(64)) is not None:
                    normalise_tile("na", aK, bK, t)

            dve.wait_ge(*at("n1_st", 16))
            for j in range(KV):
                gather_keys(0, j)
            evac_values("l1_v_ps", "l1_v", (0, 1), vaug_heads, row("L1_conv_bv_a"))
            for s in range(HEADS + N1_V + 17):
                t, r = divmod(s + NH8 - 2, NH8)
                if r < KV and 0 < t < T:
                    gather_keys(t, r)
                t, r = divmod(s - N1_V - O_ADD, NH8)
                if r == 0 and 0 <= t < T:
                    dve.wait_ge(*at("n1_proj", t + 1))
                    dve.tensor_tensor(bK[:, t, :], ps[:, 6 + t % 2, 0:P], bK[:, t, :], ALU.add).then_inc(S("n1_add"), 1)
                if r == 1 and 0 <= t < T:
                    dve.wait_ge(*at("n1_add", t + 1))
                    stats_of("ln1", bK, t)
                if r == 2 and 0 <= t < T:
                    mean_of("ln1", t)
                if s in CONV_ADD:
                    residual("gt_ps", "g_tok", (3, 3), cK, "L1_conv_ln1_b", (CONV_ADD.index(s),))
                t, r = divmod(s - N1_V - O_NORM, NH8)
                if r == 0 and 0 <= t < T:
                    dve.wait_ge(*at("n1_vt", t + 1))
                    normalise("n1", t, 6 + t % 2, NH8, HD8, 32)
                if s < HEADS:
                    dve.wait_ge(*at("n1_s", s + 1))
                    dve.tensor_reduce(nmx[:, s // NH8, s % NH8:s % NH8 + 1], ps[:, s % N1_S, :], AX.X, ALU.max,
                                      negate=True).then_inc(S("n1_nmx"), 1)
                m = s - N1_T
                if 0 <= m < HEADS and not by_act(m, N1_ACT):
                    evac_pT("n1", m, HALF)
                early_norms(s)
                if s in (1, 2):
                    residual("x1t_ps", "x1_tok", (4, 5), aK, "L1_conv_ln2_b", (s - 1,))
                if s in (3, 4):
                    residual("n1t_ps", "n1_tok", (6, 7), bK, "L1_conv_bo_a", (s - 3,))
            dve.wait_ge(*at("n1_add", T))

            def n2_queries(i):
                dve.wait_ge(*at("n2_q_ps", i + 1))
                dve.tensor_scalar(halves(aT)[i], ps[:, 2 + i, :], HD4 ** -0.5, None, ALU.mult).then_inc(S("n2_q"), 1)

            def n2_values(i):
                evac_values("n2_v_ps", "n2_v", (6, 7), lambda i: vaug4[:, 4 * i:4 * i + 4, :, 0:HD4], halves_of=(i,))

            for t in range(4, T):
                gain_tile("ln1", bK, "L1_conv_ln1_g", t)
            dve.wait_ge(*at("g_tok", 2))
            for t in range(4, T):
                add_tile("ln1", bK, cK, t)
            half_stats("ln2", cK, 1, "ln1")
            for t in range(4, T):
                gain_tile("ln2", cK, "L1_conv_ln2_g", t)
            n2_queries(0)
            for t in range(4, T):
                add_tile("ln2", cK, aK, t)
            half_stats("na", aK, 1, "ln2")

            dve.wait_ge(*at("ones_cols", 3))
            n2_values(0)
            normalise_half("na", aK, bK, 1)
            n2_queries(1)
            n2_values(1)
            for s in range(T + 7):
                if s < T:
                    dve.wait_ge(*at("n2_s", NH4 * (s + 1)))
                    if s >= 4:
                        dve.wait_ge(*at("n2_pt", s - 3))
                    v = pS[:, s % 4, :].rearrange("p (h k) -> p h k", h=NH4)
                    dve.tensor_tensor(v, ps[:, s % 2, :].rearrange("p (h k) -> p h k", h=NH4),
                                      band[:, :].unsqueeze(1).broadcast_to([P, NH4, P]), ALU.add).then_inc(S("n2_sr"), 1)
                    dve.wait_ge(*at("n2_sr", s + 1))
                    dve.tensor_reduce(nmx[:, s, 0:NH4], v, AX.X, ALU.max, negate=True).then_inc(S("n2_nmx"), 1)
                t = s - 6
                if 0 <= t < T:
                    dve.wait_ge(*at("n2_add", t + 1))
                    stats_of("nb", aK, t)
                t = s - 3
                if 0 <= t < T:
                    dve.wait_ge(*at("n2_pv", t + 1))
                    normalise("n2", t, 4 + t % 2, NH4, HD4)
                t = s - 5
                if 0 <= t < T:
                    dve.wait_ge(*at("n2_proj", t + 1))
                    dve.wait_ge(*at("xb2_ready", t // 4 + 1))
                    dve.tensor_tensor(aK[:, t, :], ps[:, 7, 0:P], aK[:, t, :], ALU.add).then_inc(S("n2_add"), 1)
                t = s - 6
                if 0 <= t < T:
                    mean_of("nb", t)
                if s in (T + 4, T + 5):
                    for t in (2 * (s - T - 4), 2 * (s - T - 4) + 1):
                        normalise_tile("nb", aK, bK, t)
                if s == T + 6:
                    half_stats("nn", bK, 0, "nb")
            dve.wait_ge(*at("n2_add", T))

            def over_experts(v):
                return v.unsqueeze(2).broadcast_to([P, T, E])

            def router_logits(pre, k, bank):
                dve.wait_ge(*at(f"{pre}_lg_ps", 2))
                link(dve.tensor_tensor(lg[:, :, :], ps[:, bank, 0:T * E].rearrange("p (t e) -> p t e", e=E),
                                       rrow[:, k, :].unsqueeze(1).broadcast_to([P, T, E]), ALU.add))
                link(dve.tensor_reduce(lm[:, :], lg[:, :, :], AX.X, ALU.max))
                dve.tensor_tensor(lg[:, :, :], lg[:, :, :], over_experts(lm[:, :]), ALU.subtract).then_inc(S(f"{pre}_lg"), 1)
                dve.wait_ge(*at(f"{pre}_lg", 1))

            tril = tril8[:, :, :].unsqueeze(1).broadcast_to([P, T, E, E])

            def rank_experts():
                li = lg[:, :, :].unsqueeze(3).broadcast_to([P, T, E, E])
                lj = lg[:, :, :].unsqueeze(2).broadcast_to([P, T, E, E])
                link(dve.tensor_tensor(cm2, lj, li, ALU.is_equal))
                link(dve.tensor_tensor(cm2, cm2, tril, ALU.mult))
                link(dve.tensor_tensor(cmp_, lj, li, ALU.is_gt))
                link(dve.tensor_tensor(cmp_, cmp_, cm2, ALU.add))
                link(dve.tensor_reduce(rank[:, :, :], cmp_, AX.X, ALU.add))

            def x_low(e):
                if e >= 2:
                    dve.wait_ge(*at("m2_fc1", 8 * (e - 1)))
                dve.wait_ge(*at("m2_xe", e + 1))
                dve.wait_ge(*at("m2_x_high", e + 1))
                dve.tensor_tensor(xpart2[:, e % 2, 1, :], (bT, cT)[e % 2][:, :], xpart2[:, e % 2, 0, :].bitcast(F32),
                                  ALU.subtract).then_inc(S("m2_x_low"), 1)

            def w_low(e):
                dve.wait_ge(*at("m2_w_high", e + 1))
                dve.tensor_tensor(wpart2[:, e % 2, 1, :], fw1[:, e, :], wpart2[:, e % 2, 0, :].bitcast(F32),
                                  ALU.subtract).then_inc(S("m2_w_low"), 1)

            def accumulate(pre, acc):
                for e in range(E):
                    if e + 2 < E:
                        x_low(e + 2)
                        w_low(e + 2)
                    for t in range(T):
                        if t % 4 == 0:
                            dve.wait_ge(*at(f"{pre}_fc2", 2 * e + t // 4 + 1))
                        if e:
                            dve.wait_ge(*at(f"{pre}_acc", T * (e - 1) + t + 1))
                        dve.scalar_tensor_tensor(acc[:, t, :], ps[:, 4 + 2 * (e % 2) + t // 4, P * (t % 4):P * (t % 4) + P],
                                                 cw[:, t, e:e + 1], acc[:, t, :],
                                                 ALU.mult, ALU.add).then_inc(S(f"{pre}_acc"), 1)
                        if e == E - 1 and t % 4 == 3:
                            dve.wait_ge(*at(f"{pre}_acc", T * e + t + 1))
                            for u in range(t - 3, t + 1):
                                stats_of("nc", acc, u)
                            for u in range(t - 3, t + 1):
                                mean_of("nc", u)

            normalise_half("nb", aK, bK, 1)
            half_stats("nn", bK, 1, "nb")
            for i in range(2):
                normalise_half("nn", bK, cK, i)
            w_low(0)
            w_low(1)
            x_low(0)
            x_low(1)
            router_logits("m2", 0, 4)
            rank_experts()
            dve.wait_ge(*at("m2_ex", 1))
            link(dve.scalar_tensor_tensor(ex[:, :, :], rank[:, :, :], 2.0, ex[:, :, :], ALU.is_lt, ALU.mult))
            link(dve.tensor_reduce(sm[:, :], ex[:, :, :], AX.X, ALU.add))
            link(dve.reciprocal(rsm[:, :], sm[:, :]))
            dve.tensor_tensor(cw[:, :, :], ex[:, :, :], over_experts(rsm[:, :]), ALU.mult).then_inc(S("m2_cw"), 1)
            for i in range(2):
                dve.wait_ge(*at("m2_b2_ps", i + 1))
                v = aK[:, 4 * i:4 * i + 4, :]
                dve.tensor_tensor(v, ps[:, 6 + i, :].rearrange("p (t c) -> p t c", t=4), v, ALU.add).then_inc(S("m2_b2"), 1)
            dve.wait_ge(*at("m2_b2", 2))
            accumulate("m2", aK)
            dve.wait_ge(*at("m2_acc", T * E))

            normalise_half("nc", aK, bK, 0)
            normalise_half("nc", aK, bK, 1)
            for i in range(2):
                dve.wait_ge(*at("n3_q_ps", i + 1))
                dve.tensor_scalar(aT[0:U, HALF * i:HALF * i + HALF], ps[0:U, 2 + i, :], U ** -0.5, None,
                                  ALU.mult).then_inc(S("n3_q"), 1)
            evac_values("n3_v_ps", "n3_v", (6, 7), lambda i: vaug1[:, 4 * i:4 * i + 4, 0:U].unsqueeze(2))
            dve.wait_ge(*at("xb3_ready", 2))
            for s in range(T + 4):
                if s < T:
                    dve.wait_ge(*at("n3_s", s + 1))
                    dve.tensor_reduce(nmx[:, s, 0:1], ps[:, 2 * (s % 2):2 * (s % 2) + 2, :], AX.XY, ALU.max,
                                      negate=True).then_inc(S("n3_nmx"), 1)
                t = s - 2
                if 0 <= t < T:
                    dve.wait_ge(*at("n3_pv", t + 1))
                    normalise("n3", t, 6 + t % 2, 1, U)
                t = s - 1
                if 0 <= t < T:
                    dve.wait_ge(*at("n3_pt", 2 * t + 1))
                    if t >= 2:
                        dve.wait_ge(*at("n3_pv", t - 1))
                    dve.tensor_copy(pT[:, 2 * (t % 2), :], ps[:, 4, :]).then_inc(S("n3_ptd"), 1)
                t = s - 4
                if 0 <= t < T:
                    dve.wait_ge(*at("n3_add", t + 1))
                    stats_of("nd", aK, t)
                t = s - 3
                if 0 <= t < T:
                    dve.wait_ge(*at("n3_proj", t + 1))
                    dve.tensor_tensor(aK[:, t, :], ps[:, 6 + t % 2, 0:P], aK[:, t, :], ALU.add).then_inc(S("n3_add"), 1)
                t = s - 4
                if 0 <= t < T:
                    mean_of("nd", t)
            dve.wait_ge(*at("n3_add", T))

            for i in range(2):
                normalise_half("nd", aK, bK, i)
            router_logits("m3", 1, 2)
            link(dve.tensor_scalar(kept[:, :, :], lg[:, :, :], 0.0, None, ALU.is_ge))
            link(dve.tensor_tensor(cm2, kept[:, :, :].unsqueeze(2).broadcast_to([P, T, E, E]), tril, ALU.mult))
            link(dve.tensor_reduce(cw[:, :, :], cm2, AX.X, ALU.add))
            dve.scalar_tensor_tensor(rank[:, :, :], cw[:, :, :], 1.0, kept[:, :, :], ALU.is_lt, ALU.mult).then_inc(S("m3_hot"), 1)
            dve.wait_ge(*at("m3_hot", 1))
            link(dve.tensor_tensor(before[:, 1:T, :], rank[:, 1:T, :], rank[:, 0:T - 1, :], ALU.add))
            link(dve.tensor_copy(before[:, 0, :], rank[:, 0, :]))
            link(dve.tensor_tensor(before2[:, 2:T, :], before[:, 2:T, :], before[:, 0:T - 2, :], ALU.add))
            link(dve.tensor_copy(before2[:, 0:2, :], before[:, 0:2, :]))
            dve.tensor_tensor(before[:, 4:T, :], before2[:, 4:T, :], before2[:, 0:4, :], ALU.add).then_inc(S("m3_before"), 1)
            dve.tensor_copy(before[:, 0:4, :], before2[:, 0:4, :]).then_inc(S("m3_before"), 1)
            dve.wait_ge(*at("m3_ex", 1))
            link(dve.tensor_reduce(sm[:, :], ex[:, :, :], AX.X, ALU.add))
            link(dve.reciprocal(rsm[:, :], sm[:, :]))
            link(dve.tensor_tensor(lmask[:, :], rsm[:, :], rsm[:, :], ALU.not_equal))
            link(dve.copy_predicated(rsm[:, :], lmask[:, :], fills[:, 0, 0:T]))
            dve.wait_ge(*at("m3_pos", 1))
            dve.wait_ge(*at("places_ready", 4))
            pos = ps[:, 3, 0:T * E].rearrange("p (t e) -> p t e", e=E)
            link(dve.scalar_tensor_tensor(cw[:, :, :], pos, float(CAP) + 0.5, rank[:, :, :], ALU.is_lt, ALU.mult))
            link(dve.tensor_tensor(ex[:, :, :], pos, placeoff.unsqueeze(1).broadcast_to([P, T, E]), ALU.add))
            link(dve.tensor_tensor(ex[:, :, :], ex[:, :, :], cw[:, :, :], ALU.mult))
            link(dve.tensor_reduce(slot[:, :], ex[:, :, :], AX.X, ALU.add))
            dve.tensor_scalar(slot[:, :], slot[:, :], -1.0, None, ALU.add).then_inc(S("m3_slot"), 1)
            dve.wait_ge(*at("m3_slot", 1))
            for t in range(T):
                if t >= 2:
                    dve.wait_ge(*at("m3_gathered", t - 1))
                dve.tensor_scalar(hot(t), places, slot[:, t:t + 1], None, ALU.is_equal).then_inc(S("m3_hot_ready"), 1)
            dve.wait_ge(*at("m3_gathered", T))
            dve.tensor_copy(xg[:, HALF:2 * HALF], ps[:, 1, :]).then_inc(S("m3_xg_dve"), 1)
            dve.wait_ge(*at("slotrow", 1))

            def hot_turned(n):
                i, k = COMBINE[n]
                if n >= 6:
                    dve.wait_ge(*at("m3_combined", n - 5))
                dve.tensor_scalar(hotT(n), halves(slotrow)[i], placecol[:, k:k + 1], None,
                                  ALU.is_equal).then_inc(S("m3_hotT"), 1)

            def turned_low(g):
                dve.wait_ge(*at("m3_high", g + 1))
                k0, k1 = TURNS[g]
                dve.tensor_tensor(ypart[:, 1, k0:k1, :], ps[:, 1 + g % 2, 0:P * (k1 - k0)].rearrange("p (k c) -> p k c", c=P),
                                  ypart[:, 0, k0:k1, :].bitcast(F32), ALU.subtract).then_inc(S("m3_low"), 1)

            made = 0
            for e in range(E):
                if made < 6:
                    hot_turned(made)
                    made += 1
                dve.wait_ge(*at("m3_fc2", e + 1))
                dve.tensor_scalar(yT[:, CAP * e:CAP * e + CAP], ps[:, 0 if e % 2 else 7, 0:CAP], col("L3_ffn_b2", e), 0.5,
                                  ALU.add, ALU.mult).then_inc(S("m3_y"), 1)
                if e % 4 == 3:
                    v = yT[:, CAP * (e - 3):CAP * (e + 1)].rearrange("p (k c) -> p k c", c=P)
                    m = nanm[:, 0:SC // 2, :]
                    dve.wait_ge(*at("m3_y", e + 1))
                    link(dve.tensor_tensor(m, v, v, ALU.not_equal))
                    link(dve.copy_predicated(v, m, fills[:, 0:1, :].broadcast_to([P, SC // 2, P])))
                    dve.tensor_scalar(v, v, BIG, -BIG, ALU.min, ALU.max).then_inc(S("m3_clean"), 1)
                if e == E - 2:
                    turned_low(0)
                    turned_low(1)
            for n in range(made, 12):
                hot_turned(n)
            turned_low(2)
            turned_low(3)
            for n in range(12, 2 * SC):
                hot_turned(n)
            for i in range(2):
                dve.wait_ge(*at("m3_out_ps", i + 1))
                y, m, f, r = (v[:, 4 * i:4 * i + 4, :] for v in (cK, nanm, bK, aK))
                link(dve.scalar_tensor_tensor(y, ps[:, 5 + i, :].rearrange("p (t c) -> p t c", c=P), 2.0,
                                              rsm[:, 4 * i:4 * i + 4].unsqueeze(2).broadcast_to([P, 4, P]),
                                              ALU.mult, ALU.mult))
                link(dve.tensor_scalar(m, y, 0.0, 0.0, ALU.mult, ALU.not_equal))
                link(dve.tensor_scalar(f, y, 1.0e4, -1.0e4, ALU.min, ALU.max))
                dve.copy_predicated(y, m, f).then_inc(S("y_clean"), 1)
                if i == 1:
                    dve.wait_ge(*at("y_clean", 2))
                    dve.tensor_tensor(r, r, y, ALU.add).then_inc(S("y_ready_1"), 1)


def kernel(**inputs):
    import numpy as _np
    import concourse.bacc as _bacc
    from concourse.bass_utils import run_bass_kernel_spmd as _run

    a = {name: _np.asarray(v) for name, v in inputs.items()}

    def experts_first(w):
        return w.transpose(1, 0, 2)

    def experts_second(w):
        return w.reshape(E, FC, P, P).transpose(2, 0, 1, 3)

    def stacked(b):
        return _np.tile(b.reshape(4, 32), (1, 4)).reshape(4 * P)

    a["n0_q_b"], a["n0_k_b"] = stacked(a["L0_conv_qkv_b"][:P]), stacked(a["L0_conv_qkv_b"][P:2 * P])
    a["n1_q_b"], a["n1_k_b"] = stacked(a["L1_conv_bq_a"]), stacked(a["L1_conv_bk_a"])
    qkv = a["L0_conv_qkv_w"].reshape(3, P, P)
    laid = {
        "xT": a["x"].reshape(N, P).T,
        "first": _np.concatenate([qkv[0].T, qkv[1].T, qkv[2].T, a["L0_conv_proj_w"].T]
                                 + [a[name].reshape(-1, P).T for name in VEC], axis=1),
        "rpbT": _np.pad(a["L0_conv_rpb"].transpose(2, 0, 1), ((0, 0), (0, 0), (1, 1))),
        "rows": _np.concatenate([a["L0_conv_qkv_b"][2 * P:]] + [a[name] for name in ROWVEC[1:]]
                                + [a["L2_ffn_br"], a["L3_ffn_gate_b"]]),
        "w1": _np.stack([a["L1_conv_" + name] for name in
                         ("wq_proj", "wk_proj", "wv_proj", "wq_a", "wk_a", "wv_a", "wo_a")], axis=1),
        "convw": a["L1_conv_conv_w"].reshape(25, P, P).transpose(1, 0, 2),
        "late": _np.concatenate([a["L2_attn_Wqkv"], a["L2_attn_Wproj"], a["L3_attn_W_q"], a["L3_attn_W_k"],
                                 a["L3_attn_W_v"], a["L2_ffn_Wr"], a["L3_ffn_gate_w"]], axis=1),
        "w3o": a["L3_attn_W_o"],
        "fb2": a["L2_ffn_b2"],
        "m2_w1": experts_first(a["L2_ffn_W1"]), "m2_w2": experts_second(a["L2_ffn_W2"]),
        "m3_w1": experts_first(a["L3_ffn_w1"]), "m3_w2": experts_second(a["L3_ffn_w2"]),
    }
    nc = _bacc.Bacc("TRN2", target_bir_lowering=False, num_devices=1)
    arrays, args = {}, {}
    for name, v in laid.items():
        v = _np.ascontiguousarray(v)
        arrays[f"in_{name}_dram"] = v
        args[name] = nc.dram_tensor(f"in_{name}_dram", v.shape, mybir.dt.from_np(v.dtype), kind="ExternalInput").ap()
    out = nc.dram_tensor("out_0_dram", (1, IMG, IMG, P), F32, kind="ExternalOutput").ap()
    build(nc, args, out)
    r = _run(nc, [arrays], core_ids=[0])
    return r.results[0]["out_0_dram"]
```
